# Optimizing a Trainium2 kernel written in Bass

```python
import numpy as np
import jax
import jax.numpy as jnp

def _softmax(x, axis=-1):
    return jax.nn.softmax(x, axis=axis)

def _gelu(x):
    return jax.nn.gelu(x, approximate=True)

def _silu(x):
    return jax.nn.silu(x)

def _sigmoid(x):
    return jax.nn.sigmoid(x)

def _layernorm(x, axis=-1, eps=1e-05):
    m = jnp.mean(x, axis=axis, keepdims=True)
    v = jnp.var(x, axis=axis, keepdims=True)
    return (x - m) / jnp.sqrt(v + eps)

def _scatter_add(tgt, idx, src, axis=0):
    return tgt.at[idx].add(src)

def _segment_sum(src, seg, n):
    return jax.ops.segment_sum(src, seg, n)
kernel_name = 'mk_seq_postln_d4_jaxref_r8_4db1c6'

def setup_inputs(seed: int=0):
    np.random.seed(seed)
    _w = jnp.asarray

    def _L0_attn_setup():
        import jax, jax.numpy as jnp
        import numpy as np
        MAX_LR = 0.01
        NS_A, NS_B, NS_C = (3.4445, -4.775, 2.0315)

        def newtonschulz5(G, steps=5, eps=1e-07):
            transpose = G.shape[-2] > G.shape[-1]
            X = jnp.swapaxes(G, -2, -1) if transpose else G
            X = X / (jnp.linalg.norm(X, axis=(-2, -1), keepdims=True) + eps)
            for _ in range(steps):
                A = X @ jnp.swapaxes(X, -2, -1)
                Bm = NS_B * A + NS_C * (A @ A)
                X = NS_A * X + Bm @ X
            return jnp.swapaxes(X, -2, -1) if transpose else X

        def _reference_tuple_inner(tokens, wq, wk, wv, wo, w_lr, w_target, w_gates, rms_w):
            N = tokens.shape[1]
            scale = wq.shape[-1] ** (-0.5)
            eps = jnp.finfo(tokens.dtype).eps
            t = tokens * jax.lax.rsqrt(jnp.mean(tokens * tokens, -1, keepdims=True) + eps) * rms_w
            gates = jnp.swapaxes(jax.nn.sigmoid(t @ w_gates), -2, -1)[..., None]
            q = jnp.einsum('bnd,hde->bhne', t, wq)
            k = jnp.einsum('bnd,hde->bhne', t, wk)
            v = jnp.einsum('bnd,hde->bhne', t, wv)
            score = jnp.einsum('bhie,bhje->bhij', q, k) * scale
            causal_mask = jnp.triu(jnp.ones((N, N), bool), 1)
            score = jnp.where(causal_mask, -jnp.finfo(score.dtype).max, score)
            attn = jax.nn.softmax(score, axis=-1)
            out = jnp.einsum('bhij,bhje->bhie', attn, v) * gates
            pred_values = jnp.einsum('bhne,hed->bnd', out, wo)
            tv = t[:, 1:] @ w_target
            tv = (tv - tv.mean(-1, keepdims=True)) * jax.lax.rsqrt(tv.var(-1, keepdims=True) + 1e-05)
            ts = t[:, :-1]
            pv = pred_values[:, :-1]
            o = out[:, :, :-1]
            g = gates[:, :, :-1]
            a = attn[:, :, :-1, :-1]
            qs, ks_, vs = (q[:, :, :-1], k[:, :, :-1], v[:, :, :-1])
            lrs = jax.nn.sigmoid(ts @ w_lr) * MAX_LR
            lr, mlr = (lrs[..., 0], lrs[..., 1])
            error = tv - pv
            dout = jnp.einsum('bnd,hed->bhne', error, wo)
            du = dout * g
            delta = jnp.sum(dout * o, -1, keepdims=True)
            dv = jnp.einsum('bhij,bhie->bhje', a, du)
            dattn = jnp.einsum('bhje,bhie->bhij', vs, du)
            dscore = scale * a * (dattn - delta)
            dq = jnp.einsum('bhje,bhij->bhie', ks_, dscore)
            dk = jnp.einsum('bhie,bhij->bhje', qs, dscore)
            t_qk = ts * lr[..., None]
            t_v = ts * mlr[..., None]
            o_wo = o * mlr[:, None, :, None]
            dwq = jnp.einsum('bhie,bid->bhde', dq, t_qk)
            dwk = jnp.einsum('bhje,bjd->bhde', dk, t_qk)
            dwv = jnp.einsum('bhje,bjd->bhde', dv, t_v)
            dwo = jnp.einsum('bnd,bhne->bhed', error, o_wo)
            dwv = newtonschulz5(dwv)
            dwo = newtonschulz5(dwo)
            return (pred_values, dwq, dwk, dwv, dwo)
        key = jax.random.key(seed)
        ks = jax.random.split(key, 9)
        B, N, D, H, DH = (4, 128, 128, 8, 64)
        s = D ** (-0.5)
        return {'tokens': jax.random.normal(ks[0], (B, N, D), jnp.float32), 'wq': jax.random.normal(ks[1], (H, D, DH), jnp.float32) * s, 'wk': jax.random.normal(ks[2], (H, D, DH), jnp.float32) * s, 'wv': jax.random.normal(ks[3], (H, D, DH), jnp.float32) * s, 'wo': jax.random.normal(ks[4], (H, DH, D), jnp.float32) * s, 'w_lr': jax.random.normal(ks[5], (D, 2), jnp.float32) * 0.02, 'w_target': jax.random.normal(ks[6], (D, D), jnp.float32) * 0.02, 'w_gates': jax.random.normal(ks[7], (D, H), jnp.float32) * 0.02, 'rms_w': jnp.ones((D,), jnp.float32)}
    _L0_attn_in = _L0_attn_setup()

    def _L0_ffn_setup():
        import jax, jax.numpy as jnp
        import numpy as np
        E, K, D, H = (8, 2, 128, 256)
        B, S = (1, 128)

        def _grouped_swiglu(x_sorted, counts, w1, w2, w3):
            if hasattr(jax.lax, 'ragged_dot'):
                gs = counts.astype(jnp.int32)
                h = jax.nn.silu(jax.lax.ragged_dot(x_sorted, w1, gs)) * jax.lax.ragged_dot(x_sorted, w3, gs)
                return jax.lax.ragged_dot(h, w2, gs)
            pos = jnp.arange(x_sorted.shape[0])
            eid = jnp.searchsorted(jnp.cumsum(counts), pos, side='right')
            out = jnp.zeros((x_sorted.shape[0], w2.shape[-1]), x_sorted.dtype)
            for e in range(w1.shape[0]):
                xm = jnp.where((eid == e)[:, None], x_sorted, 0.0)
                he = jax.nn.silu(xm @ w1[e]) * (xm @ w3[e])
                out = out + he @ w2[e]
            return out
        key = jax.random.key(seed)
        k0, k1, k2, k3, k4 = jax.random.split(key, 5)
        sD = 1.0 / np.sqrt(D)
        sH = 1.0 / np.sqrt(H)
        return {'hidden_states': jax.random.normal(k0, (B, S, D), jnp.float32), 'gate_w': jax.random.normal(k1, (E, D), jnp.float32) * sD, 'w1': jax.random.normal(k2, (E, D, H), jnp.float32) * sD, 'w2': jax.random.normal(k3, (E, H, D), jnp.float32) * sH, 'w3': jax.random.normal(k4, (E, D, H), jnp.float32) * sD}
    _L0_ffn_in = _L0_ffn_setup()

    def _L1_attn_setup():
        import jax, jax.numpy as jnp
        import numpy as np
        DIM = 128
        HEADS = 16
        DIM_HEAD = 64
        DIM_INNER = HEADS * DIM_HEAD

        def rms_norm(x, gamma):
            eps = 1e-12
            norm = jnp.maximum(jnp.linalg.norm(x, axis=-1, keepdims=True), eps)
            return x / norm * x.shape[-1] ** 0.5 * (gamma + 1.0)
        key = jax.random.key(seed)
        k1, k2, k3 = jax.random.split(key, 3)
        x = jax.random.normal(k1, (2, 256, DIM), dtype=jnp.float32)
        gamma = jnp.zeros((DIM,), dtype=jnp.float32)
        w_qkv = jax.random.normal(k2, (DIM, DIM_INNER * 3), dtype=jnp.float32) * DIM ** (-0.5)
        w_out = jax.random.normal(k3, (DIM_INNER, DIM), dtype=jnp.float32) * DIM_INNER ** (-0.5)
        return {'x': x, 'gamma': gamma, 'w_qkv': w_qkv, 'w_out': w_out}
    _L1_attn_in = _L1_attn_setup()

    def _L1_ffn_setup():
        import jax, jax.numpy as jnp
        import numpy as np
        DIM = 128
        DEPTH = 2
        HEADS = 8
        DIM_HEAD = 64
        WINDOW = 64
        INNER = HEADS * DIM_HEAD
        HID = int(DIM * 4 * 2 / 3)
        B, N = (2, 1024)
        QK_SCALE = 8.0

        def shift_token(t):
            t1, t2 = jnp.split(t, 2, axis=-1)
            t2 = jnp.pad(t2, ((0, 0), (1, 0), (0, 0)))[:, :-1]
            return jnp.concatenate([t1, t2], axis=-1)

        def l2norm(t):
            return t / jnp.clip(jnp.linalg.norm(t, axis=-1, keepdims=True), 1e-12)

        def rotate_half(x):
            x1, x2 = jnp.split(x, 2, axis=-1)
            return jnp.concatenate([-x2, x1], axis=-1)

        def rotary_xpos(q, k):
            n = q.shape[-2]
            half_idx = jnp.arange(0, DIM_HEAD, 2, dtype=jnp.float32)
            inv_freq = 1.0 / 10000.0 ** (half_idx / DIM_HEAD)
            t = jnp.arange(n, dtype=jnp.float32)
            freqs = t[:, None] * inv_freq[None, :]
            freqs = jnp.concatenate([freqs, freqs], axis=-1)
            base = (half_idx + 0.4 * DIM_HEAD) / (1.4 * DIM_HEAD)
            power = (t - n // 2) / float(WINDOW // 2)
            scale = base[None, :] ** power[:, None]
            scale = jnp.concatenate([scale, scale], axis=-1)
            cos, sin = (jnp.cos(freqs), jnp.sin(freqs))
            q = q * cos * scale + rotate_half(q) * sin * scale
            k = k * cos / scale + rotate_half(k) * sin / scale
            return (q, k)

        def local_attention(q, k, v):
            b, h, n, d = q.shape
            w = n // WINDOW
            bq = q.reshape(b, h, w, WINDOW, d) * QK_SCALE
            bk = k.reshape(b, h, w, WINDOW, d)
            bv = v.reshape(b, h, w, WINDOW, d)

            def look_around(t):
                p = jnp.pad(t, ((0, 0), (0, 0), (1, 0), (0, 0), (0, 0)))
                return jnp.concatenate([p[:, :, :w], p[:, :, 1:]], axis=3)
            bk, bv = (look_around(bk), look_around(bv))
            bt = jnp.arange(n).reshape(w, WINDOW)
            btp = jnp.pad(bt, ((1, 0), (0, 0)), constant_values=-1)
            btk = jnp.concatenate([btp[:w], btp[1:]], axis=1)
            sim = jnp.einsum('bhwid,bhwjd->bhwij', bq, bk)
            i = bt[:, :, None]
            j = btk[:, None, :]
            mask = (i < j) | (i > j + WINDOW) | (j == -1)
            sim = jnp.where(mask, -jnp.finfo(sim.dtype).max, sim)
            attn = jax.nn.softmax(sim, axis=-1)
            out = jnp.einsum('bhwij,bhwjd->bhwid', attn, bv)
            return out.reshape(b, h, n, d)

        def _layer(x, wqkv, qs, ksc, wo, lg, lb, w1, b1, w2, b2):
            b, n, _ = x.shape
            h = shift_token(x)
            qkv = h @ wqkv
            q, k, v = jnp.split(qkv, 3, axis=-1)
            to_heads = lambda t: t.reshape(b, n, HEADS, DIM_HEAD).transpose(0, 2, 1, 3)
            q, k, v = (to_heads(q), to_heads(k), to_heads(v))
            q = l2norm(q) * qs
            k = l2norm(k) * ksc
            q, k = rotary_xpos(q, k)
            o = local_attention(q, k, v)
            o = o.transpose(0, 2, 1, 3).reshape(b, n, INNER)
            x = x + o @ wo
            h = shift_token(x)
            mu = h.mean(-1, keepdims=True)
            var = h.var(-1, keepdims=True)
            h = (h - mu) / jnp.sqrt(var + 1e-05) * lg + lb
            h = h @ w1 + b1
            a, g = jnp.split(h, 2, axis=-1)
            h = a * jax.nn.gelu(g, approximate=False)
            x = x + h @ w2 + b2
            return x
        key = jax.random.key(seed)
        ks = jax.random.split(key, 6)
        return {'x': jax.random.normal(ks[0], (B, N, DIM), jnp.float32), 'wqkv': jax.random.normal(ks[1], (DEPTH, DIM, 3 * INNER), jnp.float32) * 0.02, 'q_scale': jnp.ones((DEPTH, DIM_HEAD), jnp.float32), 'k_scale': jnp.ones((DEPTH, DIM_HEAD), jnp.float32), 'wo': jax.random.normal(ks[2], (DEPTH, INNER, DIM), jnp.float32) * 0.02, 'ln_g': jnp.ones((DEPTH, DIM), jnp.float32), 'ln_b': jnp.zeros((DEPTH, DIM), jnp.float32), 'w1': jax.random.normal(ks[3], (DEPTH, DIM, 2 * HID), jnp.float32) * 0.02, 'b1': jnp.zeros((DEPTH, 2 * HID), jnp.float32), 'w2': jax.random.normal(ks[4], (DEPTH, HID, DIM), jnp.float32) * 0.02, 'b2': jnp.zeros((DEPTH, DIM), jnp.float32)}
    _L1_ffn_in = _L1_ffn_setup()

    def _L2_attn_setup():
        import jax, jax.numpy as jnp
        import numpy as np
        DIM = 128
        NUM_HEAD = 16
        DIM_HEAD = DIM // NUM_HEAD
        RMS_EPS = 1.1920929e-07
        EPS_LIN = 1e-06
        THETA = 10000.0

        def rmsnorm(x, g, eps=RMS_EPS):
            return x * jax.lax.rsqrt(jnp.mean(x * x, axis=-1, keepdims=True) + eps) * g

        def rope_cos_sin(seq_len, dim_head, dtype=jnp.float32):
            inv_freq = 1.0 / THETA ** (jnp.arange(0, dim_head, 2, dtype=dtype) / dim_head)
            t = jnp.arange(seq_len, dtype=dtype)
            freqs = jnp.outer(t, inv_freq)
            return (jnp.cos(freqs), jnp.sin(freqs))

        def apply_rope(t, cos, sin):
            tr = t[..., 0::2]
            ti = t[..., 1::2]
            out_r = tr * cos - ti * sin
            out_i = tr * sin + ti * cos
            return jnp.stack([out_r, out_i], axis=-1).reshape(t.shape)
        key = jax.random.key(seed)
        ks = jax.random.split(key, 5)
        B, L = (4, 512)
        x = jax.random.normal(ks[0], (B, L, DIM), dtype=jnp.float32)
        Wqkv = jax.random.normal(ks[1], (3 * DIM, DIM), dtype=jnp.float32) * 0.02
        bqkv = jax.random.normal(ks[2], (3 * DIM,), dtype=jnp.float32) * 0.02
        gq = jnp.ones((DIM,), dtype=jnp.float32)
        gk = jnp.ones((DIM,), dtype=jnp.float32)
        Wout = jax.random.normal(ks[3], (DIM, DIM), dtype=jnp.float32) * 0.02
        bout = jax.random.normal(ks[4], (DIM,), dtype=jnp.float32) * 0.02
        gout = jnp.ones((DIM,), dtype=jnp.float32)
        return {'x': x, 'Wqkv': Wqkv, 'bqkv': bqkv, 'gq': gq, 'gk': gk, 'Wout': Wout, 'bout': bout, 'gout': gout}
    _L2_attn_in = _L2_attn_setup()

    def _L2_ffn_setup():
        import jax, jax.numpy as jnp
        import numpy as np
        DIM = 128

        def _reference_tuple_inner(x, W_r, W_k, W_v, mu_r, mu_k):
            B, T, C = x.shape
            x_prev = jnp.concatenate([jnp.zeros((B, 1, C), x.dtype), x[:, :-1, :]], axis=1)
            xr = mu_r * x + (1.0 - mu_r) * x_prev
            xk = mu_k * x + (1.0 - mu_k) * x_prev
            r = jax.nn.sigmoid(jnp.einsum('btc,dc->btd', xr, W_r))
            k = jnp.einsum('btc,dc->btd', xk, W_k)
            k_act = jnp.square(jax.nn.relu(k))
            out = r * jnp.einsum('btc,dc->btd', k_act, W_v)
            new_state = x[:, -1, :]
            return (out, new_state)
        key = jax.random.key(seed)
        ks = jax.random.split(key, 6)
        B, T, C = (8, 256, DIM)
        x = jax.random.normal(ks[0], (B, T, C), dtype=jnp.float32)
        s = 1.0 / np.sqrt(C)
        W_r = jax.random.uniform(ks[1], (C, C), jnp.float32, -s, s)
        W_k = jax.random.uniform(ks[2], (C, C), jnp.float32, -s, s)
        W_v = jax.random.uniform(ks[3], (C, C), jnp.float32, -s, s)
        mu_r = jax.random.uniform(ks[4], (C,), jnp.float32)
        mu_k = jax.random.uniform(ks[5], (C,), jnp.float32)
        return {'x': x, 'W_r': W_r, 'W_k': W_k, 'W_v': W_v, 'mu_r': mu_r, 'mu_k': mu_k}
    _L2_ffn_in = _L2_ffn_setup()

    def _L3_attn_setup():
        import jax, jax.numpy as jnp
        import numpy as np
        from jax import lax
        B, T, HID = (4, 128, 128)
        H, DK, DV = (8, 128, 128)
        KCONV = 4
        EPS = 1e-06
        KEY_DIM = H * DK
        VAL_DIM = H * DV
        CONV_DIM = 2 * KEY_DIM + VAL_DIM
        key = jax.random.key(seed)
        ks = jax.random.split(key, 11)
        s = 0.02
        return {'hidden_states': jax.random.normal(ks[0], (B, T, HID), jnp.float32), 'qkv_w': jax.random.normal(ks[1], (CONV_DIM, HID), jnp.float32) * s, 'z_w': jax.random.normal(ks[2], (VAL_DIM, HID), jnp.float32) * s, 'b_w': jax.random.normal(ks[3], (H, HID), jnp.float32) * s, 'a_w': jax.random.normal(ks[4], (H, HID), jnp.float32) * s, 'conv_w': jax.random.normal(ks[5], (CONV_DIM, 1, KCONV), jnp.float32) * 0.2, 'dt_bias': jnp.ones((H,), jnp.float32), 'A_log': jnp.log(jax.random.uniform(ks[6], (H,), jnp.float32, 0.001, 16.0)), 'norm_w': jnp.ones((DV,), jnp.float32), 'out_w': jax.random.normal(ks[7], (HID, VAL_DIM), jnp.float32) * s}
    _L3_attn_in = _L3_attn_setup()

    def _L3_ffn_setup():
        import jax, jax.numpy as jnp
        import numpy as np
        B, K, D = (128, 32, 128)
        E = 32
        H = int(D * 0.25)

        def _rsqrt_uniform(key, shape, d):
            bound = d ** (-0.5)
            return jax.random.uniform(key, shape, jnp.float32, -bound, bound)
        key = jax.random.key(seed)
        ks = jax.random.split(key, 7)
        return {'x': jax.random.normal(ks[0], (B, K, D), jnp.float32), 'router_w': _rsqrt_uniform(ks[1], (E, D), D), 'router_b': _rsqrt_uniform(ks[2], (E,), D), 'weights1': _rsqrt_uniform(ks[3], (E, D, H), H), 'bias1': _rsqrt_uniform(ks[4], (E, H), H), 'weights2': _rsqrt_uniform(ks[5], (E, H, D), D), 'bias2': _rsqrt_uniform(ks[6], (E, D), D)}
    _L3_ffn_in = _L3_ffn_setup()
    _d = {'L0_attn_tokens': _L0_attn_in['tokens'], 'L0_attn_wq': _L0_attn_in['wq'], 'L0_attn_wk': _L0_attn_in['wk'], 'L0_attn_wv': _L0_attn_in['wv'], 'L0_attn_wo': _L0_attn_in['wo'], 'L0_attn_w_lr': _L0_attn_in['w_lr'], 'L0_attn_w_target': _L0_attn_in['w_target'], 'L0_attn_w_gates': _L0_attn_in['w_gates'], 'L0_attn_rms_w': _L0_attn_in['rms_w'], 'L0_ffn_gate_w': _L0_ffn_in['gate_w'], 'L0_ffn_w1': _L0_ffn_in['w1'], 'L0_ffn_w2': _L0_ffn_in['w2'], 'L0_ffn_w3': _L0_ffn_in['w3'], 'L1_attn_gamma': _L1_attn_in['gamma'], 'L1_attn_w_qkv': _L1_attn_in['w_qkv'], 'L1_attn_w_out': _L1_attn_in['w_out'], 'L1_ffn_wqkv': _L1_ffn_in['wqkv'], 'L1_ffn_q_scale': _L1_ffn_in['q_scale'], 'L1_ffn_k_scale': _L1_ffn_in['k_scale'], 'L1_ffn_wo': _L1_ffn_in['wo'], 'L1_ffn_ln_g': _L1_ffn_in['ln_g'], 'L1_ffn_ln_b': _L1_ffn_in['ln_b'], 'L1_ffn_w1': _L1_ffn_in['w1'], 'L1_ffn_b1': _L1_ffn_in['b1'], 'L1_ffn_w2': _L1_ffn_in['w2'], 'L1_ffn_b2': _L1_ffn_in['b2'], 'L2_attn_Wqkv': _L2_attn_in['Wqkv'], 'L2_attn_bqkv': _L2_attn_in['bqkv'], 'L2_attn_gq': _L2_attn_in['gq'], 'L2_attn_gk': _L2_attn_in['gk'], 'L2_attn_Wout': _L2_attn_in['Wout'], 'L2_attn_bout': _L2_attn_in['bout'], 'L2_attn_gout': _L2_attn_in['gout'], 'L2_ffn_W_r': _L2_ffn_in['W_r'], 'L2_ffn_W_k': _L2_ffn_in['W_k'], 'L2_ffn_W_v': _L2_ffn_in['W_v'], 'L2_ffn_mu_r': _L2_ffn_in['mu_r'], 'L2_ffn_mu_k': _L2_ffn_in['mu_k'], 'L3_attn_qkv_w': _L3_attn_in['qkv_w'], 'L3_attn_z_w': _L3_attn_in['z_w'], 'L3_attn_b_w': _L3_attn_in['b_w'], 'L3_attn_a_w': _L3_attn_in['a_w'], 'L3_attn_conv_w': _L3_attn_in['conv_w'], 'L3_attn_dt_bias': _L3_attn_in['dt_bias'], 'L3_attn_A_log': _L3_attn_in['A_log'], 'L3_attn_norm_w': _L3_attn_in['norm_w'], 'L3_attn_out_w': _L3_attn_in['out_w'], 'L3_ffn_router_w': _L3_ffn_in['router_w'], 'L3_ffn_router_b': _L3_ffn_in['router_b'], 'L3_ffn_weights1': _L3_ffn_in['weights1'], 'L3_ffn_bias1': _L3_ffn_in['bias1'], 'L3_ffn_weights2': _L3_ffn_in['weights2'], 'L3_ffn_bias2': _L3_ffn_in['bias2']}
    _x0 = _d['L0_attn_tokens']
    _d['L0_attn_tokens'] = jax.random.normal(jax.random.fold_in(jax.random.key(seed), 1), (4, 512, 128), dtype=_x0.dtype)
    del _x0
    return _d

def reference(L0_attn_tokens, L0_attn_wq, L0_attn_wk, L0_attn_wv, L0_attn_wo, L0_attn_w_lr, L0_attn_w_target, L0_attn_w_gates, L0_attn_rms_w, L0_ffn_gate_w, L0_ffn_w1, L0_ffn_w2, L0_ffn_w3, L1_attn_gamma, L1_attn_w_qkv, L1_attn_w_out, L1_ffn_wqkv, L1_ffn_q_scale, L1_ffn_k_scale, L1_ffn_wo, L1_ffn_ln_g, L1_ffn_ln_b, L1_ffn_w1, L1_ffn_b1, L1_ffn_w2, L1_ffn_b2, L2_attn_Wqkv, L2_attn_bqkv, L2_attn_gq, L2_attn_gk, L2_attn_Wout, L2_attn_bout, L2_attn_gout, L2_ffn_W_r, L2_ffn_W_k, L2_ffn_W_v, L2_ffn_mu_r, L2_ffn_mu_k, L3_attn_qkv_w, L3_attn_z_w, L3_attn_b_w, L3_attn_a_w, L3_attn_conv_w, L3_attn_dt_bias, L3_attn_A_log, L3_attn_norm_w, L3_attn_out_w, L3_ffn_router_w, L3_ffn_router_b, L3_ffn_weights1, L3_ffn_bias1, L3_ffn_weights2, L3_ffn_bias2):

    def _L0_attn_ref(tokens, wq, wk, wv, wo, w_lr, w_target, w_gates, rms_w):
        import jax, jax.numpy as jnp
        import numpy as np
        MAX_LR = 0.01
        NS_A, NS_B, NS_C = (3.4445, -4.775, 2.0315)

        def newtonschulz5(G, steps=5, eps=1e-07):
            transpose = G.shape[-2] > G.shape[-1]
            X = jnp.swapaxes(G, -2, -1) if transpose else G
            X = X / (jnp.linalg.norm(X, axis=(-2, -1), keepdims=True) + eps)
            for _ in range(steps):
                A = X @ jnp.swapaxes(X, -2, -1)
                Bm = NS_B * A + NS_C * (A @ A)
                X = NS_A * X + Bm @ X
            return jnp.swapaxes(X, -2, -1) if transpose else X

        def _reference_tuple_inner(tokens, wq, wk, wv, wo, w_lr, w_target, w_gates, rms_w):
            N = tokens.shape[1]
            scale = wq.shape[-1] ** (-0.5)
            eps = jnp.finfo(tokens.dtype).eps
            t = tokens * jax.lax.rsqrt(jnp.mean(tokens * tokens, -1, keepdims=True) + eps) * rms_w
            gates = jnp.swapaxes(jax.nn.sigmoid(t @ w_gates), -2, -1)[..., None]
            q = jnp.einsum('bnd,hde->bhne', t, wq)
            k = jnp.einsum('bnd,hde->bhne', t, wk)
            v = jnp.einsum('bnd,hde->bhne', t, wv)
            score = jnp.einsum('bhie,bhje->bhij', q, k) * scale
            causal_mask = jnp.triu(jnp.ones((N, N), bool), 1)
            score = jnp.where(causal_mask, -jnp.finfo(score.dtype).max, score)
            attn = jax.nn.softmax(score, axis=-1)
            out = jnp.einsum('bhij,bhje->bhie', attn, v) * gates
            pred_values = jnp.einsum('bhne,hed->bnd', out, wo)
            tv = t[:, 1:] @ w_target
            tv = (tv - tv.mean(-1, keepdims=True)) * jax.lax.rsqrt(tv.var(-1, keepdims=True) + 1e-05)
            ts = t[:, :-1]
            pv = pred_values[:, :-1]
            o = out[:, :, :-1]
            g = gates[:, :, :-1]
            a = attn[:, :, :-1, :-1]
            qs, ks_, vs = (q[:, :, :-1], k[:, :, :-1], v[:, :, :-1])
            lrs = jax.nn.sigmoid(ts @ w_lr) * MAX_LR
            lr, mlr = (lrs[..., 0], lrs[..., 1])
            error = tv - pv
            dout = jnp.einsum('bnd,hed->bhne', error, wo)
            du = dout * g
            delta = jnp.sum(dout * o, -1, keepdims=True)
            dv = jnp.einsum('bhij,bhie->bhje', a, du)
            dattn = jnp.einsum('bhje,bhie->bhij', vs, du)
            dscore = scale * a * (dattn - delta)
            dq = jnp.einsum('bhje,bhij->bhie', ks_, dscore)
            dk = jnp.einsum('bhie,bhij->bhje', qs, dscore)
            t_qk = ts * lr[..., None]
            t_v = ts * mlr[..., None]
            o_wo = o * mlr[:, None, :, None]
            dwq = jnp.einsum('bhie,bid->bhde', dq, t_qk)
            dwk = jnp.einsum('bhje,bjd->bhde', dk, t_qk)
            dwv = jnp.einsum('bhje,bjd->bhde', dv, t_v)
            dwo = jnp.einsum('bnd,bhne->bhed', error, o_wo)
            dwv = newtonschulz5(dwv)
            dwo = newtonschulz5(dwo)
            return (pred_values, dwq, dwk, dwv, dwo)
        return _reference_tuple_inner(tokens, wq, wk, wv, wo, w_lr, w_target, w_gates, rms_w)[0]

    def _L0_ffn_ref(hidden_states, gate_w, w1, w2, w3):
        import jax, jax.numpy as jnp
        import numpy as np
        E, K, D, H = (8, 2, 128, 256)
        B, S = (1, 128)

        def _grouped_swiglu(x_sorted, counts, w1, w2, w3):
            if hasattr(jax.lax, 'ragged_dot'):
                gs = counts.astype(jnp.int32)
                h = jax.nn.silu(jax.lax.ragged_dot(x_sorted, w1, gs)) * jax.lax.ragged_dot(x_sorted, w3, gs)
                return jax.lax.ragged_dot(h, w2, gs)
            pos = jnp.arange(x_sorted.shape[0])
            eid = jnp.searchsorted(jnp.cumsum(counts), pos, side='right')
            out = jnp.zeros((x_sorted.shape[0], w2.shape[-1]), x_sorted.dtype)
            for e in range(w1.shape[0]):
                xm = jnp.where((eid == e)[:, None], x_sorted, 0.0)
                he = jax.nn.silu(xm @ w1[e]) * (xm @ w3[e])
                out = out + he @ w2[e]
            return out
        x = hidden_states.reshape(-1, D)
        N = x.shape[0]
        scores = jax.nn.softmax(x @ gate_w.T, axis=-1)
        top_scores, sel = jax.lax.top_k(scores, K)
        sel_flat = sel.T.reshape(-1)
        scores_flat = top_scores.T.reshape(-1)
        order = jnp.argsort(sel_flat, stable=True)
        tok_sorted = order % N
        scores_sorted = scores_flat[order]
        counts = jnp.bincount(sel_flat, length=E)
        x_sorted = x[tok_sorted]
        y = _grouped_swiglu(x_sorted, counts, w1, w2, w3)
        weighted = y * scores_sorted[:, None]
        out = jnp.zeros((N, D), x.dtype).at[tok_sorted].add(weighted)
        return out.reshape(hidden_states.shape)

    def _L1_attn_ref(x, gamma, w_qkv, w_out):
        import jax, jax.numpy as jnp
        import numpy as np
        DIM = 128
        HEADS = 16
        DIM_HEAD = 64
        DIM_INNER = HEADS * DIM_HEAD

        def rms_norm(x, gamma):
            eps = 1e-12
            norm = jnp.maximum(jnp.linalg.norm(x, axis=-1, keepdims=True), eps)
            return x / norm * x.shape[-1] ** 0.5 * (gamma + 1.0)
        b, n, _ = x.shape
        scale = DIM_HEAD ** (-0.5)
        xn = rms_norm(x, gamma)
        qkv = xn @ w_qkv
        qkv = qkv.reshape(b, n, 3, HEADS, DIM_HEAD)
        qkv = jnp.transpose(qkv, (2, 0, 3, 1, 4))
        q, k, v = (qkv[0], qkv[1], qkv[2])
        q = q * scale
        sim = jnp.einsum('bhid,bhjd->bhij', q, k)
        attn = jax.nn.softmax(sim, axis=-1)
        out = jnp.einsum('bhij,bhjd->bhid', attn, v)
        out = jnp.transpose(out, (0, 2, 1, 3)).reshape(b, n, DIM_INNER)
        return out @ w_out

    def _L1_ffn_ref(x, wqkv, q_scale, k_scale, wo, ln_g, ln_b, w1, b1, w2, b2):
        import jax, jax.numpy as jnp
        import numpy as np
        DIM = 128
        DEPTH = 2
        HEADS = 8
        DIM_HEAD = 64
        WINDOW = 64
        INNER = HEADS * DIM_HEAD
        HID = int(DIM * 4 * 2 / 3)
        B, N = (2, 1024)
        QK_SCALE = 8.0

        def shift_token(t):
            t1, t2 = jnp.split(t, 2, axis=-1)
            t2 = jnp.pad(t2, ((0, 0), (1, 0), (0, 0)))[:, :-1]
            return jnp.concatenate([t1, t2], axis=-1)

        def l2norm(t):
            return t / jnp.clip(jnp.linalg.norm(t, axis=-1, keepdims=True), 1e-12)

        def rotate_half(x):
            x1, x2 = jnp.split(x, 2, axis=-1)
            return jnp.concatenate([-x2, x1], axis=-1)

        def rotary_xpos(q, k):
            n = q.shape[-2]
            half_idx = jnp.arange(0, DIM_HEAD, 2, dtype=jnp.float32)
            inv_freq = 1.0 / 10000.0 ** (half_idx / DIM_HEAD)
            t = jnp.arange(n, dtype=jnp.float32)
            freqs = t[:, None] * inv_freq[None, :]
            freqs = jnp.concatenate([freqs, freqs], axis=-1)
            base = (half_idx + 0.4 * DIM_HEAD) / (1.4 * DIM_HEAD)
            power = (t - n // 2) / float(WINDOW // 2)
            scale = base[None, :] ** power[:, None]
            scale = jnp.concatenate([scale, scale], axis=-1)
            cos, sin = (jnp.cos(freqs), jnp.sin(freqs))
            q = q * cos * scale + rotate_half(q) * sin * scale
            k = k * cos / scale + rotate_half(k) * sin / scale
            return (q, k)

        def local_attention(q, k, v):
            b, h, n, d = q.shape
            w = n // WINDOW
            bq = q.reshape(b, h, w, WINDOW, d) * QK_SCALE
            bk = k.reshape(b, h, w, WINDOW, d)
            bv = v.reshape(b, h, w, WINDOW, d)

            def look_around(t):
                p = jnp.pad(t, ((0, 0), (0, 0), (1, 0), (0, 0), (0, 0)))
                return jnp.concatenate([p[:, :, :w], p[:, :, 1:]], axis=3)
            bk, bv = (look_around(bk), look_around(bv))
            bt = jnp.arange(n).reshape(w, WINDOW)
            btp = jnp.pad(bt, ((1, 0), (0, 0)), constant_values=-1)
            btk = jnp.concatenate([btp[:w], btp[1:]], axis=1)
            sim = jnp.einsum('bhwid,bhwjd->bhwij', bq, bk)
            i = bt[:, :, None]
            j = btk[:, None, :]
            mask = (i < j) | (i > j + WINDOW) | (j == -1)
            sim = jnp.where(mask, -jnp.finfo(sim.dtype).max, sim)
            attn = jax.nn.softmax(sim, axis=-1)
            out = jnp.einsum('bhwij,bhwjd->bhwid', attn, bv)
            return out.reshape(b, h, n, d)

        def _layer(x, wqkv, qs, ksc, wo, lg, lb, w1, b1, w2, b2):
            b, n, _ = x.shape
            h = shift_token(x)
            qkv = h @ wqkv
            q, k, v = jnp.split(qkv, 3, axis=-1)
            to_heads = lambda t: t.reshape(b, n, HEADS, DIM_HEAD).transpose(0, 2, 1, 3)
            q, k, v = (to_heads(q), to_heads(k), to_heads(v))
            q = l2norm(q) * qs
            k = l2norm(k) * ksc
            q, k = rotary_xpos(q, k)
            o = local_attention(q, k, v)
            o = o.transpose(0, 2, 1, 3).reshape(b, n, INNER)
            x = x + o @ wo
            h = shift_token(x)
            mu = h.mean(-1, keepdims=True)
            var = h.var(-1, keepdims=True)
            h = (h - mu) / jnp.sqrt(var + 1e-05) * lg + lb
            h = h @ w1 + b1
            a, g = jnp.split(h, 2, axis=-1)
            h = a * jax.nn.gelu(g, approximate=False)
            x = x + h @ w2 + b2
            return x
        for l in range(DEPTH):
            x = _layer(x, wqkv[l], q_scale[l], k_scale[l], wo[l], ln_g[l], ln_b[l], w1[l], b1[l], w2[l], b2[l])
        return x

    def _L2_attn_ref(x, Wqkv, bqkv, gq, gk, Wout, bout, gout):
        import jax, jax.numpy as jnp
        import numpy as np
        DIM = 128
        NUM_HEAD = 16
        DIM_HEAD = DIM // NUM_HEAD
        RMS_EPS = 1.1920929e-07
        EPS_LIN = 1e-06
        THETA = 10000.0

        def rmsnorm(x, g, eps=RMS_EPS):
            return x * jax.lax.rsqrt(jnp.mean(x * x, axis=-1, keepdims=True) + eps) * g

        def rope_cos_sin(seq_len, dim_head, dtype=jnp.float32):
            inv_freq = 1.0 / THETA ** (jnp.arange(0, dim_head, 2, dtype=dtype) / dim_head)
            t = jnp.arange(seq_len, dtype=dtype)
            freqs = jnp.outer(t, inv_freq)
            return (jnp.cos(freqs), jnp.sin(freqs))

        def apply_rope(t, cos, sin):
            tr = t[..., 0::2]
            ti = t[..., 1::2]
            out_r = tr * cos - ti * sin
            out_i = tr * sin + ti * cos
            return jnp.stack([out_r, out_i], axis=-1).reshape(t.shape)
        B, L, D = x.shape
        qkv = x @ Wqkv.T + bqkv
        q, k, v = jnp.split(qkv, 3, axis=-1)
        q = rmsnorm(q, gq)
        k = rmsnorm(k, gk)
        split = lambda t: t.reshape(B, L, NUM_HEAD, DIM_HEAD).transpose(0, 2, 1, 3)
        q, k, v = (split(q), split(k), split(v))
        cos, sin = rope_cos_sin(L, DIM_HEAD)
        cos = cos[None, None]
        sin = sin[None, None]
        q = apply_rope(q, cos, sin)
        k = apply_rope(k, cos, sin)
        qf = jax.nn.relu(q)
        kf = jax.nn.relu(k)
        vpad = jnp.concatenate([v, jnp.ones_like(v[..., :1])], axis=-1)
        vk = jnp.einsum('bhlp,bhld->bhpd', vpad, kf)
        res = jnp.einsum('bhpd,bhld->bhlp', vk, qf)
        attn = res[..., :-1] / (res[..., -1:] + EPS_LIN)
        attn = attn.transpose(0, 2, 1, 3).reshape(B, L, D)
        out = rmsnorm(attn @ Wout.T + bout, gout)
        return out

    def _L2_ffn_ref(x, W_r, W_k, W_v, mu_r, mu_k):
        import jax, jax.numpy as jnp
        import numpy as np
        DIM = 128

        def _reference_tuple_inner(x, W_r, W_k, W_v, mu_r, mu_k):
            B, T, C = x.shape
            x_prev = jnp.concatenate([jnp.zeros((B, 1, C), x.dtype), x[:, :-1, :]], axis=1)
            xr = mu_r * x + (1.0 - mu_r) * x_prev
            xk = mu_k * x + (1.0 - mu_k) * x_prev
            r = jax.nn.sigmoid(jnp.einsum('btc,dc->btd', xr, W_r))
            k = jnp.einsum('btc,dc->btd', xk, W_k)
            k_act = jnp.square(jax.nn.relu(k))
            out = r * jnp.einsum('btc,dc->btd', k_act, W_v)
            new_state = x[:, -1, :]
            return (out, new_state)
        return _reference_tuple_inner(x, W_r, W_k, W_v, mu_r, mu_k)[0]

    def _L3_attn_ref(hidden_states, qkv_w, z_w, b_w, a_w, conv_w, dt_bias, A_log, norm_w, out_w):
        import jax, jax.numpy as jnp
        import numpy as np
        from jax import lax
        B, T, HID = (4, 128, 128)
        H, DK, DV = (8, 128, 128)
        KCONV = 4
        EPS = 1e-06
        KEY_DIM = H * DK
        VAL_DIM = H * DV
        CONV_DIM = 2 * KEY_DIM + VAL_DIM
        b_, t_, _ = hidden_states.shape
        mixed = jnp.einsum('bth,ch->btc', hidden_states, qkv_w)
        x = mixed.transpose(0, 2, 1)
        x = lax.conv_general_dilated(x, conv_w, window_strides=(1,), padding=[(KCONV - 1, 0)], feature_group_count=CONV_DIM, dimension_numbers=('NCH', 'OIH', 'NCH'))
        mixed = x.transpose(0, 2, 1)
        z = jnp.einsum('bth,vh->btv', hidden_states, z_w).reshape(b_, t_, H, DV)
        bb = jnp.einsum('bth,nh->btn', hidden_states, b_w)
        aa = jnp.einsum('bth,nh->btn', hidden_states, a_w)
        q, k, v = jnp.split(mixed, 3, axis=-1)
        q = q.reshape(b_, t_, H, DK)
        k = k.reshape(b_, t_, H, DK)
        v = v.reshape(b_, t_, H, DV)
        beta = jax.nn.sigmoid(bb)
        g = -jnp.exp(A_log) * jax.nn.softplus(aa + dt_bias)
        alpha = jnp.exp(g)

        def step(S, inp):
            q_t, k_t, v_t, beta_t, alpha_t = inp
            S = S * alpha_t[..., None, None]
            kv = jnp.einsum('bhk,bhkv->bhv', k_t, S)
            S = S + jnp.einsum('bhk,bhv->bhkv', k_t, (v_t - kv) * beta_t[..., None])
            o_t = jnp.einsum('bhk,bhkv->bhv', q_t, S)
            return (S, o_t)
        qt = q.transpose(1, 0, 2, 3)
        kt = k.transpose(1, 0, 2, 3)
        vt = v.transpose(1, 0, 2, 3)
        bt = beta.transpose(1, 0, 2)
        at = alpha.transpose(1, 0, 2)
        S0 = jnp.zeros((b_, H, DK, DV), hidden_states.dtype)
        _, o = lax.scan(step, S0, (qt, kt, vt, bt, at))
        o = o.transpose(1, 0, 2, 3)
        var = jnp.mean(jnp.square(o), axis=-1, keepdims=True)
        o = o * lax.rsqrt(var + EPS) * norm_w
        o = o * (z * jax.nn.sigmoid(z))
        out = jnp.einsum('btv,hv->bth', o.reshape(b_, t_, VAL_DIM), out_w)
        return out

    def _L3_ffn_ref(x, router_w, router_b, weights1, bias1, weights2, bias2):
        import jax, jax.numpy as jnp
        import numpy as np
        B, K, D = (128, 32, 128)
        E = 32
        H = int(D * 0.25)

        def _rsqrt_uniform(key, shape, d):
            bound = d ** (-0.5)
            return jax.random.uniform(key, shape, jnp.float32, -bound, bound)
        b, k, d = x.shape
        x_flat = x.reshape(-1, d)
        n = x_flat.shape[0]
        logits = x_flat @ router_w.T + router_b
        routed_idx = jnp.argmax(logits, axis=-1)

        def expert_mlp(w1, b1, w2, b2):
            h = jax.nn.relu(x_flat @ w1 + b1)
            return jax.nn.relu(h @ w2 + b2)
        y_all = jax.vmap(expert_mlp)(weights1, bias1, weights2, bias2)
        out_flat = y_all[routed_idx, jnp.arange(n)]
        return out_flat.reshape(b, k, d)
    x = L0_attn_tokens
    x = _layernorm(x + _L0_attn_ref(x, L0_attn_wq, L0_attn_wk, L0_attn_wv, L0_attn_wo, L0_attn_w_lr, L0_attn_w_target, L0_attn_w_gates, L0_attn_rms_w), axis=-1)
    x = _layernorm(x + _L0_ffn_ref(x, L0_ffn_gate_w, L0_ffn_w1, L0_ffn_w2, L0_ffn_w3), axis=-1)
    x = _layernorm(x + _L1_attn_ref(x, L1_attn_gamma, L1_attn_w_qkv, L1_attn_w_out), axis=-1)
    x = _layernorm(x + _L1_ffn_ref(x, L1_ffn_wqkv, L1_ffn_q_scale, L1_ffn_k_scale, L1_ffn_wo, L1_ffn_ln_g, L1_ffn_ln_b, L1_ffn_w1, L1_ffn_b1, L1_ffn_w2, L1_ffn_b2), axis=-1)
    x = _layernorm(x + _L2_attn_ref(x, L2_attn_Wqkv, L2_attn_bqkv, L2_attn_gq, L2_attn_gk, L2_attn_Wout, L2_attn_bout, L2_attn_gout), axis=-1)
    x = _layernorm(x + _L2_ffn_ref(x, L2_ffn_W_r, L2_ffn_W_k, L2_ffn_W_v, L2_ffn_mu_r, L2_ffn_mu_k), axis=-1)
    x = _layernorm(x + _L3_attn_ref(x, L3_attn_qkv_w, L3_attn_z_w, L3_attn_b_w, L3_attn_a_w, L3_attn_conv_w, L3_attn_dt_bias, L3_attn_A_log, L3_attn_norm_w, L3_attn_out_w), axis=-1)
    x = _layernorm(x + _L3_ffn_ref(x, L3_ffn_router_w, L3_ffn_router_b, L3_ffn_weights1, L3_ffn_bias1, L3_ffn_weights2, L3_ffn_bias2), axis=-1)
    return x

_drawn_inputs = setup_inputs


def setup_inputs(seed=0):
    import zlib

    import numpy as np

    out = dict(_drawn_inputs(seed))
    spreads = {'L0_attn_rms_w': (1.0, 0.2),
     'L1_attn_gamma': (0.0, 0.1),
     'L1_ffn_q_scale': (1.0, 0.6),
     'L1_ffn_k_scale': (1.0, 0.6),
     'L1_ffn_ln_g': (1.0, 0.6),
     'L1_ffn_ln_b': (0.0, 0.8),
     'L1_ffn_b1': (0.0, 0.471),
     'L1_ffn_b2': (0.0, 0.1),
     'L2_attn_gq': (1.0, 0.2),
     'L2_attn_gk': (1.0, 0.541),
     'L2_attn_gout': (1.0, 0.2),
     'L3_attn_dt_bias': (1.0, 0.6),
     'L3_attn_norm_w': (1.0, 0.539)}
    factors = {'L1_ffn_w1': 3.434,
     'L1_ffn_w2': 3.38,
     'L2_ffn_mu_r': 3.041,
     'L3_attn_b_w': 8.0,
     'L3_attn_a_w': 64.0,
     'L3_attn_A_log': 64.0,
     'L3_ffn_bias1': 4.266}
    for name, (base, spread) in spreads.items():
        noise = np.random.default_rng([zlib.crc32(name.encode()), seed]).standard_normal(out[name].shape)
        drawn = base * np.exp(spread * noise) if base else spread * noise
        out[name] = jnp.asarray(drawn.astype(out[name].dtype))
    for name, factor in factors.items():
        out[name] = (out[name] * factor).astype(out[name].dtype)
    return out
```

```python
from contextlib import ExitStack, contextmanager

import numpy as np

import concourse.bass as bass
from concourse import mybir

F32 = mybir.dt.float32
BF16 = mybir.dt.bfloat16
U32 = mybir.dt.uint32
ALU = mybir.AluOpType
ACT = mybir.ActivationFunctionType
AX_X = mybir.AxisListType.X

P = 128
B, N, D = 4, 512, 128
T = N // P
TILES = B * T
TOKENS = B * N

CREDIT = 1


def give_credit(engine, *semaphores):
    for s in semaphores:
        engine.sem_inc(s, CREDIT)


class Core:

    def __init__(self, nc, stack, dram):
        self.nc, self.stack, self.dram = nc, stack, dram
        self.sems, self.spent_sems = ExitStack(), ExitStack()
        self.in_use, self.spent = [], []
        self.x_tok = self.sbuf(stack, "x_tok", [P, TILES, D])
        self.branch = self.sbuf(stack, "branch", [P, TILES, D])
        self.xn_chan = self.sbuf(stack, "xn_chan", [P, TOKENS])
        self.identity = self.sbuf(stack, "identity", [P, P])
        self.identity_bf = self.sbuf(stack, "identity_bf", [P, P], BF16)
        self.banks = [stack.enter_context(nc.psum_tensor(f"bank{i}", [P, 512], F32)) for i in range(8)]

    def sbuf(self, stack, name, shape, dtype=F32):
        return stack.enter_context(self.nc.sbuf_tensor(name, shape, dtype))

    def sem(self, name):
        s = self.sems.enter_context(self.nc.semaphore(name))
        self.in_use.append(s)
        return s

    @contextmanager
    def stage(self):
        with self.nc.Block() as block:
            yield block
        assert not self.spent, "the stage has not cleared its forerunner's semaphores"
        self.spent_sems.close()
        self.spent_sems, self.sems = self.sems, ExitStack()
        self.spent, self.in_use = self.in_use, []

    def clear_spent(self, sp):
        for s in self.spent:
            sp.sem_clear(s)
        self.spent = []


def load_tokens(core):
    nc, dram = core.nc, core.dram
    loaded = core.sem("tokens_loaded")
    converted = core.sem("identity_converted")
    with core.stage() as block:
        @block.sync
        def _(sp):
            core.clear_spent(sp)
            sp.dma_start(core.identity[:], dram["identity"]).then_inc(loaded, 16)
            sp.dma_start(core.x_tok[:], dram["tokens"].rearrange("b (t p) d -> p (b t) d", p=P)).then_inc(loaded, 16)
            sp.wait_ge(loaded, 32)

        @block.vector
        def _(dve):
            dve.wait_ge(loaded, 32)
            nc.vector.tensor_copy(core.identity_bf[:], core.identity[:]).then_inc(converted, 1)


def join(core, name, add_branch, rms=None, scale=None, scale_plus=0.0, shift=None, layernorm=False, to_chan=True,
         residual_norm=True, branch_bias=None, keep=None, store=None):
    nc, dram = core.nc, core.dram
    G = T
    with ExitStack() as st:
        def buf(n, shape, dtype=F32):
            return core.sbuf(st, f"{name}_{n}", shape, dtype)

        def sem(n):
            return core.sem(f"{name}_{n}")

        parts = buf("parts", [P, TILES, 6])
        moments = buf("moments", [P, TILES, 2])
        power = buf("power", [P, TILES])
        rstd = buf("rstd", [P, TILES])
        parts2 = buf("parts2", [P, TILES, 6])
        moments2 = buf("moments2", [P, TILES, 2])
        rstd2 = buf("rstd2", [P, TILES])
        squares = buf("squares", [P, D])
        staged = buf("staged", [P, G, D])
        column = buf("column", [P, 2])
        row = buf("row", [P, D]) if branch_bias is not None else None
        shifted = buf("shifted", [P, TILES, D]) if shift else None

        columns_loaded, column_ready = sem("columns_loaded"), sem("column_ready")
        power_ready = sem("power_ready")
        sums_ready, parts_ready, moments_ready, rstd_ready, x_ready = (
            sem("sums_ready"), sem("parts_ready"), sem("moments_ready"), sem("rstd_ready"), sem("x_ready"))
        squares_ready, mean_ready, rrms_ready = sem("squares_ready"), sem("mean_ready"), sem("rrms_ready")
        head_ready, shift_loaded = sem("head_ready"), sem("shift_loaded")
        parts2_ready, moments2_ready, rstd2_ready = sem("parts2_ready"), sem("moments2_ready"), sem("rstd2_ready")
        staged_ready, transposed, evacuated = sem("staged_ready"), sem("transposed"), sem("evacuated")
        stored, kept = sem("stored"), sem("kept")
        loads = 16 * ((scale is not None) + 2 * bool(layernorm) + (row is not None))
        norm_source = shifted if shift else core.x_tok

        with core.stage() as block:
            @block.sync
            def _(sp):
                core.clear_spent(sp)
                if scale is not None:
                    sp.dma_start(column[:, 0:1], dram[scale]).then_inc(columns_loaded, 16)
                if layernorm:
                    sp.dma_start(column[:, 0:1], dram[layernorm[0]]).then_inc(columns_loaded, 16)
                    sp.dma_start(column[:, 1:2], dram[layernorm[1]]).then_inc(columns_loaded, 16)
                if row is not None:
                    sp.dma_start(row[:], dram[branch_bias].partition_broadcast(P)).then_inc(columns_loaded, 16)
                if loads:
                    sp.wait_ge(columns_loaded, loads)
                if store is not None:
                    sp.wait_ge(x_ready, B)
                    sp.dma_start(store.rearrange("b (t p) d -> p (b t) d", p=P), core.x_tok[:]).then_inc(stored, 16)
                    sp.wait_ge(stored, 16)
                if shift:
                    if add_branch:
                        sp.wait_ge(x_ready, B)
                    sp.wait_ge(head_ready, 2)
                    sp.dma_start(shifted[1:P, :, 64:D], core.x_tok[0:P - 1, :, 64:D]).then_inc(shift_loaded, 16)
                    for b in range(B):
                        sp.dma_start(shifted[0:1, b * T + 1:(b + 1) * T, 64:D],
                                     core.x_tok[P - 1:P, b * T:(b + 1) * T - 1, 64:D]).then_inc(shift_loaded, 16)

            @block.vector
            def _(dve):
                if add_branch:
                    if row is not None:
                        dve.wait_ge(columns_loaded, loads)
                    with dve.Fori(0, B) as g:
                        x_g = core.x_tok[:, bass.ts(g, G), :]
                        br_g = core.branch[:, bass.ts(g, G), :]
                        if row is not None:
                            nc.vector.tensor_tensor(br_g, br_g, row[:].unsqueeze(1).broadcast_to([P, G, D]),
                                                    ALU.add).then_inc(sums_ready, 1)
                            dve.wait_ge(sums_ready, (2 if residual_norm else 1) * g + 1)
                        nc.vector.tensor_tensor(x_g, x_g, br_g, ALU.add).then_inc(
                            sums_ready if residual_norm else x_ready, 1)
                        if residual_norm:
                            dve.wait_ge(sums_ready, (2 * g + 2) if row is not None else (g + 1))
                            for i in range(G):
                                nc.vector.bn_stats(parts[:, bass.ds(g * G + i, 1), :],
                                                   core.x_tok[:, bass.ds(g * G + i, 1), :]).then_inc(parts_ready, 1)
                    if residual_norm:
                        for i in range(TILES):
                            dve.wait_ge(parts_ready, i + 1)
                            nc.vector.bn_aggr(moments[:, i, :], parts[:, i, :]).then_inc(moments_ready, 1)
                        dve.wait_ge(rstd_ready, 2)
                        with dve.Fori(0, B) as g:
                            for i in range(G):
                                x_i = core.x_tok[:, bass.ds(g * G + i, 1), :]
                                tick = nc.vector.tensor_scalar(
                                    x_i, x_i, moments[:, bass.ds(g * G + i, 1), 0:1],
                                    rstd[:, bass.ds(g * G + i, 1)], ALU.subtract, ALU.mult)
                            tick.then_inc(x_ready, 1)
                if shift:
                    if add_branch:
                        dve.wait_ge(x_ready, B)
                    for b in range(B):
                        tick = nc.vector.memset(shifted[0:1, b * T, 64:D], 0.0)
                    tick.then_inc(head_ready, 1)
                    nc.vector.tensor_copy(shifted[:, :, 0:64], core.x_tok[:, :, 0:64]).then_inc(head_ready, 1)
                    dve.wait_ge(head_ready, 2)
                    dve.wait_ge(shift_loaded, 16 * (B + 1))
                if layernorm:
                    for i in range(TILES):
                        nc.vector.bn_stats(parts2[:, i, :], shifted[:, i, :]).then_inc(parts2_ready, 1)
                    for i in range(TILES):
                        dve.wait_ge(parts2_ready, i + 1)
                        nc.vector.bn_aggr(moments2[:, i, :], parts2[:, i, :]).then_inc(moments2_ready, 1)
                    dve.wait_ge(rstd2_ready, 2)
                if rms is not None:
                    dve.wait_ge(squares_ready, CREDIT + TILES)
                    eps, floor = rms
                    nc.vector.tensor_scalar(rstd2[:], rstd2[:], 1.0 / D, eps, ALU.mult, ALU.add).then_inc(mean_ready, 1)
                    dve.wait_ge(mean_ready, 1)
                    nc.vector.tensor_scalar(rstd2[:], rstd2[:], floor, None, ALU.max).then_inc(mean_ready, 1)
                    dve.wait_ge(rrms_ready, 1)
                if scale is not None:
                    dve.wait_ge(columns_loaded, loads)
                    nc.vector.tensor_scalar(column[:, 0:1], column[:, 0:1], scale_plus, None,
                                            ALU.add).then_inc(column_ready, 1)
                if to_chan:
                    with dve.Fori(0, B) as g:
                        dve.wait_ge(transposed, CREDIT + g)
                        if layernorm:
                            for i in range(G):
                                tick = nc.vector.tensor_scalar(
                                    staged[:, i, :], norm_source[:, bass.ds(g * G + i, 1), :],
                                    moments2[:, bass.ds(g * G + i, 1), 0:1], rstd2[:, bass.ds(g * G + i, 1)],
                                    ALU.subtract, ALU.mult)
                        elif rms is not None:
                            for i in range(G):
                                tick = nc.vector.tensor_scalar(
                                    staged[:, i, :], norm_source[:, bass.ds(g * G + i, 1), :],
                                    rstd2[:, bass.ds(g * G + i, 1)], None, ALU.mult)
                        else:
                            if add_branch and not shift:
                                dve.wait_ge(x_ready, g + 1)
                            tick = nc.vector.tensor_copy(staged[:], norm_source[:, bass.ts(g, G), :])
                        tick.then_inc(staged_ready, 1)

            @block.gpsimd
            def _(pool):
                nc.gpsimd.memset(power[:], -0.5).then_inc(power_ready, 1)
                pool.wait_ge(power_ready, 1)
                if add_branch and residual_norm:
                    pool.wait_ge(moments_ready, TILES)
                    nc.gpsimd.tensor_scalar(rstd[:], moments[:, :, 1], 1e-5, None, ALU.add).then_inc(rstd_ready, 1)
                    pool.wait_ge(rstd_ready, 1)
                    nc.gpsimd.tensor_tensor(rstd[:], rstd[:], power[:], ALU.pow).then_inc(rstd_ready, 1)
                if keep is not None:
                    pool.wait_ge(x_ready, B)
                    nc.gpsimd.tensor_copy(keep[:], core.x_tok[:]).then_inc(kept, 1)
                if layernorm:
                    pool.wait_ge(moments2_ready, TILES)
                    nc.gpsimd.tensor_scalar(rstd2[:], moments2[:, :, 1], 1e-5, None, ALU.add).then_inc(rstd2_ready, 1)
                    pool.wait_ge(rstd2_ready, 1)
                    nc.gpsimd.tensor_tensor(rstd2[:], rstd2[:], power[:], ALU.pow).then_inc(rstd2_ready, 1)
                if rms is not None:
                    pool.wait_ge(mean_ready, 2)
                    nc.gpsimd.tensor_tensor(rstd2[:], rstd2[:], power[:], ALU.pow).then_inc(rrms_ready, 1)

            @block.scalar
            def _(act):
                if rms is not None:
                    give_credit(act, squares_ready)
                    with act.Fori(0, B) as g:
                        if add_branch:
                            act.wait_ge(x_ready, g + 1)
                        for i in range(G):
                            act.wait_ge(squares_ready, CREDIT + g * G + i)
                            nc.scalar.activation(squares[:], core.x_tok[:, bass.ds(g * G + i, 1), :], ACT.Square,
                                                 accum_out=rstd2[:, bass.ds(g * G + i, 1)]).then_inc(squares_ready, 1)
                if to_chan:
                    if scale is not None:
                        act.wait_ge(column_ready, 1)
                    if layernorm:
                        act.wait_ge(columns_loaded, loads)
                    give_credit(act, evacuated)
                    with act.Fori(0, B) as g:
                        act.wait_ge(transposed, CREDIT + g + 1)
                        out = core.xn_chan[:, bass.ts(g, G * P)]
                        if layernorm:
                            tick = nc.scalar.activation(out, core.banks[0][:], ACT.Identity, bias=column[:, 1:2],
                                                        scale=column[:, 0:1])
                        elif scale is not None:
                            tick = nc.scalar.activation(out, core.banks[0][:], ACT.Copy, scale=column[:, 0:1])
                        else:
                            tick = nc.scalar.copy(out, core.banks[0][:])
                        tick.then_inc(evacuated, 1)

            @block.tensor
            def _(pe):
                if to_chan:
                    give_credit(pe, transposed)
                    with pe.Fori(0, B) as g:
                        pe.wait_ge(staged_ready, g + 1)
                        pe.wait_ge(evacuated, CREDIT + g)
                        for i in range(G):
                            tick = nc.tensor.transpose(core.banks[0][:, bass.ts(i, P)], staged[:, i, :],
                                                       core.identity[:])
                        tick.then_inc(transposed, 1)


def attention(core, name, weights, pairs, causal=False, gates=None):
    nc, dram = core.nc, core.dram
    E = 64
    STEPS = B * 2 * T
    LAG_T, LAG_PV = 2, 3
    OT_AT, OUT_AT, ADD_AT = 13, 14, 15
    WO_AT = 6
    POSITIONS = 8 * (B - 1) + ADD_AT + 1
    S_RING, P_RING, PT_RING = 2, 3, 2
    with ExitStack() as st:
        def buf(n, shape, dtype=F32):
            return core.sbuf(st, f"{name}_{n}", shape, dtype)

        def sem(n):
            return core.sem(f"{name}_{n}")

        w_land, w_now = buf("w_land", [P, 4, P]), buf("w_now", [P, 4, P])
        q_chan, k_chan, v_tok = buf("q_chan", [P, 2, N]), buf("k_chan", [P, 2, N]), buf("v_tok", [P, 2, T, P])
        neg_max, row_sum = buf("neg_max", [P, STEPS]), buf("row_sum", [P, STEPS])
        coef = buf("coef", [P, STEPS])
        probs, probs_t = buf("probs", [P, P_RING, N]), buf("probs_t", [P, PT_RING, T, P])
        heads_out, heads_out_t = buf("heads_out", [P, T, P]), buf("heads_out_t", [P, T, P])
        proj_bank = core.banks[0]
        score_banks = core.banks[1:1 + S_RING]
        pt_banks = core.banks[3:3 + PT_RING]
        pv_banks, out_bank = core.banks[5:7], core.banks[7]
        if causal:
            mask_f, mask = buf("mask_f", [P, P]), buf("mask", [P, P], BF16)
        if gates:
            w_gates, gate = buf("w_gates", [P, 2 * pairs]), buf("gate", [P, 2 * pairs, TILES])

        constants_loaded, mask_ready = sem("constants_loaded"), sem("mask_ready")
        gate_scores_ready, gate_ready = sem("gate_scores_ready"), sem("gate_ready")
        branch_zeroed = sem("branch_zeroed")
        w_loaded, w_ready, wo_ready = sem("w_loaded"), sem("w_ready"), sem("wo_ready")
        proj_ready, proj_copied = sem("proj_ready"), sem("proj_copied")
        scores_ready, max_ready, probs_ready = sem("scores_ready"), sem("max_ready"), sem("probs_ready")
        pt_ready, pt_copied, pv_ready = sem("pt_ready"), sem("pt_copied"), sem("pv_ready")
        inverse_ready, coef_ready, normed = sem("inverse_ready"), sem("coef_ready"), sem("normed")
        ot_ready, ot_copied, out_ready, added = sem("ot_ready"), sem("ot_copied"), sem("out_ready"), sem("added")
        n_constants = 16 * (bool(causal) + bool(gates))

        def width(s):
            return (s % T + 1) * P if causal else N

        with core.stage() as block:
            @block.sync
            def _(sp):
                core.clear_spent(sp)
                if causal:
                    sp.dma_start(mask_f[:], dram["causal_mask"]).then_inc(constants_loaded, 16)
                if gates:
                    sp.dma_start(w_gates[:], dram[gates]).then_inc(constants_loaded, 16)
                with sp.Fori(0, pairs) as pair:
                    sp.wait_ge(wo_ready, CREDIT + pair)
                    sp.dma_start(w_land[:], dram[weights][bass.ds(pair, 1), :, :, :]).then_inc(w_loaded, 16)

            @block.gpsimd
            def _(pool):
                nc.gpsimd.memset(core.branch[:], 0.0).then_inc(branch_zeroed, 1)

            @block.tensor
            def _(pe):
                if gates:
                    pe.wait_ge(constants_loaded, n_constants)
                    for t in range(TILES):
                        tick = nc.tensor.matmul(out_bank[:, t * 2 * pairs:(t + 1) * 2 * pairs],
                                                core.xn_chan[:, bass.ts(t, P)], w_gates[:])
                    tick.then_inc(gate_scores_ready, 1)
                if causal:
                    pe.wait_ge(mask_ready, 1)

                def project(pair, b, which):
                    pe.wait_ge(proj_copied, CREDIT + 3 * B * pair + (3 * b + which))
                    if which < 2:
                        tick = nc.tensor.matmul(proj_bank[:], w_now[:, which, :], core.xn_chan[:, bass.ts(b, N)])
                    else:
                        for t in range(T):
                            tick = nc.tensor.matmul(proj_bank[:, bass.ts(t, P)],
                                                    core.xn_chan[:, bass.ts(b * T + t, P)], w_now[:, 2, :])
                    tick.then_inc(proj_ready, 1)

                def scores(pair, s):
                    b, h, i = s // (2 * T), s // T % 2, s % T
                    if s % (2 * T) == 0:
                        pe.wait_ge(proj_copied, CREDIT + 3 * B * pair + (3 * b + 3))
                    if s >= S_RING:
                        pe.wait_ge(probs_ready, STEPS * pair + (s - S_RING + 1))
                    rows = slice(h * E, (h + 1) * E)
                    bank = score_banks[s % S_RING]
                    tick = nc.tensor.matmul(bank[:, 0:width(s)], q_chan[rows, b % 2, bass.ts(i, P)],
                                            k_chan[rows, b % 2, 0:width(s)], start=True, stop=not causal)
                    if causal:
                        tick = nc.tensor.matmul(bank[:, i * P:(i + 1) * P], core.identity_bf[:], mask[:],
                                                start=False, stop=True)
                    tick.then_inc(scores_ready, 1)

                def transpose(pair, s):
                    pe.wait_ge(probs_ready, STEPS * pair + (s + 1))
                    if s >= PT_RING:
                        pe.wait_ge(pt_copied, STEPS * pair + (s - PT_RING + 1))
                    for j in range(width(s) // P):
                        tick = nc.tensor.transpose(pt_banks[s % PT_RING][:, bass.ts(j, P)],
                                                   probs[:, s % P_RING, bass.ts(j, P)], core.identity[:])
                    tick.then_inc(pt_ready, 1)

                def product(pair, s):
                    b, h, i = s // (2 * T), s // T % 2, s % T
                    pe.wait_ge(pt_copied, STEPS * pair + (s + 1))
                    if i == 0 and b > 0:
                        pe.wait_ge(normed, 2 * B * pair + (2 * b + h - 1))
                    for j in range(width(s) // P):
                        tick = nc.tensor.matmul(pv_banks[h][:, bass.ts(i, E)],
                                                probs_t[:, s % PT_RING, j, :], v_tok[:, b % 2, j, h * E:(h + 1) * E],
                                                start=(j == 0), stop=(j == width(s) // P - 1))
                    tick.then_inc(pv_ready, 1)

                def out_transpose(pair, b):
                    pe.wait_ge(normed, 2 * B * pair + (2 * b + 2))
                    pe.wait_ge(added, CREDIT + B * pair + b)
                    for t in range(T):
                        tick = nc.tensor.transpose(out_bank[:, bass.ts(t, P)], heads_out[:, t, :], core.identity[:])
                    tick.then_inc(ot_ready, 1)

                def out_product(pair, b):
                    pe.wait_ge(ot_copied, CREDIT + B * pair + (b + 1))
                    if b == 0:
                        pe.wait_ge(wo_ready, CREDIT + pair + 1)
                    for t in range(T):
                        tick = nc.tensor.matmul(out_bank[:, bass.ts(t, P)], heads_out_t[:, t, :], w_now[:, 3, :])
                    tick.then_inc(out_ready, 1)

                if gates:
                    pe.wait_ge(gate_ready, 1)
                give_credit(pe, out_ready, ot_ready)
                with pe.Fori(0, pairs) as pair:
                    pe.wait_ge(w_ready, pair + 1)
                    for which in range(3):
                        project(pair, 0, which)
                    for at in range(POSITIONS):
                        if at < STEPS:
                            scores(pair, at)
                        if at < STEPS - 2 * T and at % (2 * T) in (2, 4, 6):
                            project(pair, at // (2 * T) + 1, at % (2 * T) // 2 - 1)
                        if 0 <= at - LAG_T < STEPS:
                            transpose(pair, at - LAG_T)
                        if 0 <= at - LAG_PV < STEPS:
                            product(pair, at - LAG_PV)
                        if at >= OT_AT and (at - OT_AT) % 8 == 0:
                            out_transpose(pair, (at - OT_AT) // 8)
                        if at >= OUT_AT and (at - OUT_AT) % 8 == 0:
                            out_product(pair, (at - OUT_AT) // 8)

            @block.scalar
            def _(act):
                if gates:
                    act.wait_ge(gate_scores_ready, 1)
                    nc.scalar.activation(gate[:].rearrange("p h t -> p t h"),
                                         out_bank[:, 0:TILES * 2 * pairs].rearrange("p (t h) -> p t h", t=TILES),
                                         ACT.Sigmoid).then_inc(gate_ready, 1)

                def copy_projection(pair, b, which):
                    act.wait_ge(proj_ready, 3 * B * pair + (3 * b + which + 1))
                    if which == 0:
                        tick = nc.scalar.activation(q_chan[:, b % 2, :], proj_bank[:], ACT.Copy, scale=E ** -0.5)
                    elif which == 1:
                        tick = nc.scalar.copy(k_chan[:, b % 2, :], proj_bank[:])
                    else:
                        tick = nc.scalar.copy(v_tok[:, b % 2, :, :], proj_bank[:].rearrange("p (t c) -> p t c", t=T))
                    tick.then_inc(proj_copied, 1)

                give_credit(act, proj_copied, ot_copied, wo_ready)
                with act.Fori(0, pairs) as pair:
                    act.wait_ge(w_loaded, 16 * pair + 16)
                    nc.scalar.copy(w_now[:, 0:3, :], w_land[:, 0:3, :]).then_inc(w_ready, 1)
                    for which in range(3):
                        copy_projection(pair, 0, which)
                    for at in range(POSITIONS):
                        if at < STEPS:
                            act.wait_ge(max_ready, STEPS * pair + (at + 1))
                            if at >= P_RING:
                                act.wait_ge(pt_ready, STEPS * pair + (at - P_RING + 1))
                            nc.scalar.activation(probs[:, at % P_RING, 0:width(at)],
                                                 score_banks[at % S_RING][:, 0:width(at)], ACT.Exp,
                                                 bias=neg_max[:, at:at + 1],
                                                 accum_out=row_sum[:, at:at + 1]).then_inc(probs_ready, 1)
                        if at < STEPS - 2 * T and at % (2 * T) in (2, 4, 6):
                            copy_projection(pair, at // (2 * T) + 1, at % (2 * T) // 2 - 1)
                        if at == WO_AT:
                            act.wait_ge(out_ready, CREDIT + B * pair)
                            nc.scalar.copy(w_now[:, 3, :], w_land[:, 3, :]).then_inc(wo_ready, 1)
                        if at >= OT_AT and (at - OT_AT) % 8 == 0:
                            b = (at - OT_AT) // 8
                            act.wait_ge(ot_ready, CREDIT + B * pair + (b + 1))
                            act.wait_ge(out_ready, CREDIT + B * pair + b)
                            nc.scalar.copy(heads_out_t[:], out_bank[:].rearrange("p (t c) -> p t c", t=T)
                                           ).then_inc(ot_copied, 1)

            @block.vector
            def _(dve):
                if causal:
                    dve.wait_ge(constants_loaded, n_constants)
                    nc.vector.tensor_copy(mask[:], mask_f[:]).then_inc(mask_ready, 1)

                def normalize(pair, b, h):
                    s = (2 * b + h) * T
                    steps = slice(s, s + T)
                    dve.wait_ge(probs_ready, STEPS * pair + (s + T))
                    nc.vector.reciprocal(coef[:, steps], row_sum[:, steps]).then_inc(inverse_ready, 1)
                    dve.wait_ge(inverse_ready, 2 * B * pair + (2 * b + h + 1))
                    if gates:
                        nc.vector.tensor_tensor(coef[:, steps], coef[:, steps],
                                                gate[:, bass.ds(pair * 2 + h, 1), b * T:(b + 1) * T].rearrange(
                                                    "p o t -> p (o t)"), ALU.mult).then_inc(coef_ready, 1)
                        dve.wait_ge(coef_ready, 2 * B * pair + (2 * b + h + 1))
                    dve.wait_ge(pv_ready, STEPS * pair + (s + T))
                    dve.wait_ge(ot_ready, CREDIT + B * pair + b)
                    nc.vector.tensor_tensor(
                        heads_out[:, :, h * E:(h + 1) * E],
                        pv_banks[h][:, 0:T * E].rearrange("p (t c) -> p t c", t=T),
                        coef[:, steps].unsqueeze(2).broadcast_to([P, T, E]), ALU.mult).then_inc(normed, 1)

                if gates:
                    dve.wait_ge(gate_ready, 1)
                dve.wait_ge(branch_zeroed, 1)
                give_credit(dve, added)
                with dve.Fori(0, pairs) as pair:
                    for at in range(POSITIONS):
                        if at < STEPS:
                            dve.wait_ge(scores_ready, STEPS * pair + (at + 1))
                            nc.vector.tensor_reduce(neg_max[:, at:at + 1], score_banks[at % S_RING][:, 0:width(at)],
                                                    AX_X, ALU.max, negate=True).then_inc(max_ready, 1)
                        s = at - LAG_T
                        if 0 <= s < STEPS:
                            dve.wait_ge(pt_ready, STEPS * pair + (s + 1))
                            if s >= PT_RING:
                                dve.wait_ge(pv_ready, STEPS * pair + (s - PT_RING + 1))
                            nc.vector.tensor_copy(
                                probs_t[:, s % PT_RING, 0:width(s) // P, :],
                                pt_banks[s % PT_RING][:, 0:width(s)].rearrange("p (j c) -> p j c", c=P)
                            ).then_inc(pt_copied, 1)
                        if at >= 7 and (at - 7) % 4 == 0 and (at - 7) // 4 < 2 * B:
                            normalize(pair, (at - 7) // 8, (at - 7) // 4 % 2)
                        if at >= ADD_AT and (at - ADD_AT) % 8 == 0:
                            b = (at - ADD_AT) // 8
                            dve.wait_ge(out_ready, CREDIT + B * pair + (b + 1))
                            dve.wait_ge(added, CREDIT + B * pair + b)
                            acc = core.branch[:, b * T:(b + 1) * T, :]
                            nc.vector.tensor_tensor(acc, acc, out_bank[:].rearrange("p (t c) -> p t c", t=T),
                                                    ALU.add).then_inc(added, 1)


def two_of_eight(core, name, weights, gate):
    nc, dram = core.nc, core.dram
    X = 8
    HALF = 2
    STEPS = B * HALF
    LAG = 2
    with ExitStack() as st:
        def buf(n, shape, dtype=F32):
            return core.sbuf(st, f"{name}_{n}", shape, dtype)

        def sem(n):
            return core.sem(f"{name}_{n}")

        w_gate, numbers = buf("w_gate", [P, X]), buf("numbers", [P, X])
        score, top = buf("score", [P, TILES, X]), buf("top", [P, TILES, X])
        extreme = buf("extreme", [P, TILES])
        places, places_f = buf("places", [P, TILES, X], U32), buf("places_f", [P, TILES, X])
        chosen, chosen2 = buf("chosen", [P, TILES, X]), buf("chosen2", [P, TILES, X])
        w = [buf(f"w{u}", [P, 3, 2 * P]) for u in range(2)]
        gated, hidden = buf("gated", [P, 2, N]), buf("hidden", [P, 4, N])
        gate_bank = core.banks[6]
        w1_banks, w3_banks, y_banks = core.banks[0:2], core.banks[2:4], core.banks[4:6]

        loaded, logits_ready, zeroed = sem("loaded"), sem("logits_ready"), sem("zeroed")
        softmax_step, exp_ready, chosen_ready = sem("softmax_step"), sem("exp_ready"), sem("chosen_ready")
        w_loaded = [sem(f"w_loaded{u}") for u in range(2)]
        w1_ready, w3_ready, silu_ready = sem("w1_ready"), sem("w3_ready"), sem("silu_ready")
        hidden_ready, added = sem("hidden_ready"), sem("added")
        y_ready = [sem(f"y_ready{u}") for u in range(2)]

        with core.stage() as block:
            @block.sync
            def _(sp):
                core.clear_spent(sp)
                sp.dma_start(w_gate[:], dram[gate]).then_inc(loaded, 16)
                sp.dma_start(numbers[:], dram["numbers8"].partition_broadcast(P)).then_inc(loaded, 16)
                with sp.Fori(0, X // 2) as turn:
                    for u in range(2):
                        sp.wait_ge(y_ready[u], CREDIT + B * turn)
                        sp.dma_start(w[u][:], dram[weights][bass.ds(turn * 2 + u, 1), :, :, :]).then_inc(w_loaded[u], 16)

            @block.gpsimd
            def _(pool):
                nc.gpsimd.memset(core.branch[:], 0.0).then_inc(zeroed, 1)

            @block.tensor
            def _(pe):
                pe.wait_ge(loaded, 32)
                for t in range(TILES):
                    tick = nc.tensor.matmul(gate_bank[:, bass.ts(t, X)], core.xn_chan[:, bass.ts(t, P)], w_gate[:])
                tick.then_inc(logits_ready, 1)
                give_credit(pe, *y_ready)
                with pe.Fori(0, X // 2) as turn:
                    for u in range(2):
                        pe.wait_ge(w_loaded[u], 16 * turn + 16)
                        for at in range(STEPS + LAG):
                            if at < STEPS:
                                b, half = at // HALF, at % HALF
                                n = STEPS * u + at
                                x = core.xn_chan[:, bass.ts(b, N)]
                                if n >= 2:
                                    pe.wait_ge(silu_ready, 2 * STEPS * turn + (n - 1))
                                nc.tensor.matmul(w1_banks[at % 2][:], w[u][:, 0, bass.ts(half, P)], x
                                                 ).then_inc(w1_ready, 1)
                                if n >= 2:
                                    pe.wait_ge(hidden_ready, 2 * STEPS * turn + (n - 1))
                                nc.tensor.matmul(w3_banks[at % 2][:], w[u][:, 1, bass.ts(half, P)], x
                                                 ).then_inc(w3_ready, 1)
                            if at >= LAG and at % 2 == 1:
                                b = (at - LAG) // HALF
                                m = B * u + b
                                pe.wait_ge(hidden_ready, 2 * STEPS * turn + (STEPS * u + 2 * b + 2))
                                if m >= 2:
                                    pe.wait_ge(added, CREDIT + 2 * B * turn + (m - 1))
                                for t in range(T):
                                    for half in range(HALF):
                                        tick = nc.tensor.matmul(
                                            y_banks[b % 2][:, bass.ts(t, P)],
                                            hidden[:, 2 * (b % 2) + half, bass.ts(t, P)],
                                            w[u][:, 2, bass.ts(half, P)], start=(half == 0), stop=(half == 1))
                                tick.then_inc(y_ready[u], 1)

            @block.scalar
            def _(act):
                act.wait_ge(softmax_step, 2)
                nc.scalar.activation(score[:], score[:], ACT.Exp).then_inc(exp_ready, 1)
                with act.Fori(0, X // 2) as turn:
                    for n in range(2 * STEPS):
                        act.wait_ge(w1_ready, 2 * STEPS * turn + (n + 1))
                        if n >= 2:
                            act.wait_ge(hidden_ready, 2 * STEPS * turn + (n - 1))
                        nc.scalar.activation(gated[:, n % 2, :], w1_banks[n % 2][:], ACT.Silu).then_inc(silu_ready, 1)

            @block.vector
            def _(dve):
                dve.wait_ge(logits_ready, 1)
                logits = gate_bank[:, 0:TILES * X].rearrange("p (t e) -> p t e", e=X)
                nc.vector.tensor_reduce(extreme[:], logits, AX_X, ALU.max).then_inc(softmax_step, 1)
                dve.wait_ge(softmax_step, 1)
                nc.vector.tensor_tensor(score[:], logits, extreme[:].unsqueeze(2).broadcast_to([P, TILES, X]),
                                        ALU.subtract).then_inc(softmax_step, 1)
                dve.wait_ge(exp_ready, 1)
                nc.vector.tensor_reduce(extreme[:], score[:], AX_X, ALU.add).then_inc(softmax_step, 1)
                dve.wait_ge(softmax_step, 3)
                nc.vector.reciprocal(extreme[:], extreme[:]).then_inc(softmax_step, 1)
                dve.wait_ge(softmax_step, 4)
                nc.vector.tensor_tensor(score[:], score[:], extreme[:].unsqueeze(2).broadcast_to([P, TILES, X]),
                                        ALU.mult).then_inc(softmax_step, 1)
                dve.wait_ge(softmax_step, 5)
                for t in range(TILES):
                    nc.vector.max(top[:, t, :], score[:, t, :]).then_inc(chosen_ready, 1)
                for t in range(TILES):
                    dve.wait_ge(chosen_ready, t + 1)
                    tick = nc.vector.max_index(places[:, t, :], top[:, t, :], score[:, t, :])
                tick.then_inc(softmax_step, 1)
                dve.wait_ge(softmax_step, 6)
                nc.vector.tensor_copy(places_f[:], places[:]).then_inc(softmax_step, 1)
                dve.wait_ge(softmax_step, 7)
                dve.wait_ge(loaded, 32)
                number = numbers[:].unsqueeze(1).broadcast_to([P, TILES, X])
                for k, c in enumerate((chosen, chosen2)):
                    nc.vector.tensor_tensor(c[:], number, places_f[:, :, k:k + 1].broadcast_to([P, TILES, X]),
                                            ALU.is_equal).then_inc(softmax_step, 1)
                dve.wait_ge(softmax_step, 9)
                nc.vector.tensor_tensor(chosen[:], chosen[:], chosen2[:], ALU.add).then_inc(softmax_step, 1)
                dve.wait_ge(softmax_step, 10)
                nc.vector.tensor_tensor(score[:], score[:], chosen[:], ALU.mult).then_inc(softmax_step, 1)
                dve.wait_ge(softmax_step, 11)
                dve.wait_ge(zeroed, 1)
                give_credit(dve, added)
                with dve.Fori(0, X // 2) as turn:
                    for u in range(2):
                        for at in range(STEPS + LAG):
                            n = STEPS * u + at
                            if at < STEPS:
                                dve.wait_ge(silu_ready, 2 * STEPS * turn + (n + 1))
                                dve.wait_ge(w3_ready, 2 * STEPS * turn + (n + 1))
                                if n >= 4:
                                    m = (n - 4) // HALF
                                    dve.wait_ge(y_ready[m // B], CREDIT + B * turn + (m % B + 1))
                                nc.vector.tensor_tensor(hidden[:, at % 4, :], gated[:, n % 2, :], w3_banks[at % 2][:],
                                                        ALU.mult).then_inc(hidden_ready, 1)
                            if at >= LAG and at % 2 == 1:
                                b = (at - LAG) // HALF
                                m = B * u + b
                                dve.wait_ge(y_ready[u], CREDIT + B * turn + (b + 1))
                                for t in range(T):
                                    acc = core.branch[:, b * T + t, :]
                                    tick = nc.vector.scalar_tensor_tensor(
                                        acc, y_banks[b % 2][:, bass.ts(t, P)],
                                        score[:, b * T + t, bass.ds(turn * 2 + u, 1)], acc, ALU.mult, ALU.add)
                                tick.then_inc(added, 1)
                                if b == B - 1:
                                    dve.wait_ge(added, CREDIT + 2 * B * turn + (m + 1))


def one_of_many(core, name):
    nc, dram = core.nc, core.dram
    X, GROUPS = 32, 8
    with ExitStack() as st:
        def buf(n, shape, dtype=F32):
            return core.sbuf(st, f"{name}_{n}", shape, dtype)

        def sem(n):
            return core.sem(f"{name}_{n}")

        w_router, router_b, numbers = buf("w_router", [P, X]), buf("router_b", [P, X]), buf("numbers", [P, X])
        w1, b1 = buf("w1", [P, GROUPS, P]), buf("b1", [P, GROUPS])
        w2, b2 = buf("w2", [P, GROUPS, D]), buf("b2", [X, D])
        spread_f, spread = buf("spread_f", [X, GROUPS, P]), buf("spread", [X, GROUPS, P], BF16)
        logits, top = buf("logits", [P, TILES, X]), buf("top", [P, TILES, 8])
        places, places_f = buf("places", [P, TILES, 8], U32), buf("places_f", [P, TILES])
        onehot, onehot_t = buf("onehot", [P, TILES, X]), buf("onehot_t", [X, TOKENS])
        onehot_bf = buf("onehot_bf", [X, TOKENS], BF16)
        relued, hidden = buf("relued", [P, 2, N]), buf("hidden", [P, GROUPS, N])
        summed = buf("summed", [P, N])
        h_banks, mask_banks, y_bank = core.banks[0:2], core.banks[2:4], core.banks[4]

        loaded, logits_ready, step = sem("loaded"), sem("logits_ready"), sem("step")
        top_ready, onehot_ready, t_ready, t_copied = (
            sem("top_ready"), sem("onehot_ready"), sem("t_ready"), sem("t_copied"))
        bias_ready, bias_copied, spread_ready = sem("bias_ready"), sem("bias_copied"), sem("spread_ready")
        h_ready, mask_ready, relu_ready, hidden_ready = (
            sem("h_ready"), sem("mask_ready"), sem("relu_ready"), sem("hidden_ready"))
        y_ready, summed_ready, finished = sem("y_ready"), sem("summed_ready"), sem("finished")
        names = [(w_router, "w_router", False), (router_b, "router_b", True), (numbers, "numbers32", True),
                 (w1, "w1_many", False), (b1, "b1_many", False), (w2, "w2_many", False), (b2, "b2_many", False),
                 (spread_f, "spread", False)]

        with core.stage() as block:
            @block.sync
            def _(sp):
                core.clear_spent(sp)
                for place, source, every_partition in names:
                    src = dram[source].partition_broadcast(P) if every_partition else dram[source]
                    sp.dma_start(place[:], src).then_inc(loaded, 16)

            @block.tensor
            def _(pe):
                pe.wait_ge(loaded, 16 * len(names))
                for t in range(TILES):
                    tick = nc.tensor.matmul(y_bank[:, bass.ts(t, X)], core.xn_chan[:, bass.ts(t, P)], w_router[:])
                tick.then_inc(logits_ready, 1)
                pe.wait_ge(onehot_ready, 1)
                for b in range(B):
                    for t in range(T):
                        tick = nc.tensor.transpose(core.banks[b][0:X, bass.ts(t, P)], onehot[:, b * T + t, :],
                                                   core.identity[:])
                    tick.then_inc(t_ready, 1)
                for b in range(B):
                    pe.wait_ge(t_copied, b + 1)
                    for t in range(T):
                        tick = nc.tensor.matmul(core.banks[b + 4][:, bass.ts(t, P)],
                                                onehot_t[:, bass.ts(b * T + t, P)], b2[:])
                    tick.then_inc(bias_ready, 1)
                pe.wait_ge(t_copied, B + 1)
                pe.wait_ge(spread_ready, 1)
                pe.wait_ge(bias_copied, B)
                with pe.Fori(0, B) as b:
                    x = core.xn_chan[:, bass.ts(b, N)]
                    for g in range(GROUPS):
                        if g >= 2:
                            pe.wait_ge(relu_ready, GROUPS * b + (g - 1))
                            pe.wait_ge(hidden_ready, GROUPS * b + (g - 1))
                        nc.tensor.matmul(h_banks[g % 2][:], w1[:, g, :], x).then_inc(h_ready, 1)
                        nc.tensor.matmul(mask_banks[g % 2][:], spread[:, g, :], onehot_bf[:, bass.ts(b, N)]
                                         ).then_inc(mask_ready, 1)
                    pe.wait_ge(hidden_ready, GROUPS * b + GROUPS)
                    pe.wait_ge(summed_ready, CREDIT + b)
                    for t in range(T):
                        for g in range(GROUPS):
                            tick = nc.tensor.matmul(y_bank[:, bass.ts(t, P)], hidden[:, g, bass.ts(t, P)], w2[:, g, :],
                                                    start=(g == 0), stop=(g == GROUPS - 1))
                    tick.then_inc(y_ready, 1)

            @block.scalar
            def _(act):
                act.wait_ge(loaded, 16 * len(names))
                nc.scalar.copy(spread[:], spread_f[:]).then_inc(spread_ready, 1)
                for b in range(B):
                    act.wait_ge(bias_ready, b + 1)
                    nc.scalar.copy(core.branch[:, bass.ts(b, T), :],
                                   core.banks[b + 4][:].rearrange("p (t c) -> p t c", t=T)).then_inc(bias_copied, 1)
                with act.Fori(0, B) as b:
                    for g in range(GROUPS):
                        act.wait_ge(h_ready, GROUPS * b + (g + 1))
                        if g >= 2:
                            act.wait_ge(hidden_ready, GROUPS * b + (g - 1))
                        nc.scalar.activation(relued[:, g % 2, :], h_banks[g % 2][:], ACT.Relu, bias=b1[:, g:g + 1]
                                             ).then_inc(relu_ready, 1)
                    act.wait_ge(summed_ready, CREDIT + b + 1)
                    nc.scalar.activation(core.branch[:, bass.ts(b, T), :], summed[:].rearrange("p (t c) -> p t c", t=T),
                                         ACT.Relu).then_inc(finished, 1)

            @block.vector
            def _(dve):
                dve.wait_ge(loaded, 16 * len(names))
                dve.wait_ge(logits_ready, 1)
                nc.vector.tensor_tensor(logits[:], y_bank[:].rearrange("p (t e) -> p t e", e=X),
                                        router_b[:].unsqueeze(1).broadcast_to([P, TILES, X]), ALU.add).then_inc(step, 1)
                dve.wait_ge(step, 1)
                for t in range(TILES):
                    nc.vector.max(top[:, t, :], logits[:, t, :]).then_inc(top_ready, 1)
                for t in range(TILES):
                    dve.wait_ge(top_ready, t + 1)
                    tick = nc.vector.max_index(places[:, t, :], top[:, t, :], logits[:, t, :])
                tick.then_inc(step, 1)
                dve.wait_ge(step, 2)
                nc.vector.tensor_copy(places_f[:], places[:, :, 0]).then_inc(step, 1)
                dve.wait_ge(step, 3)
                nc.vector.tensor_tensor(onehot[:], numbers[:].unsqueeze(1).broadcast_to([P, TILES, X]),
                                        places_f[:].unsqueeze(2).broadcast_to([P, TILES, X]),
                                        ALU.is_equal).then_inc(onehot_ready, 1)
                for b in range(B):
                    dve.wait_ge(t_ready, b + 1)
                    nc.vector.tensor_copy(onehot_t[:, bass.ts(b, N)], core.banks[b][0:X, :]).then_inc(t_copied, 1)
                dve.wait_ge(t_copied, B)
                nc.vector.tensor_copy(onehot_bf[:], onehot_t[:]).then_inc(t_copied, 1)
                dve.wait_ge(bias_copied, B)
                give_credit(dve, summed_ready)
                with dve.Fori(0, B) as b:
                    for g in range(GROUPS):
                        dve.wait_ge(relu_ready, GROUPS * b + (g + 1))
                        dve.wait_ge(mask_ready, GROUPS * b + (g + 1))
                        nc.vector.tensor_tensor(hidden[:, g, :], relued[:, g % 2, :], mask_banks[g % 2][:],
                                                ALU.mult).then_inc(hidden_ready, 1)
                    dve.wait_ge(y_ready, b + 1)
                    nc.vector.tensor_tensor(summed[:].rearrange("p (t c) -> p t c", t=T),
                                            y_bank[:].rearrange("p (t c) -> p t c", t=T),
                                            core.branch[:, bass.ts(b, T), :], ALU.add).then_inc(summed_ready, 1)


def linear_attention(core, name):
    nc, dram = core.nc, core.dram
    PAIRS = D // 2
    EPS_RMS, EPS_DEN = 1.1920929e-07, 1e-06
    with ExitStack() as st:
        def buf(n, shape, dtype=F32):
            return core.sbuf(st, f"{name}_{n}", shape, dtype)

        def sem(n):
            return core.sem(f"{name}_{n}")

        w_qkv, b_qkv = buf("w_qkv", [P, 3 * D]), buf("b_qkv", [P, 3 * D])
        w_out, b_out, g_out = buf("w_out", [P, D]), buf("b_out", [P, D]), buf("g_out", [P, D])
        g_qk = buf("g_qk", [P, 2, D])
        cos, sin, same_head = buf("cos", [P, T, PAIRS]), buf("sin", [P, T, PAIRS]), buf("same_head", [P, D])
        power = buf("power", [P, 2 * T])
        x_now = buf("x_now", [P, N])
        qk, v = buf("qk", [P, T, 2, D]), buf("v", [P, T, D + 1])
        squares, qk_rms, out_rms = buf("squares", [P, D]), buf("qk_rms", [P, 2 * T]), buf("out_rms", [P, T])
        turned = buf("turned", [P, T, 2, D])
        product = [buf(f"product{i}", [P, T, 2, PAIRS]) for i in range(4)]
        feature, feature_t = buf("feature", [P, T, 2, D]), buf("feature_t", [P, T, P])
        vk = buf("vk", [P, 2, D])
        inverse, attn, attn_t = buf("inverse", [P, T, D]), buf("attn", [P, T, D]), buf("attn_t", [P, T, P])
        projected = buf("projected", [P, T, D])
        qkv_banks, t_bank, vk_bank, res_banks, out_bank = (
            core.banks[0:4], core.banks[4], core.banks[5], core.banks[6:8], core.banks[5])

        loads = [(w_qkv[:], "w_qkv2", False), (b_qkv[:], "b_qkv2", True), (w_out[:], "w_out2", False),
                 (b_out[:], "b_out2", True), (g_out[:], "g_out2", True), (g_qk[:, 0, :], "g_q2", True), (g_qk[:, 1, :], "g_k2", True),
                 (cos[:], "cos2", False), (sin[:], "sin2", False), (same_head[:], "same_head", False)]
        loaded, constants_ready, x_ready = sem("loaded"), sem("constants_ready"), sem("x_ready")
        qkv_ready, qk_ready, v_ready, squares_ready = sem("qkv_ready"), sem("qk_ready"), sem("v_ready"), sem("squares_ready")
        mean_ready, rms_ready, scaled = sem("mean_ready"), sem("rms_ready"), sem("scaled")
        products_ready, turned_ready, feature_ready = sem("products_ready"), sem("turned_ready"), sem("feature_ready")
        vk_ready, vk_masked, ft_ready, ft_copied = sem("vk_ready"), sem("vk_masked"), sem("ft_ready"), sem("ft_copied")
        res_ready, inverse_step, attn_ready = sem("res_ready"), sem("inverse_step"), sem("attn_ready")
        at_ready, at_copied, out_ready, projected_ready = (
            sem("at_ready"), sem("at_copied"), sem("out_ready"), sem("projected_ready"))
        out_squares, out_mean, out_rms_ready, branch_ready = (
            sem("out_squares"), sem("out_mean"), sem("out_rms_ready"), sem("branch_ready"))

        with core.stage() as block:
            @block.sync
            def _(sp):
                core.clear_spent(sp)
                for place, source, every_partition in loads:
                    src = dram[source].partition_broadcast(P) if every_partition else dram[source]
                    sp.dma_start(place, src).then_inc(loaded, 16)

            @block.gpsimd
            def _(pool):
                nc.gpsimd.memset(power[:], -0.5).then_inc(constants_ready, 1)
                nc.gpsimd.memset(v[:, :, D:D + 1], 1.0).then_inc(constants_ready, 1)
                pool.wait_ge(constants_ready, 2)
                with pool.Fori(0, B) as b:
                    pool.wait_ge(mean_ready, b + 1)
                    nc.gpsimd.tensor_tensor(qk_rms[:], qk_rms[:], power[:], ALU.pow).then_inc(rms_ready, 1)
                    pool.wait_ge(out_mean, b + 1)
                    nc.gpsimd.tensor_tensor(out_rms[:], out_rms[:], power[:, 0:T], ALU.pow).then_inc(out_rms_ready, 1)

            @block.tensor
            def _(pe):
                pe.wait_ge(loaded, 16 * len(loads))
                pe.wait_ge(constants_ready, 2)
                with pe.Fori(0, B) as b:
                    pe.wait_ge(x_ready, b + 1)
                    for t in range(T):
                        nc.tensor.matmul(qkv_banks[t][:, 0:3 * D], x_now[:, bass.ts(t, P)], w_qkv[:]
                                         ).then_inc(qkv_ready, 1)
                    pe.wait_ge(v_ready, T * b + T)
                    pe.wait_ge(feature_ready, b + 1)
                    for t in range(T):
                        tick = nc.tensor.matmul(vk_bank[:, 0:D + 1], feature[:, t, 1, :], v[:, t, :],
                                                start=(t == 0), stop=(t == T - 1))
                    tick.then_inc(vk_ready, 1)
                    for t in range(T):
                        tick = nc.tensor.transpose(t_bank[:, bass.ts(t, P)], feature[:, t, 0, :], core.identity[:])
                    tick.then_inc(ft_ready, 1)
                    pe.wait_ge(ft_copied, b + 1)
                    pe.wait_ge(vk_masked, 3 * b + 3)
                    for t in range(T):
                        tick = nc.tensor.matmul(res_banks[t // 2][:, bass.ts(t % 2, 2 * D)], feature_t[:, t, :],
                                                vk[:].rearrange("p a d -> p (a d)"))
                    tick.then_inc(res_ready, 1)
                    pe.wait_ge(attn_ready, 2 * b + 2)
                    for t in range(T):
                        tick = nc.tensor.transpose(t_bank[:, bass.ts(t, P)], attn[:, t, :], core.identity[:])
                    tick.then_inc(at_ready, 1)
                    pe.wait_ge(at_copied, b + 1)
                    for t in range(T):
                        tick = nc.tensor.matmul(out_bank[:, bass.ts(t, P)], attn_t[:, t, :], w_out[:])
                    tick.then_inc(out_ready, 1)

            @block.scalar
            def _(act):
                with act.Fori(0, B) as b:
                    nc.scalar.copy(x_now[:], core.xn_chan[:, bass.ts(b, N)]).then_inc(x_ready, 1)
                    for t in range(T):
                        act.wait_ge(qk_ready, T * b + (t + 1))
                        for which in range(2):
                            if t or which:
                                act.wait_ge(squares_ready, 2 * T * b + (2 * t + which))
                            nc.scalar.activation(squares[:], qk[:, t, which, :], ACT.Square,
                                                 accum_out=qk_rms[:, 2 * t + which:2 * t + which + 1]
                                                 ).then_inc(squares_ready, 1)
                    act.wait_ge(turned_ready, 2 * b + 2)
                    nc.scalar.activation(feature[:], turned[:], ACT.Relu).then_inc(feature_ready, 1)
                    act.wait_ge(ft_ready, b + 1)
                    nc.scalar.copy(feature_t[:], t_bank[:].rearrange("p (t c) -> p t c", t=T)).then_inc(ft_copied, 1)
                    act.wait_ge(at_ready, b + 1)
                    nc.scalar.copy(attn_t[:], t_bank[:].rearrange("p (t c) -> p t c", t=T)).then_inc(at_copied, 1)
                    act.wait_ge(projected_ready, b + 1)
                    for t in range(T):
                        if t:
                            act.wait_ge(out_squares, T * b + t)
                        nc.scalar.activation(squares[:], projected[:, t, :], ACT.Square,
                                             accum_out=out_rms[:, t:t + 1]).then_inc(out_squares, 1)

            @block.vector
            def _(dve):
                dve.wait_ge(loaded, 16 * len(loads))
                dve.wait_ge(constants_ready, 2)
                with dve.Fori(0, B) as b:
                    for t in range(T):
                        dve.wait_ge(qkv_ready, T * b + (t + 1))
                        nc.vector.tensor_tensor(qk[:, t, :, :].rearrange("p a d -> p (a d)"), qkv_banks[t][:, 0:2 * D],
                                                b_qkv[:, 0:2 * D], ALU.add).then_inc(qk_ready, 1)
                        nc.vector.tensor_tensor(v[:, t, 0:D], qkv_banks[t][:, 2 * D:3 * D], b_qkv[:, 2 * D:3 * D],
                                                ALU.add).then_inc(v_ready, 1)
                    dve.wait_ge(squares_ready, 2 * T * b + 2 * T)
                    nc.vector.tensor_scalar(qk_rms[:], qk_rms[:], 1.0 / D, EPS_RMS, ALU.mult, ALU.add
                                            ).then_inc(mean_ready, 1)
                    dve.wait_ge(rms_ready, b + 1)
                    for t in range(T):
                        for which in range(2):
                            i = 2 * t + which
                            tick = nc.vector.scalar_tensor_tensor(qk[:, t, which, :], qk[:, t, which, :],
                                                                  qk_rms[:, i:i + 1], g_qk[:, which, :],
                                                                  ALU.mult, ALU.mult)
                    tick.then_inc(scaled, 1)
                    dve.wait_ge(scaled, b + 1)
                    pairs = qk[:].rearrange("p t a (m two) -> p t a m two", two=2)
                    table = [x[:].unsqueeze(2).broadcast_to([P, T, 2, PAIRS]) for x in (cos, sin)]
                    for i, (which, tab) in enumerate(((0, 0), (1, 1), (0, 1), (1, 0))):
                        nc.vector.tensor_tensor(product[i][:], pairs[:, :, :, :, which], table[tab], ALU.mult
                                                ).then_inc(products_ready, 1)
                    out = turned[:].rearrange("p t a (m two) -> p t a m two", two=2)
                    dve.wait_ge(products_ready, 4 * b + 2)
                    nc.vector.tensor_tensor(out[:, :, :, :, 0], product[0][:], product[1][:], ALU.subtract
                                            ).then_inc(turned_ready, 1)
                    dve.wait_ge(products_ready, 4 * b + 4)
                    nc.vector.tensor_tensor(out[:, :, :, :, 1], product[2][:], product[3][:], ALU.add
                                            ).then_inc(turned_ready, 1)
                    dve.wait_ge(vk_ready, b + 1)
                    nc.vector.tensor_tensor(vk[:, 0, :], vk_bank[:, 0:D], same_head[:], ALU.mult).then_inc(vk_masked, 1)
                    nc.vector.tensor_copy(inverse[:, 0, 0:1], vk_bank[:, D:D + 1]).then_inc(vk_masked, 1)
                    dve.wait_ge(vk_masked, 3 * b + 2)
                    nc.vector.tensor_scalar(vk[:, 1, :], same_head[:], inverse[:, 0, 0:1], None, ALU.mult
                                            ).then_inc(vk_masked, 1)
                    dve.wait_ge(vk_masked, 3 * b + 3)
                    dve.wait_ge(res_ready, b + 1)
                    for half in range(2):
                        res = res_banks[half][:].rearrange("p (t a d) -> p t a d", t=2, a=2)
                        inv = inverse[:, 2 * half:2 * half + 2, :]
                        nc.vector.tensor_scalar(inv, res[:, :, 1, :], EPS_DEN, None, ALU.add).then_inc(inverse_step, 1)
                        dve.wait_ge(inverse_step, 4 * b + (2 * half + 1))
                        nc.vector.reciprocal(inv, inv).then_inc(inverse_step, 1)
                        dve.wait_ge(inverse_step, 4 * b + (2 * half + 2))
                        nc.vector.tensor_tensor(attn[:, 2 * half:2 * half + 2, :], res[:, :, 0, :], inv, ALU.mult
                                                ).then_inc(attn_ready, 1)
                    dve.wait_ge(out_ready, b + 1)
                    nc.vector.tensor_tensor(projected[:], out_bank[:].rearrange("p (t c) -> p t c", t=T),
                                            b_out[:].unsqueeze(1).broadcast_to([P, T, D]), ALU.add
                                            ).then_inc(projected_ready, 1)
                    dve.wait_ge(out_squares, T * b + T)
                    nc.vector.tensor_scalar(out_rms[:], out_rms[:], 1.0 / D, EPS_RMS, ALU.mult, ALU.add
                                            ).then_inc(out_mean, 1)
                    dve.wait_ge(out_rms_ready, b + 1)
                    for t in range(T):
                        tick = nc.vector.scalar_tensor_tensor(core.branch[:, bass.ds(b * T + t, 1), :].rearrange(
                            "p o d -> p (o d)"), projected[:, t, :], out_rms[:, t:t + 1], g_out[:], ALU.mult, ALU.mult)
                    tick.then_inc(branch_ready, 1)


def token_mix(core, name):
    nc, dram = core.nc, core.dram
    with ExitStack() as st:
        def buf(n, shape, dtype=F32):
            return core.sbuf(st, f"{name}_{n}", shape, dtype)

        def sem(n):
            return core.sem(f"{name}_{n}")

        w_r, w_k, w_v, mu = buf("w_r", [P, D]), buf("w_k", [P, D]), buf("w_v", [P, D]), buf("mu", [P, 2])
        x_now = buf("x_now", [P, 1 + N])
        change, x_r, x_k = buf("change", [P, N]), buf("x_r", [P, N]), buf("x_k", [P, N])
        relued, squared, receptance = buf("relued", [P, N]), buf("squared", [P, N]), buf("receptance", [P, N])
        loads = [(w_r, "w_r"), (w_k, "w_k"), (w_v, "w_v"), (mu, "mu")]
        loaded, zeroed, x_ready, change_ready = sem("loaded"), sem("zeroed"), sem("x_ready"), sem("change_ready")
        mixed, k_ready, r_ready, relu_ready = sem("mixed"), sem("k_ready"), sem("r_ready"), sem("relu_ready")
        squared_ready, sigmoid_ready, v_ready, done = (
            sem("squared_ready"), sem("sigmoid_ready"), sem("v_ready"), sem("done"))
        k_bank, r_bank, v_bank = core.banks[0:3]

        with core.stage() as block:
            @block.sync
            def _(sp):
                core.clear_spent(sp)
                for place, source in loads:
                    sp.dma_start(place[:], dram[source]).then_inc(loaded, 16)

            @block.tensor
            def _(pe):
                pe.wait_ge(loaded, 16 * len(loads))
                with pe.Fori(0, B) as b:
                    pe.wait_ge(mixed, 2 * b + 1)
                    pe.wait_ge(squared_ready, CREDIT + b)
                    nc.tensor.matmul(k_bank[:], w_k[:], x_k[:]).then_inc(k_ready, 1)
                    pe.wait_ge(mixed, 2 * b + 2)
                    for t in range(T):
                        tick = nc.tensor.matmul(r_bank[:, bass.ts(t, P)], x_r[:, bass.ts(t, P)], w_r[:])
                    tick.then_inc(r_ready, 1)
                    pe.wait_ge(squared_ready, CREDIT + b + 1)
                    pe.wait_ge(done, CREDIT + b)
                    for t in range(T):
                        tick = nc.tensor.matmul(v_bank[:, bass.ts(t, P)], squared[:, bass.ts(t, P)], w_v[:])
                    tick.then_inc(v_ready, 1)

            @block.scalar
            def _(act):
                act.wait_ge(zeroed, 1)
                give_credit(act, sigmoid_ready)
                with act.Fori(0, B) as b:
                    nc.scalar.copy(x_now[:, 1:1 + N], core.xn_chan[:, bass.ts(b, N)]).then_inc(x_ready, 1)
                    act.wait_ge(k_ready, b + 1)
                    nc.scalar.activation(relued[:], k_bank[:], ACT.Relu).then_inc(relu_ready, 1)
                    act.wait_ge(r_ready, b + 1)
                    nc.scalar.activation(receptance[:], r_bank[:], ACT.Sigmoid).then_inc(sigmoid_ready, 1)

            @block.vector
            def _(dve):
                nc.vector.memset(x_now[:, 0:1], 0.0).then_inc(zeroed, 1)
                dve.wait_ge(loaded, 16 * len(loads))
                give_credit(dve, squared_ready, done)
                with dve.Fori(0, B) as b:
                    dve.wait_ge(x_ready, b + 1)
                    nc.vector.tensor_tensor(change[:], x_now[:, 1:1 + N], x_now[:, 0:N], ALU.subtract
                                            ).then_inc(change_ready, 1)
                    dve.wait_ge(change_ready, b + 1)
                    for i, place in ((1, x_k), (0, x_r)):
                        nc.vector.scalar_tensor_tensor(place[:], change[:], mu[:, i:i + 1], x_now[:, 0:N],
                                                       ALU.mult, ALU.add).then_inc(mixed, 1)
                    dve.wait_ge(relu_ready, b + 1)
                    nc.vector.tensor_tensor(squared[:], relued[:], k_bank[:], ALU.mult).then_inc(squared_ready, 1)
                    dve.wait_ge(v_ready, b + 1)
                    dve.wait_ge(sigmoid_ready, CREDIT + b + 1)
                    nc.vector.tensor_tensor(core.branch[:, bass.ts(b, T), :],
                                            receptance[:].rearrange("p (t c) -> p t c", t=T),
                                            v_bank[:].rearrange("p (t c) -> p t c", t=T), ALU.mult).then_inc(done, 1)


def local_attention(core, name, layer):
    nc, dram = core.nc, core.dram
    H, E, W = 8, 64, 64
    HALF = E // 2
    INNER = H * E
    PAIRS = H // 2
    KEYS = W + P
    STEPS = T * PAIRS
    LAG_T, LAG_PV = 2, 3
    OT_AT, OUT_AT = 8, 9
    POSITIONS = PAIRS * (T - 1) + OUT_AT + 2
    S_RING, PT_RING, P_RING = 3, 2, 3
    with ExitStack() as st:
        def buf(n, shape, dtype=F32):
            return core.sbuf(st, f"{name}_{n}", shape, dtype)

        def sem(n):
            return core.sem(f"{name}_{n}")

        w_qkv, w_out = buf("w_qkv", [P, 3, INNER]), buf("w_out", [P, PAIRS, D])
        table = [buf(f"table{i}", [P, T, E]) for i in range(4)]
        head_scale = buf("head_scale", [P, 4, E])
        mask_f, mask = buf("mask_f", [P, KEYS]), buf("mask", [P, 2, KEYS], BF16)
        power = buf("power", [P, H])
        x_now = buf("x_now", [P, N])
        k_raw, squares = buf("k_raw", [P, 2, INNER]), buf("squares", [P, 2, INNER])
        norm = buf("norm", [P, 2, 2, H])
        part = [buf(f"part{i}", [P, INNER]) for i in range(4)]
        rotated = [buf("q_rotated", [P, 2, INNER]), buf("k_rotated", [P, 2, INNER])]
        chan = [buf("q_chan", [P, PAIRS, N]), buf("k_chan", [P, PAIRS, N])]
        v_tok = buf("v_tok", [P, T, INNER])
        neg_max, row_sum, inverse = buf("neg_max", [P, T, H]), buf("row_sum", [P, T, H]), buf("inverse", [P, T, H])
        probs = buf("probs", [P, P_RING, 2, 2 * P])
        probs_t = buf("probs_t", [P, PT_RING, 4, P])
        heads_out, heads_out_t = buf("heads_out", [P, INNER]), buf("heads_out_t", [P, PAIRS, P])
        score_banks, pt_banks, pv_banks, out_bank = core.banks[0:3], core.banks[3:5], core.banks[5:7], core.banks[7]

        loads = [(w_qkv[:], dram["w_qkv_local"][layer]), (w_out[:], dram["w_out_local"][layer]),
                 (mask_f[:], dram["local_mask"]), (head_scale[:], dram["head_scale"][layer].partition_broadcast(P))]
        loads += [(table[i][:], dram["rotary"][i]) for i in range(4)]
        loaded, table_ready, mask_ready, zeroed, power_ready = (
            sem("loaded"), sem("table_ready"), sem("mask_ready"), sem("zeroed"), sem("power_ready"))
        x_ready, q_ready, k_ready, v_ready = sem("x_ready"), sem("q_ready"), sem("k_ready"), sem("v_ready")
        v_copied, k_copied, squared = sem("v_copied"), sem("k_copied"), sem("squared")
        sum_ready, floored, norm_ready = sem("sum_ready"), sem("floored"), sem("norm_ready")
        part_ready = [sem("q_part_ready"), sem("k_part_ready")]
        whole_ready = [sem("q_whole_ready"), sem("k_whole_ready")]
        rotated_ready = [sem("q_rotated_ready"), sem("k_rotated_ready")]
        t_ready, chan_ready = sem("t_ready"), sem("chan_ready")
        scores_ready, max_ready, probs_ready = sem("scores_ready"), sem("max_ready"), sem("probs_ready")
        pt_ready, pt_copied, pv_ready = sem("pt_ready"), sem("pt_copied"), sem("pv_ready")
        inverse_ready, normed = sem("inverse_ready"), sem("normed")
        ot_ready, ot_copied, out_ready, out_copied = (
            sem("ot_ready"), sem("ot_copied"), sem("out_ready"), sem("out_copied"))

        def heads_of(step):
            first = 4 * (step % PAIRS // 2) + step % 2
            return first, first + 2

        def halves(x):
            return x.rearrange("p (h two c) -> p h two c", h=H, two=2)

        def by_head(x):
            return x.rearrange("p (h c) -> p h c", h=H)

        with core.stage() as block:
            @block.sync
            def _(sp):
                core.clear_spent(sp)
                for place, source in loads:
                    sp.dma_start(place, source).then_inc(loaded, 16)

            def rotate(engine, api, source, b, t, which):
                cos_part, sin_part = part[2 * which][:], part[2 * which + 1][:]
                engine.wait_ge(rotated_ready[which], CREDIT + T * b + t)
                cos = table[2 * which][:, t, :].unsqueeze(1).broadcast_to([P, H, E])
                api.tensor_tensor(by_head(cos_part), by_head(source), cos, ALU.mult).then_inc(part_ready[which], 1)
                for half in range(2):
                    sin = table[2 * which + 1][:, t, half * HALF:(half + 1) * HALF].unsqueeze(1).broadcast_to([P, H, HALF])
                    api.tensor_tensor(halves(sin_part)[:, :, half, :], halves(source)[:, :, 1 - half, :], sin,
                                      ALU.mult).then_inc(part_ready[which], 1)
                engine.wait_ge(part_ready[which], CREDIT + 3 * T * b + (3 * t + 3))
                api.tensor_tensor(cos_part, cos_part, sin_part, ALU.add).then_inc(whole_ready[which], 1)
                engine.wait_ge(whole_ready[which], CREDIT + T * b + (t + 1))

            def scale(engine, api, b, t, which):
                engine.wait_ge(norm_ready, T * b + (t + 1))
                if t >= 2:
                    engine.wait_ge(t_ready, 2 * T * b + (2 * (t - 2) + which + 1))
                api.tensor_tensor(by_head(rotated[which][:, t % 2, :]), by_head(part[2 * which][:]),
                                  norm[:, t % 2, which, :].unsqueeze(2).broadcast_to([P, H, E]),
                                  ALU.mult).then_inc(rotated_ready[which], 1)

            @block.gpsimd
            def _(pool):
                nc.gpsimd.memset(power[:], -0.5).then_inc(power_ready, 1)
                nc.gpsimd.memset(probs[:], 0.0).then_inc(zeroed, 1)
                pool.wait_ge(power_ready, 1)
                pool.wait_ge(table_ready, 4)
                give_credit(pool, part_ready[1], whole_ready[1], rotated_ready[1])
                with pool.Fori(0, B) as b:
                    for t in range(T):
                        pool.wait_ge(floored, T * b + (t + 1))
                        nc.gpsimd.tensor_tensor(norm[:, t % 2, :, :], norm[:, t % 2, :, :],
                                                power[:].unsqueeze(1).broadcast_to([P, 2, H]), ALU.pow
                                                ).then_inc(norm_ready, 1)
                        pool.wait_ge(k_copied, T * b + (t + 1))
                        rotate(pool, nc.gpsimd, k_raw[:, t % 2, :], b, t, 1)
                        scale(pool, nc.gpsimd, b, t, 1)

            @block.tensor
            def _(pe):
                def project(b, t):
                    banks = core.banks[0:3] if t % 2 == 0 else core.banks[3:6]
                    if t >= 2:
                        pe.wait_ge(v_copied, T * b + (t - 1))
                        pe.wait_ge(whole_ready[0], CREDIT + T * b + (t - 1))
                        pe.wait_ge(squared, 2 * T * b + (2 * (t - 2) + 2))
                        pe.wait_ge(k_copied, T * b + (t - 1))
                    x = x_now[:, bass.ts(t, P)]
                    for which, done in enumerate((q_ready, k_ready, v_ready)):
                        nc.tensor.matmul(banks[which][:], x, w_qkv[:, which, :]).then_inc(done, 1)

                def to_chan(b, t, which):
                    pe.wait_ge(rotated_ready[which], CREDIT + T * b + (t + 1))
                    if t:
                        pe.wait_ge(chan_ready, 2 * T * b + (2 * (t - 1) + which + 1))
                    for pair in range(PAIRS):
                        tick = nc.tensor.transpose(core.banks[6 + which][:, bass.ts(pair, P)],
                                                   rotated[which][:, t % 2, bass.ts(pair, P)], core.identity[:])
                    tick.then_inc(t_ready, 1)

                def scores(b, s):
                    t = s // PAIRS
                    if s >= S_RING:
                        pe.wait_ge(probs_ready, STEPS * b + (s - S_RING + 1))
                    bank = score_banks[s % S_RING]
                    skip = 0 if t else W
                    both = bank[:, 0:2 * KEYS].rearrange("p (h k) -> p h k", h=2)
                    nc.tensor.matmul(both[:, :, skip:KEYS], core.identity_bf[:], mask[:, :, skip:KEYS],
                                     start=True, stop=False)
                    for h, head in enumerate(heads_of(s)):
                        rows, pair = slice(head % 2 * E, (head % 2 + 1) * E), head // 2
                        tick = nc.tensor.matmul(both[:, h, skip:KEYS], chan[0][rows, pair, bass.ts(t, P)],
                                                chan[1][rows, pair, t * P - W + skip:(t + 1) * P],
                                                start=False, stop=(h == 1))
                    tick.then_inc(scores_ready, 1)

                def transpose(b, s):
                    pe.wait_ge(probs_ready, STEPS * b + (s + 1))
                    if s >= PT_RING:
                        pe.wait_ge(pt_copied, STEPS * b + (s - PT_RING + 1))
                    for h in range(2):
                        for keys in range(2 if s >= PAIRS else 1):
                            part_of = probs[:, s % P_RING, h, bass.ts(keys if s >= PAIRS else 1, P)]
                            tick = nc.tensor.transpose(pt_banks[s % PT_RING][:, bass.ts(2 * h + keys, P)], part_of,
                                                       core.identity[:])
                    tick.then_inc(pt_ready, 1)

                def product(b, s):
                    t = s // PAIRS
                    pe.wait_ge(pt_copied, STEPS * b + (s + 1))
                    if s % PAIRS == 0 and t >= 2:
                        pe.wait_ge(normed, T * b + (t - 1))
                    for h, head in enumerate(heads_of(s)):
                        key_tiles = [t - 1, t] if t else [t]
                        for n, k in enumerate(key_tiles):
                            tick = nc.tensor.matmul(pv_banks[t % 2][:, bass.ts(head, E)],
                                                    probs_t[:, s % PT_RING, 2 * h + n, :], v_tok[:, k, bass.ts(head, E)],
                                                    start=(n == 0), stop=(n == len(key_tiles) - 1))
                    tick.then_inc(pv_ready, 1)

                pe.wait_ge(loaded, 16 * len(loads))
                pe.wait_ge(mask_ready, 2)
                give_credit(pe, ot_ready)
                with pe.Fori(0, B) as b:
                    pe.wait_ge(x_ready, b + 1)
                    project(b, 0)
                    project(b, 1)
                    pe.wait_ge(out_copied, CREDIT + T * b)
                    for t in range(T):
                        to_chan(b, t, 0)
                        to_chan(b, t, 1)
                        if t + 2 < T:
                            project(b, t + 2)
                    pe.wait_ge(chan_ready, 2 * T * b + 2 * T)
                    pe.wait_ge(v_copied, T * b + T)
                    for at in range(POSITIONS):
                        if at < STEPS:
                            scores(b, at)
                        if 0 <= at - LAG_T < STEPS:
                            transpose(b, at - LAG_T)
                        if 0 <= at - LAG_PV < STEPS:
                            product(b, at - LAG_PV)
                        if at >= OT_AT and (at - OT_AT) % PAIRS == 0 and (at - OT_AT) // PAIRS < T:
                            t = (at - OT_AT) // PAIRS
                            pe.wait_ge(normed, T * b + (t + 1))
                            pe.wait_ge(out_copied, CREDIT + T * b + t)
                            for pair in range(PAIRS):
                                tick = nc.tensor.transpose(out_bank[:, bass.ts(pair, P)], heads_out[:, bass.ts(pair, P)],
                                                           core.identity[:])
                            tick.then_inc(ot_ready, 1)
                        if at >= OUT_AT and (at - OUT_AT) % PAIRS == 0 and (at - OUT_AT) // PAIRS < T:
                            t = (at - OUT_AT) // PAIRS
                            pe.wait_ge(ot_copied, T * b + (t + 1))
                            for pair in range(PAIRS):
                                tick = nc.tensor.matmul(out_bank[:, 0:D], heads_out_t[:, pair, :], w_out[:, pair, :],
                                                        start=(pair == 0), stop=(pair == PAIRS - 1))
                            tick.then_inc(out_ready, 1)

            @block.scalar
            def _(act):
                give_credit(act, out_copied)
                act.wait_ge(zeroed, 1)
                with act.Fori(0, B) as b:
                    nc.scalar.copy(x_now[:], core.xn_chan[:, bass.ts(b, N)]).then_inc(x_ready, 1)

                    def gather(t):
                        banks = core.banks[0:3] if t % 2 == 0 else core.banks[3:6]
                        act.wait_ge(q_ready, T * b + (t + 1))
                        if t:
                            act.wait_ge(sum_ready, T * b + t)
                        nc.scalar.activation(squares[:, 0, :], banks[0][:], ACT.Square).then_inc(squared, 1)
                        act.wait_ge(k_ready, T * b + (t + 1))
                        nc.scalar.activation(squares[:, 1, :], banks[1][:], ACT.Square).then_inc(squared, 1)
                        if t >= 2:
                            act.wait_ge(whole_ready[1], CREDIT + T * b + (t - 1))
                        nc.scalar.copy(k_raw[:, t % 2, :], banks[1][:]).then_inc(k_copied, 1)
                        act.wait_ge(v_ready, T * b + (t + 1))
                        nc.scalar.copy(v_tok[:, t, :], banks[2][:]).then_inc(v_copied, 1)

                    def copy_chan(t):
                        for which in range(2):
                            act.wait_ge(t_ready, 2 * T * b + (2 * t + which + 1))
                            nc.scalar.copy(chan[which][:, :, bass.ts(t, P)],
                                           core.banks[6 + which][:].rearrange("p (q c) -> p q c", q=PAIRS)
                                           ).then_inc(chan_ready, 1)

                    gather(0)
                    gather(1)
                    for t in range(T):
                        copy_chan(t)
                        if t + 2 < T:
                            gather(t + 2)
                    for at in range(POSITIONS):
                        if at < STEPS:
                            t = at // PAIRS
                            act.wait_ge(max_ready, STEPS * b + (at + 1))
                            if at >= P_RING:
                                act.wait_ge(pt_ready, STEPS * b + (at - P_RING + 1))
                            skip = 0 if t else W
                            both = score_banks[at % S_RING][:, 0:2 * KEYS].rearrange("p (h k) -> p h k", h=2)
                            for h, head in enumerate(heads_of(at)):
                                tick = nc.scalar.activation(probs[:, at % P_RING, h, W + skip:2 * P],
                                                            both[:, h, skip:KEYS], ACT.Exp,
                                                            bias=neg_max[:, t, head:head + 1],
                                                            accum_out=row_sum[:, t, head:head + 1])
                            tick.then_inc(probs_ready, 1)
                        if at >= OT_AT and (at - OT_AT) % PAIRS == 0 and (at - OT_AT) // PAIRS < T:
                            t = (at - OT_AT) // PAIRS
                            act.wait_ge(ot_ready, CREDIT + T * b + (t + 1))
                            nc.scalar.copy(heads_out_t[:], out_bank[:].rearrange("p (q c) -> p q c", q=PAIRS)
                                           ).then_inc(ot_copied, 1)
                        if at > OUT_AT and (at - OUT_AT - 1) % PAIRS == 0 and (at - OUT_AT - 1) // PAIRS < T:
                            t = (at - OUT_AT - 1) // PAIRS
                            act.wait_ge(out_ready, T * b + (t + 1))
                            nc.scalar.copy(core.branch[:, bass.ds(b * T + t, 1), :].rearrange("p o d -> p (o d)"),
                                           out_bank[:, 0:D]).then_inc(out_copied, 1)

            @block.vector
            def _(dve):
                dve.wait_ge(loaded, 16 * len(loads))
                for h in range(2):
                    nc.vector.tensor_copy(mask[:, h, :], mask_f[:]).then_inc(mask_ready, 1)
                for i in range(4):
                    nc.vector.tensor_tensor(table[i][:], table[i][:], head_scale[:, i, :].unsqueeze(1).broadcast_to(
                        [P, T, E]), ALU.mult).then_inc(table_ready, 1)
                dve.wait_ge(table_ready, 4)
                give_credit(dve, part_ready[0], whole_ready[0], rotated_ready[0])
                with dve.Fori(0, B) as b:
                    for t in range(T):
                        banks = core.banks[0:3] if t % 2 == 0 else core.banks[3:6]
                        dve.wait_ge(squared, 2 * T * b + (2 * t + 2))
                        if t >= 2:
                            for which in range(2):
                                dve.wait_ge(rotated_ready[which], CREDIT + T * b + (t - 1))
                        nc.vector.tensor_reduce(norm[:, t % 2, :, :], squares[:].rearrange(
                            "p a (h c) -> p a h c", h=H), AX_X, ALU.add).then_inc(sum_ready, 1)
                        dve.wait_ge(sum_ready, T * b + (t + 1))
                        nc.vector.tensor_scalar(norm[:, t % 2, :, :], norm[:, t % 2, :, :], 1e-24, None, ALU.max
                                                ).then_inc(floored, 1)
                        rotate(dve, nc.vector, banks[0][:], b, t, 0)
                        scale(dve, nc.vector, b, t, 0)
                    for at in range(POSITIONS):
                        if at < STEPS:
                            t, first = at // PAIRS, heads_of(at)[0]
                            skip = 0 if t else W
                            dve.wait_ge(scores_ready, STEPS * b + (at + 1))
                            nc.vector.tensor_reduce(
                                neg_max[:, t, first:first + 3:2],
                                score_banks[at % S_RING][:, 0:2 * KEYS].rearrange("p (h k) -> p h k", h=2)[:, :, skip:KEYS],
                                AX_X, ALU.max, negate=True).then_inc(max_ready, 1)
                        s = at - LAG_T
                        if 0 <= s < STEPS:
                            dve.wait_ge(pt_ready, STEPS * b + (s + 1))
                            if s >= PT_RING:
                                dve.wait_ge(pv_ready, STEPS * b + (s - PT_RING + 1))
                            blocks = probs_t[:, s % PT_RING, :, :].rearrange("p (h k) c -> p h k c", h=2)
                            source = pt_banks[s % PT_RING][:].rearrange("p (h k c) -> p h k c", h=2, k=2)
                            if s < PAIRS:
                                blocks, source = blocks[:, :, 0, :], source[:, :, 0, :]
                            nc.vector.tensor_copy(blocks, source).then_inc(pt_copied, 1)
                        if at > LAG_PV + PAIRS - 1 and (at - LAG_PV - PAIRS) % PAIRS == 0 and (at - LAG_PV) // PAIRS <= T:
                            t = (at - LAG_PV) // PAIRS - 1
                            dve.wait_ge(probs_ready, STEPS * b + PAIRS * (t + 1))
                            nc.vector.reciprocal(inverse[:, t, :], row_sum[:, t, :]).then_inc(inverse_ready, 1)
                            dve.wait_ge(inverse_ready, T * b + (t + 1))
                            dve.wait_ge(pv_ready, STEPS * b + PAIRS * (t + 1))
                            dve.wait_ge(ot_ready, CREDIT + T * b + t)
                            nc.vector.tensor_tensor(by_head(heads_out[:]), by_head(pv_banks[t % 2][:]),
                                                    inverse[:, t, :].unsqueeze(2).broadcast_to([P, H, E]),
                                                    ALU.mult).then_inc(normed, 1)


def gated_gelu(core, name, layer, plus=None):
    nc, dram = core.nc, core.dram
    HID = 341
    CHUNKS = [(c, min(P, HID - c)) for c in range(0, HID, P)]
    C = len(CHUNKS)
    with ExitStack() as st:
        def buf(n, shape, dtype=F32):
            return core.sbuf(st, f"{name}_{n}", shape, dtype)

        def sem(n):
            return core.sem(f"{name}_{n}")

        w1, w2, b1 = buf("w1", [P, 2 * HID]), buf("w2", [P, C, D]), buf("b1", [P, 2, C])
        gelu, hidden = buf("gelu", [P, 2, N]), buf("hidden", [P, 2, C, N])
        a_banks, g_banks, y_banks = core.banks[0:2], core.banks[2:4], core.banks[4:6]
        loaded, g_ready, a_ready, gelu_ready = sem("loaded"), sem("g_ready"), sem("a_ready"), sem("gelu_ready")
        hidden_ready, y_ready, y_copied = sem("hidden_ready"), sem("y_ready"), sem("y_copied")
        loads = [(w1[:], dram["w1_gelu"][layer]), (w2[:], dram["w2_gelu"][layer]), (b1[:], dram["b1_gelu"][layer])]

        with core.stage() as block:
            @block.sync
            def _(sp):
                core.clear_spent(sp)
                for place, source in loads:
                    sp.dma_start(place, source).then_inc(loaded, 16)

            @block.tensor
            def _(pe):
                pe.wait_ge(loaded, 16 * len(loads))
                give_credit(pe, y_ready)
                with pe.Fori(0, B // 2) as turn:
                    for u in range(2):
                        x = core.xn_chan[:, bass.ts(turn * 2 + u, N)]
                        for c, (first, rows) in enumerate(CHUNKS):
                            n = C * u + c
                            if n >= 2:
                                pe.wait_ge(gelu_ready, 2 * C * turn + (n - 1))
                            nc.tensor.matmul(g_banks[n % 2][0:rows, :], w1[:, HID + first:HID + first + rows], x
                                             ).then_inc(g_ready, 1)
                            if n >= 2:
                                pe.wait_ge(hidden_ready, 2 * C * turn + (n - 1))
                            nc.tensor.matmul(a_banks[n % 2][0:rows, :], w1[:, first:first + rows], x
                                             ).then_inc(a_ready, 1)
                    for u in range(2):
                        pe.wait_ge(hidden_ready, 2 * C * turn + C * (u + 1))
                        pe.wait_ge(y_copied, CREDIT + 2 * turn)
                        for t in range(T):
                            for c, (_, rows) in enumerate(CHUNKS):
                                tick = nc.tensor.matmul(y_banks[u][:, bass.ts(t, P)], hidden[0:rows, u, c, bass.ts(t, P)],
                                                        w2[0:rows, c, :], start=(c == 0), stop=(c == C - 1))
                        tick.then_inc(y_ready, 1)

            @block.scalar
            def _(act):
                act.wait_ge(loaded, 16 * len(loads))
                with act.Fori(0, B // 2) as turn:
                    for n in range(2 * C):
                        rows = CHUNKS[n % C][1]
                        act.wait_ge(g_ready, 2 * C * turn + (n + 1))
                        if n >= 2:
                            act.wait_ge(hidden_ready, 2 * C * turn + (n - 1))
                        nc.scalar.activation(gelu[0:rows, n % 2, :], g_banks[n % 2][0:rows, :], ACT.Gelu,
                                             bias=b1[0:rows, 1, n % C:n % C + 1]).then_inc(gelu_ready, 1)

            @block.vector
            def _(dve):
                dve.wait_ge(loaded, 16 * len(loads))
                give_credit(dve, y_copied)
                with dve.Fori(0, B // 2) as turn:
                    for n in range(2 * C):
                        u, c = n // C, n % C
                        rows = CHUNKS[c][1]
                        dve.wait_ge(a_ready, 2 * C * turn + (n + 1))
                        dve.wait_ge(gelu_ready, 2 * C * turn + (n + 1))
                        if c == 0:
                            dve.wait_ge(y_ready, CREDIT + 2 * turn)
                        nc.vector.scalar_tensor_tensor(hidden[0:rows, u, c, :], a_banks[n % 2][0:rows, :],
                                                       b1[0:rows, 0, c:c + 1], gelu[0:rows, n % 2, :],
                                                       ALU.add, ALU.mult).then_inc(hidden_ready, 1)
                    for u in range(2):
                        dve.wait_ge(y_ready, CREDIT + 2 * turn + (u + 1))
                        tiles = bass.ts(turn * 2 + u, T)
                        out = core.branch[:, tiles, :]
                        y = y_banks[u][:].rearrange("p (t c) -> p t c", t=T)
                        if plus is None:
                            nc.vector.tensor_copy(out, y).then_inc(y_copied, 1)
                        else:
                            nc.vector.tensor_tensor(out, y, plus[:, tiles, :], ALU.add).then_inc(y_copied, 1)


def windowed_layers(core, layers=2):
    with ExitStack() as st:
        kept = core.sbuf(st, "x_kept", [P, TILES, D])
        join(core, "shift_first", True, shift=True, keep=kept)
        for n in range(layers):
            local_attention(core, f"local{n}", n)
            join(core, f"local_sum{n}", True, residual_norm=False, shift=True, layernorm=(f"ln_g{n}", f"ln_b{n}"))
            gated_gelu(core, f"gelu{n}", n, plus=kept if n == layers - 1 else None)
            if n < layers - 1:
                join(core, f"gelu_sum{n}", True, residual_norm=False, branch_bias=f"b2_gelu{n}", shift=True)
    return f"b2_gelu{layers - 1}"


def at_least(engine, semaphore, value):
    if not isinstance(value, int) or value > 0:
        engine.wait_ge(semaphore, value)


def delta_gates(core, name, beta, neg_beta, rows):
    nc, dram = core.nc, core.dram
    H = 8
    GATE_STEPS = 18
    LARGEST, TOP, ENOUGH = 88.72284, 120.0, 2.5e12
    with ExitStack() as st:
        def buf(n, shape, dtype=F32):
            return core.sbuf(st, f"{name}_{n}", shape, dtype)

        def sem(n):
            return core.sem(f"{name}_{n}")

        w_ab, dt_bias, a_log, zeros = buf("w_ab", [P, 2 * H]), buf("dt_bias", [P, H]), buf("a_log", [P, H]), buf("zeros", [P, P])
        gate, above, below, u, s2, series = (buf(n, [P, H, TILES]) for n in ("gate", "above", "below", "u", "s2", "series"))
        infinite = buf("infinite", [P, H])
        decay_row, product_row = buf("decay_row", [P, P]), buf("product_row", [P, P])
        loaded, ab_ready, step, exp_ready = sem("loaded"), sem("ab_ready"), sem("step"), sem("exp_ready")
        decay_ready, row_ready, stored, zeroed = sem("decay_ready"), sem("row_ready"), sem("stored"), sem("zeroed")
        log_ready = sem("log_ready")
        ab = core.banks[0][:, 0:TILES * 2 * H].rearrange("p (t w h) -> p w h t", t=TILES, w=2)
        wide = [P, H, TILES]

        with core.stage() as block:
            @block.sync
            def _(sp):
                core.clear_spent(sp)
                sp.dma_start(w_ab[:], dram["w_ab"]).then_inc(loaded, 16)
                sp.dma_start(dt_bias[:], dram["dt_bias"].partition_broadcast(P)).then_inc(loaded, 16)
                sp.dma_start(a_log[:], dram["a_log"].partition_broadcast(P)).then_inc(loaded, 16)
                sp.wait_ge(step, GATE_STEPS + 3)
                sp.dma_start(rows[:, 0, :, :], decay_row[:]).then_inc(stored, 16)
                sp.dma_start(rows[:, 1, :, :], product_row[:]).then_inc(stored, 16)
                sp.wait_ge(stored, 32)

            @block.tensor
            def _(pe):
                pe.wait_ge(loaded, 48)
                for t in range(TILES):
                    tick = nc.tensor.matmul(core.banks[0][:, bass.ts(t, 2 * H)], core.xn_chan[:, bass.ts(t, P)], w_ab[:])
                tick.then_inc(ab_ready, 1)
                pe.wait_ge(decay_ready, 1)
                nc.tensor.transpose(core.banks[1][:, 0:P], gate[:].rearrange("p h t -> p (h t)"), core.identity[:]
                                    ).then_inc(row_ready, 1)

            @block.scalar
            def _(act):
                act.wait_ge(log_ready, 3)
                nc.scalar.activation(a_log[:], a_log[:], ACT.Exp).then_inc(exp_ready, 1)
                act.wait_ge(step, 3)
                nc.scalar.activation(u[:], below[:], ACT.Exp).then_inc(exp_ready, 1)
                act.wait_ge(step, GATE_STEPS)
                nc.scalar.activation(gate[:], gate[:], ACT.Exp, scale=-1.0).then_inc(decay_ready, 1)
                nc.scalar.activation(beta[:], ab[:, 1], ACT.Sigmoid).then_inc(exp_ready, 1)

            @block.vector
            def _(dve):
                nc.vector.memset(zeros[:], 0.0).then_inc(zeroed, 1)
                dve.wait_ge(loaded, 48)
                nc.vector.tensor_scalar(infinite[:], a_log[:], LARGEST, 1000.0, ALU.is_gt, ALU.mult).then_inc(log_ready, 1)
                dve.wait_ge(log_ready, 1)
                nc.vector.tensor_tensor(a_log[:], a_log[:], infinite[:], ALU.add).then_inc(log_ready, 1)
                dve.wait_ge(log_ready, 2)
                nc.vector.tensor_scalar(a_log[:], a_log[:], 0.5, TOP / 2, ALU.mult, ALU.min).then_inc(log_ready, 1)
                dve.wait_ge(ab_ready, 1)
                n = 0

                def done(tick):
                    nonlocal n
                    n += 1
                    tick.then_inc(step, 1)
                    dve.wait_ge(step, n)

                done(nc.vector.tensor_tensor(gate[:], ab[:, 0], dt_bias[:].unsqueeze(2).broadcast_to(wide), ALU.add))
                done(nc.vector.tensor_scalar(above[:], gate[:], 0.0, None, ALU.max))
                done(nc.vector.scalar_tensor_tensor(below[:], gate[:], 0.0, above[:], ALU.min, ALU.subtract))
                dve.wait_ge(exp_ready, 2)
                done(nc.vector.tensor_scalar(s2[:], u[:], 2.0, None, ALU.add))
                done(nc.vector.reciprocal(s2[:], s2[:]))
                done(nc.vector.tensor_tensor(u[:], u[:], s2[:], ALU.mult))
                done(nc.vector.tensor_tensor(s2[:], u[:], u[:], ALU.mult))
                done(nc.vector.tensor_scalar(series[:], s2[:], 1.0 / 15, 1.0 / 13, ALU.mult, ALU.add))
                done(nc.vector.tensor_tensor(series[:], series[:], s2[:], ALU.mult))
                for k in (11, 9, 7, 5, 3):
                    done(nc.vector.scalar_tensor_tensor(series[:], series[:], 1.0 / k, s2[:], ALU.add, ALU.mult))
                done(nc.vector.scalar_tensor_tensor(series[:], series[:], 1.0, u[:], ALU.add, ALU.mult))
                done(nc.vector.scalar_tensor_tensor(series[:], series[:], 2.0, above[:], ALU.mult, ALU.add))
                root = a_log[:].unsqueeze(2).broadcast_to(wide)
                done(nc.vector.tensor_tensor(gate[:], series[:], root, ALU.mult))
                done(nc.vector.scalar_tensor_tensor(gate[:], gate[:], ENOUGH, root, ALU.min, ALU.mult))
                assert n == GATE_STEPS
                dve.wait_ge(exp_ready, 3)
                nc.vector.tensor_scalar(neg_beta[:], beta[:], -1.0, None, ALU.mult).then_inc(zeroed, 1)
                dve.wait_ge(row_ready, 1)
                dve.wait_ge(zeroed, 2)
                done(nc.vector.tensor_copy(decay_row[:], core.banks[1][:, 0:P]))
                done(nc.vector.tensor_tensor_scan(product_row[:], decay_row[:], zeros[:], 1.0, ALU.mult, ALU.add))
                done(nc.vector.memset(decay_row[:, 0:1], 0.0))


def delta_rule(core, name, beta, neg_beta, rows):
    nc, dram = core.nc, core.dram
    H, TAPS = 8, 4
    EPS = 1e-6
    SLOTS = 18
    with ExitStack() as st:
        def buf(n, shape, dtype=F32):
            return core.sbuf(st, f"{name}_{n}", shape, dtype)

        def sem(n):
            return core.sem(f"{name}_{n}")

        w_in, w_out, w_conv = buf("w_in", [P, 4, P]), buf("w_out", [P, D]), buf("w_conv", [P, 3, TAPS])
        norm_w = buf("norm_w", [P, D])
        decay, product = buf("decay", [P, TILES, P]), buf("product", [P, TILES, P])
        last_product = buf("last_product", [P, TILES])
        padded = buf("padded", [P, TAPS - 1 + N])
        kq = buf("kq", [P, B, 2, T, P])
        v_chan, v_tok = buf("v_chan", [P, N]), buf("v_tok", [P, B, T, P])
        kq_decayed = buf("kq_decayed", [P, B, 2, T, P])
        k_decayed = buf("k_decayed", [P, B, T, P])
        silu_z, z_scaled = buf("silu_z", [P, T, P]), buf("z_scaled", [P, B, T, P])
        identities = buf("identities", [P, T, P])
        d_t, d_strict = buf("d_t", [P, T, P]), buf("d_strict", [P, T, P])
        x_first = buf("x_first", [P, T, P])
        scores = buf("scores", [P, B, T, P])
        x_t, x_n, inverse = buf("x_t", [P, T, P]), buf("x_n", [P, 2, T, P]), buf("inverse", [P, 2, T, P])
        w_rhs, u = buf("w_rhs", [P, P]), buf("u", [P, P])
        state = buf("state", [P, P])
        squares, o_rms, power = buf("squares", [P, T, P]), buf("o_rms", [P, T]), buf("power", [P, T])
        gated, gated_t = buf("gated", [P, T, P]), buf("gated_t", [P, T, P])
        in_bank, g_bank, a_bank, n_bank, t_bank, r_bank, chain_bank, o_bank = core.banks

        constants_loaded, constants_ready = sem("constants_loaded"), sem("constants_ready")
        w_in_loaded, decay_loaded, product_loaded, w_out_loaded = (
            sem("w_in_loaded"), sem("decay_loaded"), sem("product_loaded"), sem("w_out_loaded"))
        last_ready, place_free = sem("last_ready"), sem("place_free")
        in_ready = [sem(f"{n}_in_ready") for n in "kqvz"]
        padded_ready, tap_ready, conv_ready = sem("padded_ready"), sem("tap_ready"), sem("conv_ready")
        silu_ready, z_ready, kq_decayed_ready = sem("silu_ready"), sem("z_ready"), sem("kq_decayed_ready")
        kt_ready, k_decayed_ready, vt_ready, v_ready = (
            sem("kt_ready"), sem("k_decayed_ready"), sem("vt_ready"), sem("v_ready"))
        d_ready, strict_ready, g_ready, a_ready = sem("d_ready"), sem("strict_ready"), sem("g_ready"), sem("a_ready")
        x_ready, scores_ready = sem("x_ready"), sem("scores_ready")
        n_ready, n_copied, t_ready, t_copied = sem("n_ready"), sem("n_copied"), sem("t_ready"), sem("t_copied")
        r_started, r_ready, r_added = sem("r_started"), sem("r_ready"), sem("r_added")
        ks_ready, w_ready, y_ready, u_ready = sem("ks_ready"), sem("w_ready"), sem("y_ready"), sem("u_ready")
        o_ready, ds_ready, state_ready = sem("o_ready"), sem("ds_ready"), sem("state_ready")
        squares_ready, mean_ready, rms_ready = sem("squares_ready"), sem("mean_ready"), sem("rms_ready")
        gated_ready, gt_ready, gt_copied, out_ready, added = (
            sem("gated_ready"), sem("gt_ready"), sem("gt_copied"), sem("out_ready"), sem("added"))

        K, Q, V, Z = range(4)
        PROJECT_AT = {0: K, 3: Q, 6: V, 9: Z}
        LEVELS = (1, 2, 4, 8, 16)
        INVERT_AT = {0: (1, "n_first")}
        slot = 1
        for power_of in LEVELS:
            for what in ("n", "t") + (("r",) if power_of > 1 else ()):
                INVERT_AT[slot] = (power_of, what)
                slot += 1
        INVERT_AT.update({15: (32, "n"), 16: (32, "r"), 17: (64, "r")})
        assert slot == 15
        N_COPY = {1: 1, 2: 2, 4: 3, 8: 4, 16: 5, 32: 6, 64: 7}
        T_COPY = {2: 1, 4: 2, 8: 3, 16: 4, 32: 5}
        R_ADD = {2: 1, 4: 2, 8: 3, 16: 4, 32: 5, 64: 6}
        RECUR_AT = {}
        slot = 0
        for c in range(T):
            for what in ("w",) * (c > 0) + ("y", "o") + ("s",) * (c < T - 1):
                RECUR_AT[slot] = (c, what)
                slot += 1
        assert slot == 14

        def x_transposed(m):
            return x_first if m == 1 else x_t

        with core.stage() as block:
            def rounds(head, work, first=False, last=False):
                for b in range(B):
                    before = None if first and b == 0 else (head, b - 1) if b else (head - 1, B - 1)
                    after = None if last and b == B - 1 else (head, b + 1) if b < B - 1 else (head + 1, 0)
                    one_round(work, (head, b), after, before)

            def one_round(work, now, after, before):
                invert, prepare, recur = work
                for slot in range(SLOTS):
                    if now is not None:
                        invert(*now, slot)
                    if before is not None:
                        recur(*before, slot)
                    if after is not None:
                        prepare(*after, slot)

            def all_rounds(engine, *work):
                one_round(work, None, (0, 0), None)
                rounds(0, work, first=True)
                with engine.Fori(1, H - 1) as head:
                    rounds(head, work)
                rounds(H - 1, work, last=True)
                one_round(work, None, None, (H - 1, B - 1))

            def count(per_group, head, b, n):
                return head * (B * per_group) + (b * per_group + n)

            def wait(engine, semaphore, per_group, head, b, n):
                at_least(engine, semaphore, count(per_group, head, b, n))

            def column(gate, head, b, c):
                t = b * T + c
                if isinstance(head, int):
                    return gate[:, head, t:t + 1]
                return gate[:, bass.ds(head, 1), t:t + 1].rearrange("p o t -> p (o t)")

            @block.sync
            def _(sp):
                core.clear_spent(sp)
                sp.dma_start(norm_w[:], dram["norm_w"].partition_broadcast(P)).then_inc(constants_loaded, 16)
                sp.dma_start(identities[:, 0, :], core.identity[:]).then_inc(constants_loaded, 16)
                for t in range(1, T):
                    sp.dma_start(identities[:, t, :], core.identity[:]).then_inc(constants_loaded, 16)

                def load(head):
                    wait(sp, in_ready[Z], 1, head, 0, 0)
                    sp.sem_inc(place_free, 1)
                    wait(sp, conv_ready, 3, head, 0, 0)
                    sp.sem_inc(place_free, 1)
                    src = bass.ds(head, 1) if not isinstance(head, int) else slice(head, head + 1)
                    sp.dma_start(w_in[:], dram["w_in"][src, :, :, :]).then_inc(w_in_loaded, 16)
                    sp.dma_start(w_conv[:], dram["w_conv"][src, :, :, :]).then_inc(w_in_loaded, 16)
                    wait(sp, kq_decayed_ready, 1, head, 0, 0)
                    sp.sem_inc(place_free, 1)
                    wait(sp, last_ready, 1, 0, 0, head)
                    sp.sem_inc(place_free, 1)
                    sp.dma_start(product[:].rearrange("p t c -> p (t c)"), rows[src, 1, :, :].rearrange(
                        "h t c -> (h t c)").partition_broadcast(P)).then_inc(product_loaded, 16)
                    wait(sp, d_ready, 1, head, 0, 0)
                    sp.sem_inc(place_free, 1)
                    sp.dma_start(decay[:].rearrange("p t c -> p (t c)"), rows[src, 0, :, :].rearrange(
                        "h t c -> (h t c)").partition_broadcast(P)).then_inc(decay_loaded, 16)
                    wait(sp, out_ready, 1, head, 0, 0)
                    sp.sem_inc(place_free, 1)
                    sp.dma_start(w_out[:], dram["w_out_delta"][src, :, :]).then_inc(w_out_loaded, 16)

                load(0)
                with sp.Fori(1, H) as head:
                    load(head)

            @block.tensor
            def _(pe):
                def project(head, b, which):
                    if which == K:
                        wait(pe, w_in_loaded, 1, 0, 0, (head + 1) * 32)
                        wait(pe, v_ready, 1, head, b, 0)
                    elif which in (Q, V):
                        wait(pe, padded_ready, 6, head, b, 2 * which)
                    else:
                        wait(pe, padded_ready, 6, head, b, 6)
                    if which == Z:
                        for t in range(T):
                            tick = nc.tensor.matmul(in_bank[:, bass.ts(t, P)], core.xn_chan[:, bass.ts(b * T + t, P)],
                                                    w_in[:, Z, :])
                    else:
                        tick = nc.tensor.matmul(in_bank[:], w_in[:, which, :], core.xn_chan[:, bass.ts(b, N)])
                    tick.then_inc(in_ready[which], 1)

                def prepare(head, b, slot):
                    if slot in PROJECT_AT:
                        project(head, b, PROJECT_AT[slot])
                    if slot == 10:
                        wait(pe, conv_ready, 3, head, b, 1)
                        wait(pe, silu_ready, 1, head, b, 1)
                        for t in range(T):
                            tick = nc.tensor.transpose(in_bank[:, bass.ts(t, P)], kq[:, b, 0, t, :], core.identity[:])
                        tick.then_inc(kt_ready, 1)
                    if slot == 11:
                        wait(pe, conv_ready, 3, head, b, 3)
                        wait(pe, k_decayed_ready, 1, head, b, 1)
                        for t in range(T):
                            tick = nc.tensor.transpose(in_bank[:, bass.ts(t, P)], v_chan[:, bass.ts(t, P)], core.identity[:])
                        tick.then_inc(vt_ready, 1)
                    if slot in (12, 13):
                        bank, done, place = ((g_bank, g_ready, 0), (a_bank, a_ready, 1))[slot - 12]
                        wait(pe, (x_ready, scores_ready)[slot - 12], 1, head, b, 0)
                        for t in range(T):
                            tick = nc.tensor.matmul(bank[:, bass.ts(t, P)], kq[:, b, 0, t, :], kq[:, b, place, t, :])
                        tick.then_inc(done, 1)

                def invert(head, b, slot):
                    m, what = INVERT_AT[slot]
                    old = N_COPY[m] - 1 if m in N_COPY else 0
                    if what == "n_first":
                        wait(pe, x_ready, 1, head, b, 1)
                        for t in range(T):
                            tick = nc.tensor.transpose(n_bank[:, bass.ts(t, P)], x_first[:, t, :], core.identity[:])
                        tick.then_inc(n_ready, 1)
                        return
                    wait(pe, n_copied, 7, head, b, N_COPY[m])
                    if m > 1 and m < 64:
                        wait(pe, t_copied, 5, head, b, T_COPY[m])
                    xn, xt = x_n[:, old % 2], x_transposed(m)
                    for t in range(T):
                        cols = bass.ts(t, P)
                        if what == "n":
                            tick = nc.tensor.matmul(n_bank[:, cols], xt[:, t, :], xn[:, t, :])
                        elif what == "t":
                            tick = nc.tensor.matmul(t_bank[:, cols], xn[:, t, :], xt[:, t, :])
                        else:
                            if t == 0:
                                wait(pe, r_started, 1, head, b, 1)
                                wait(pe, r_added, 6, head, b, R_ADD[m] - 1)
                            tick = nc.tensor.matmul(r_bank[:, cols], xn[:, t, :], inverse[:, b % 2, t, :])
                    tick.then_inc({"n": n_ready, "t": t_ready, "r": r_ready}[what], 1)

                def recur(head, b, slot):
                    if slot in RECUR_AT:
                        c, what = RECUR_AT[slot]
                        if what == "w":
                            wait(pe, state_ready, 3, head, b, c)
                            wait(pe, kq_decayed_ready, 1, head, b, 1)
                            nc.tensor.matmul(chain_bank[:, 0:P], kq_decayed[:, b, 0, c, :], state[:]).then_inc(ks_ready, 1)
                        elif what == "y":
                            if c:
                                wait(pe, w_ready, 3, head, b, c)
                            else:
                                wait(pe, v_ready, 1, head, b, 1)
                                wait(pe, r_added, 6, head, b, 6)
                                wait(pe, added, 1, head, b, 0)
                            nc.tensor.matmul(chain_bank[:, 0:P], inverse[:, b % 2, c, :],
                                             w_rhs[:] if c else v_tok[:, b, 0, :]).then_inc(y_ready, 1)
                        elif what == "o":
                            wait(pe, scores_ready, 1, head, b, 1)
                            wait(pe, u_ready, 4, head, b, c + 1)
                            out = o_bank[:, bass.ts(c, P)]
                            if c:
                                nc.tensor.matmul(out, kq_decayed[:, b, 1, c, :], state[:], start=True, stop=False)
                            else:
                                wait(pe, gated_ready, 1, head, b, 0)
                            tick = nc.tensor.matmul(out, scores[:, b, c, :], u[:], start=(c == 0), stop=True)
                            if c == T - 1:
                                tick.then_inc(o_ready, 1)
                        else:
                            wait(pe, k_decayed_ready, 1, head, b, 1)
                            nc.tensor.matmul(chain_bank[:, 0:P], k_decayed[:, b, c, :], u[:]).then_inc(ds_ready, 1)
                    if slot == 16:
                        wait(pe, gated_ready, 1, head, b, 1)
                        for t in range(T):
                            tick = nc.tensor.transpose(chain_bank[:, bass.ts(t, P)], gated[:, t, :], core.identity[:])
                        tick.then_inc(gt_ready, 1)
                    if slot == 17:
                        wait(pe, gt_copied, 1, head, b, 1)
                        wait(pe, w_out_loaded, 1, 0, 0, (head + 1) * 16)
                        for t in range(T):
                            tick = nc.tensor.matmul(chain_bank[:, bass.ts(t, P)], gated_t[:, t, :], w_out[:])
                        tick.then_inc(out_ready, 1)

                all_rounds(pe, invert, prepare, recur)

            @block.scalar
            def _(act):
                act.wait_ge(constants_ready, 3)

                def prepare(head, b, slot):
                    if slot in (0, 3, 6):
                        which = PROJECT_AT[slot]
                        wait(act, in_ready[which], 1, head, b, 1)
                        wait(act, conv_ready, 3, head, b, which)
                        nc.scalar.copy(padded[:, TAPS - 1:], in_bank[:]).then_inc(padded_ready, 1)
                        if which == V:
                            out, source = v_chan[:], in_bank[:]
                        else:
                            out, source = kq[:, b, which, :, :], in_bank[:].rearrange("p (t c) -> p t c", t=T)
                        nc.scalar.activation(out, source, ACT.Copy, scale=w_conv[:, which, TAPS - 1:TAPS]
                                             ).then_inc(padded_ready, 1)
                    if slot == 9:
                        wait(act, in_ready[Z], 1, head, b, 1)
                        wait(act, z_ready, 1, head, b, 0)
                        nc.scalar.activation(silu_z[:], in_bank[:].rearrange("p (t c) -> p t c", t=T), ACT.Silu
                                             ).then_inc(silu_ready, 1)
                    if slot == 11:
                        wait(act, vt_ready, 1, head, b, 1)
                        nc.scalar.copy(v_tok[:, b, :, :], in_bank[:].rearrange("p (t c) -> p t c", t=T)
                                       ).then_inc(v_ready, 1)

                def invert(head, b, slot):
                    m, what = INVERT_AT[slot]
                    if what in ("n_first", "n"):
                        n = 0 if what == "n_first" else N_COPY[m]
                        wait(act, n_ready, 7, head, b, n + 1)
                        nc.scalar.copy(x_n[:, n % 2], n_bank[:].rearrange("p (t c) -> p t c", t=T)).then_inc(n_copied, 1)
                    elif what == "t":
                        wait(act, t_ready, 5, head, b, T_COPY[2 * m])
                        nc.scalar.copy(x_t[:], t_bank[:].rearrange("p (t c) -> p t c", t=T)).then_inc(t_copied, 1)

                def recur(head, b, slot):
                    if slot in RECUR_AT and RECUR_AT[slot][1] == "y":
                        c = RECUR_AT[slot][0]
                        wait(act, y_ready, 4, head, b, c + 1)
                        nc.scalar.activation(u[:], chain_bank[:, 0:P], ACT.Copy, scale=column(beta, head, b, c)
                                             ).then_inc(u_ready, 1)
                    if slot == 14:
                        wait(act, o_ready, 1, head, b, 1)
                        for t in range(T):
                            tick = nc.scalar.activation(squares[:, t, :], o_bank[:, bass.ts(t, P)], ACT.Square,
                                                        accum_out=o_rms[:, t:t + 1])
                        tick.then_inc(squares_ready, 1)
                    if slot == 16:
                        wait(act, gt_ready, 1, head, b, 1)
                        nc.scalar.copy(gated_t[:], chain_bank[:].rearrange("p (t c) -> p t c", t=T)).then_inc(gt_copied, 1)

                all_rounds(act, invert, prepare, recur)

            @block.gpsimd
            def _(pool):
                nc.gpsimd.memset(power[:], -0.5).then_inc(constants_ready, 1)
                nc.gpsimd.memset(core.branch[:], 0.0).then_inc(constants_ready, 1)
                nc.gpsimd.memset(padded[:, 0:TAPS - 1], 0.0).then_inc(constants_ready, 1)
                pool.wait_ge(constants_ready, 3)
                pool.wait_ge(constants_loaded, 16 * (1 + T))

                def prepare(head, b, slot):
                    if slot == 5:
                        wait(pool, conv_ready, 3, head, b, 2)
                        wait(pool, product_loaded, 1, 0, 0, (head + 1) * 16)
                        for i in range(2):
                            tick = nc.gpsimd.tensor_tensor(kq_decayed[:, b, i], kq[:, b, i],
                                                           product[:, b * T:(b + 1) * T, :], ALU.mult)
                        tick.then_inc(kq_decayed_ready, 1)
                    if slot == 9:
                        wait(pool, d_ready, 1, head, b, 1)
                        nc.gpsimd.tensor_tensor(d_strict[:], d_t[:], identities[:], ALU.subtract).then_inc(strict_ready, 1)
                        wait(pool, silu_ready, 1, head, b, 1)
                        nc.gpsimd.tensor_tensor(z_scaled[:, b], silu_z[:], norm_w[:].unsqueeze(1).broadcast_to([P, T, P]),
                                                ALU.mult).then_inc(z_ready, 1)

                def invert(head, b, slot):
                    if slot == 0:
                        wait(pool, x_ready, 1, head, b, 1)
                        nc.gpsimd.tensor_tensor(inverse[:, b % 2], x_first[:], identities[:], ALU.add).then_inc(r_started, 1)

                def recur(head, b, slot):
                    if slot == 14:
                        wait(pool, mean_ready, 1, head, b, 1)
                        nc.gpsimd.tensor_tensor(o_rms[:], o_rms[:], power[:], ALU.pow).then_inc(rms_ready, 1)

                all_rounds(pool, invert, prepare, recur)

            @block.vector
            def _(dve):
                dve.wait_ge(constants_ready, 3)
                dve.wait_ge(constants_loaded, 16 * (1 + T))

                def tap(head, b, which, n):
                    if n == 0:
                        wait(dve, padded_ready, 6, head, b, 2 * which + 2)
                    else:
                        wait(dve, tap_ready, 6, head, b, 2 * which + n)
                    shifted = padded[:, TAPS - 2 - n:TAPS - 2 - n + N]
                    out = v_chan[:]
                    if which != V:
                        out, shifted = kq[:, b, which, :, :], shifted.rearrange("p (t c) -> p t c", t=T)
                    nc.vector.scalar_tensor_tensor(out, shifted, w_conv[:, which, TAPS - 2 - n:TAPS - 1 - n], out,
                                                   ALU.mult, ALU.add).then_inc(conv_ready if n == 2 else tap_ready, 1)

                def prepare(head, b, slot):
                    if slot < 9:
                        tap(head, b, slot // 3, slot % 3)
                    if slot == 9:
                        wait(dve, decay_loaded, 1, 0, 0, (head + 1) * 16)
                        wait(dve, strict_ready, 1, head, b, 0)
                        nc.vector.tensor_tensor_scan(
                            d_t[:].rearrange("p t c -> p (t c)"),
                            decay[:, b * T:(b + 1) * T, :].rearrange("p t c -> p (t c)"),
                            identities[:].rearrange("p t c -> p (t c)"), 0.0, ALU.mult, ALU.add).then_inc(d_ready, 1)
                    if slot == 10:
                        wait(dve, kt_ready, 1, head, b, 1)
                        wait(dve, d_ready, 1, head, b, 1)
                        nc.vector.tensor_tensor(k_decayed[:, b], in_bank[:].rearrange("p (t c) -> p t c", t=T),
                                                d_t[:, :, P - 1:P].broadcast_to([P, T, P]), ALU.mult
                                                ).then_inc(k_decayed_ready, 1)
                    if slot == 12:
                        wait(dve, g_ready, 1, head, b, 1)
                        wait(dve, strict_ready, 1, head, b, 1)
                        for t in range(T):
                            tick = nc.vector.scalar_tensor_tensor(x_first[:, t, :], g_bank[:, bass.ts(t, P)],
                                                                  column(neg_beta, head, b, t), d_strict[:, t, :],
                                                                  ALU.mult, ALU.mult)
                        tick.then_inc(x_ready, 1)
                    if slot == 13:
                        wait(dve, a_ready, 1, head, b, 1)
                        nc.vector.tensor_tensor(scores[:, b], a_bank[:].rearrange("p (t c) -> p t c", t=T), d_t[:], ALU.mult
                                                ).then_inc(scores_ready, 1)

                def invert(head, b, slot):
                    m, what = INVERT_AT[slot]
                    if what == "r":
                        wait(dve, r_ready, 6, head, b, R_ADD[m])
                        wait(dve, r_started, 1, head, b, 1)
                        wait(dve, r_added, 6, head, b, R_ADD[m] - 1)
                        r = inverse[:, b % 2]
                        nc.vector.tensor_tensor(r, r, r_bank[:].rearrange("p (t c) -> p t c", t=T), ALU.add
                                                ).then_inc(r_added, 1)

                def recur(head, b, slot):
                    if slot == 0 and b == 0:
                        wait(dve, product_loaded, 1, 0, 0, (head + 1) * 16)
                        nc.vector.tensor_copy(last_product[:], product[:, :, P - 1]).then_inc(last_ready, 1)
                    if slot in RECUR_AT:
                        c, what = RECUR_AT[slot]
                        if what == "w":
                            wait(dve, ks_ready, 3, head, b, c)
                            nc.vector.tensor_tensor(w_rhs[:], v_tok[:, b, c, :], chain_bank[:, 0:P], ALU.subtract
                                                    ).then_inc(w_ready, 1)
                        elif what == "s":
                            wait(dve, ds_ready, 3, head, b, c + 1)
                            if c == 0:
                                nc.vector.tensor_copy(state[:], chain_bank[:, 0:P]).then_inc(state_ready, 1)
                            else:
                                wait(dve, state_ready, 3, head, b, c)
                                wait(dve, last_ready, 1, 0, 0, head + 1)
                                nc.vector.scalar_tensor_tensor(state[:], state[:], last_product[:, b * T + c:b * T + c + 1],
                                                               chain_bank[:, 0:P], ALU.mult, ALU.add
                                                               ).then_inc(state_ready, 1)
                    if slot == 14:
                        wait(dve, squares_ready, 1, head, b, 1)
                        nc.vector.tensor_scalar(o_rms[:], o_rms[:], 1.0 / P, EPS, ALU.mult, ALU.add).then_inc(mean_ready, 1)
                    if slot == 15:
                        wait(dve, rms_ready, 1, head, b, 1)
                        wait(dve, z_ready, 1, head, b, 1)
                        for t in range(T):
                            tick = nc.vector.scalar_tensor_tensor(gated[:, t, :], o_bank[:, bass.ts(t, P)], o_rms[:, t:t + 1],
                                                                  z_scaled[:, b, t, :], ALU.mult, ALU.mult)
                        tick.then_inc(gated_ready, 1)
                    if slot == 17:
                        wait(dve, out_ready, 1, head, b, 1)
                        wait(dve, added, 1, head, b, 0)
                        out = core.branch[:, b * T:(b + 1) * T, :]
                        nc.vector.tensor_tensor(out, out, chain_bank[:].rearrange("p (t c) -> p t c", t=T), ALU.add
                                                ).then_inc(added, 1)

                all_rounds(dve, invert, prepare, recur)


def delta_layer(core):
    nc = core.nc
    with ExitStack() as st:
        beta = core.sbuf(st, "beta", [P, 8, TILES])
        neg_beta = core.sbuf(st, "neg_beta", [P, 8, TILES])
        rows = nc.dram_tensor("decay_rows", (8, 2, TILES, P), F32, kind="Internal").ap()
        delta_gates(core, "delta_gates", beta, neg_beta, rows)
        delta_rule(core, "delta", beta, neg_beta, rows)


def build(nc, dram):
    with ExitStack() as stack:
        core = Core(nc, stack, dram)
        load_tokens(core)
        join(core, "first", False, rms=(float(np.finfo(np.float32).eps), 0.0), scale="rms_w")
        attention(core, "causal", "w_attn0", pairs=4, causal=True, gates="w_gates")
        join(core, "sum0", True)
        two_of_eight(core, "experts8", "w_experts8", "w_gate8")
        join(core, "sum1", True, rms=(0.0, 1e-24 / D), scale="gamma", scale_plus=1.0)
        attention(core, "full", "w_attn1", pairs=8)
        last_bias = windowed_layers(core)
        join(core, "sum3", True, branch_bias=last_bias)
        linear_attention(core, "linear")
        join(core, "sum4", True)
        token_mix(core, "mix")
        join(core, "sum5", True)
        delta_layer(core)
        join(core, "sum6", True)
        one_of_many(core, "experts32")
        join(core, "sum7", True, to_chan=False, store=dram["out"])


def layout(a):
    a = {k: np.asarray(v) for k, v in a.items()}
    out = {"tokens": a["L0_attn_tokens"], "identity": np.eye(P, dtype=np.float32)}

    def by_pair(w):
        return w.reshape(D, -1, 128).transpose(1, 0, 2)

    def by_tile(x):
        return x.reshape(T, P, -1).transpose(1, 0, 2).astype(np.float32)

    def by_head(w):
        return w.transpose(1, 0, 2).reshape(D, -1)

    q, k, v = (by_pair(by_head(a[f"L0_attn_w{n}"])) for n in "qkv")
    out["w_attn0"] = np.stack([q, k, v, a["L0_attn_wo"].reshape(-1, 128, D)], 2)
    out["w_gates"] = a["L0_attn_w_gates"]
    out["rms_w"] = a["L0_attn_rms_w"][:, None]
    i = np.arange(P)
    out["causal_mask"] = np.where(i[None, :] > i[:, None], -3.0e38, 0.0).astype(np.float32)
    q, k, v = (by_pair(w) for w in np.split(a["L1_attn_w_qkv"], 3, 1))
    out["w_attn1"] = np.stack([q, k, v, a["L1_attn_w_out"].reshape(-1, 128, D)], 2)
    out["gamma"] = a["L1_attn_gamma"][:, None]
    out["w_gate8"] = a["L0_ffn_gate_w"].T
    out["numbers8"] = np.arange(8, dtype=np.float32)
    w2 = a["L0_ffn_w2"].reshape(8, 2, P, D).transpose(0, 2, 1, 3).reshape(8, P, 2 * D)
    out["w_experts8"] = np.stack([a["L0_ffn_w1"], a["L0_ffn_w3"], w2], 2)
    out["w_router"] = a["L3_ffn_router_w"].T
    out["router_b"] = a["L3_ffn_router_b"]
    out["numbers32"] = np.arange(32, dtype=np.float32)
    out["w1_many"] = a["L3_ffn_weights1"].reshape(8, 4, D, 32).transpose(2, 0, 1, 3).reshape(D, 8, P)
    out["b1_many"] = a["L3_ffn_bias1"].reshape(8, P).T
    out["w2_many"] = a["L3_ffn_weights2"].reshape(8, P, D).transpose(1, 0, 2)
    out["b2_many"] = a["L3_ffn_bias2"]
    out["spread"] = np.repeat(np.eye(32, dtype=np.float32), 32, 1).reshape(32, 8, P)
    out["w_qkv2"] = a["L2_attn_Wqkv"].T
    out["b_qkv2"] = a["L2_attn_bqkv"]
    out["w_out2"] = a["L2_attn_Wout"].T
    out["b_out2"], out["g_out2"] = a["L2_attn_bout"], a["L2_attn_gout"]
    out["g_q2"], out["g_k2"] = a["L2_attn_gq"], a["L2_attn_gk"]
    inv_freq = 1.0 / 10000.0 ** (np.arange(0, 8, 2, dtype=np.float32) / 8)
    freqs = np.tile(np.outer(np.arange(N, dtype=np.float32), inv_freq.astype(np.float32)), (1, 16))
    out["cos2"], out["sin2"] = (by_tile(f(freqs.astype(np.float32))) for f in (np.cos, np.sin))
    out["same_head"] = np.kron(np.eye(16, dtype=np.float32), np.ones((8, 8), np.float32))
    out["w_r"], out["w_k"], out["w_v"] = (a[f"L2_ffn_W_{n}"].T for n in "rkv")
    out["mu"] = np.stack([a["L2_ffn_mu_r"], a["L2_ffn_mu_k"]], 1)
    H, E, HID = 8, 64, 341
    out["w_qkv_local"] = a["L1_ffn_wqkv"].reshape(2, D, 3, H * E)
    out["w_out_local"] = a["L1_ffn_wo"].reshape(2, 4, P, D).transpose(0, 2, 1, 3)
    r, k = np.arange(P)[:, None], np.arange(64 + P)[None, :]
    out["local_mask"] = np.where((k > r + 64) | (k < r), -3.0e38, 0.0).astype(np.float32)
    qs, ks = a["L1_ffn_q_scale"], a["L1_ffn_k_scale"]
    out["head_scale"] = np.stack([qs, np.roll(qs, E // 2, 1), ks, np.roll(ks, E // 2, 1)], 1)
    half = np.arange(0, E, 2, dtype=np.float32)
    t = np.arange(N, dtype=np.float32)
    freqs = t[:, None] * (1.0 / 10000.0 ** (half / E)).astype(np.float32)[None, :]
    xpos = ((half + 0.4 * E) / (1.4 * E))[None, :] ** ((t - N // 2) / 32.0)[:, None]
    cos, sin = np.cos(freqs), np.sin(freqs)
    tables = [np.concatenate([s * f * x, f * x], 1) for x in (8.0 * xpos, 1.0 / xpos) for s, f in ((1, cos), (-1, sin))]
    out["rotary"] = np.stack([by_tile(x) for x in tables])
    pad = [(0, 0), (0, 0), (0, 3 * P - HID)]
    out["w1_gelu"] = a["L1_ffn_w1"]
    out["w2_gelu"] = np.pad(a["L1_ffn_w2"], [(0, 0), (0, 3 * P - HID), (0, 0)]).reshape(2, 3, P, D).transpose(0, 2, 1, 3)
    out["b1_gelu"] = np.pad(a["L1_ffn_b1"].reshape(2, 2, HID), pad).reshape(2, 2, 3, P).transpose(0, 3, 1, 2)
    for n in range(2):
        out[f"b2_gelu{n}"] = a["L1_ffn_b2"][n]
        out[f"ln_g{n}"], out[f"ln_b{n}"] = a["L1_ffn_ln_g"][n][:, None], a["L1_ffn_ln_b"][n][:, None]
    H = 8
    qkv = a["L3_attn_qkv_w"].reshape(3, H, P, D)[[1, 0, 2]]
    w_in = np.concatenate([qkv, a["L3_attn_z_w"].reshape(1, H, P, D)])
    out["w_in"] = w_in.transpose(1, 3, 0, 2)
    out["w_conv"] = a["L3_attn_conv_w"].reshape(3, H, P, 4)[[1, 0, 2]].transpose(1, 2, 0, 3)
    out["w_out_delta"] = a["L3_attn_out_w"].T.reshape(H, P, D)
    out["w_ab"] = np.concatenate([a["L3_attn_a_w"], a["L3_attn_b_w"]]).T
    out["dt_bias"], out["a_log"], out["norm_w"] = a["L3_attn_dt_bias"], a["L3_attn_A_log"], a["L3_attn_norm_w"]
    return out


def kernel(**inputs):
    import concourse.bacc as bacc
    from concourse.bass_utils import run_bass_kernel_spmd

    nc = bacc.Bacc("TRN2", target_bir_lowering=False, num_devices=1)
    arrays, dram = {}, {}
    for name, a in layout(inputs).items():
        a = np.ascontiguousarray(a)
        arrays[f"in_{name}"] = a
        dram[name] = nc.dram_tensor(f"in_{name}", a.shape, mybir.dt.from_np(a.dtype), kind="ExternalInput").ap()
    dram["out"] = nc.dram_tensor("out", (B, N, D), F32, kind="ExternalOutput").ap()
    build(nc, dram)
    done = run_bass_kernel_spmd(nc, [arrays], core_ids=[0])
    return done.results[0]["out"]
```

```python
from contextlib import ExitStack, contextmanager

import numpy as np

import concourse.bass as bass
from concourse import mybir

F32 = mybir.dt.float32
BF16 = mybir.dt.bfloat16
U32 = mybir.dt.uint32
ALU = mybir.AluOpType
ACT = mybir.ActivationFunctionType
AX_X = mybir.AxisListType.X

P = 128
B, N, D = 4, 512, 128
T = N // P
TILES = B * T
TOKENS = B * N

CREDIT = 1


def give_credit(engine, *semaphores):
    for s in semaphores:
        engine.sem_inc(s, CREDIT)


class Core:

    def __init__(self, nc, stack, dram):
        self.nc, self.stack, self.dram = nc, stack, dram
        self.sems, self.spent_sems = ExitStack(), ExitStack()
        self.in_use, self.spent = [], []
        self.x_tok = self.sbuf(stack, "x_tok", [P, TILES, D])
        self.branch = self.sbuf(stack, "branch", [P, TILES, D])
        self.xn_chan = self.sbuf(stack, "xn_chan", [P, TOKENS])
        self.identity = self.sbuf(stack, "identity", [P, P])
        self.identity_bf = self.sbuf(stack, "identity_bf", [P, P], BF16)
        self.psum = stack.enter_context(nc.psum_tensor("psum", [P, 8, 512], F32))
        self.banks = [self.psum[:, i, :] for i in range(8)]

    def sbuf(self, stack, name, shape, dtype=F32):
        return stack.enter_context(self.nc.sbuf_tensor(name, shape, dtype))

    def sem(self, name):
        s = self.sems.enter_context(self.nc.semaphore(name))
        self.in_use.append(s)
        return s

    @contextmanager
    def stage(self):
        with self.nc.Block() as block:
            yield block
        assert not self.spent, "the stage has not cleared its forerunner's semaphores"
        self.spent_sems.close()
        self.spent_sems, self.sems = self.sems, ExitStack()
        self.spent, self.in_use = self.in_use, []

    def clear_spent(self, sp):
        for s in self.spent:
            sp.sem_clear(s)
        self.spent = []


def join(core, name, load=False, add_branch=True, rms=None, scale=None, scale_plus=0.0, shift=False, layernorm=None,
         to_chan=True, residual_norm=True, branch_bias=None, keep=None, store=None):
    nc, dram = core.nc, core.dram
    HALF = D // 2
    with ExitStack() as st:
        def buf(n, shape, dtype=F32):
            return core.sbuf(st, f"{name}_{n}", shape, dtype)

        def sem(n):
            return core.sem(f"{name}_{n}")

        own_operand = rms is not None or layernorm is not None
        parts, moments = buf("parts", [P, TILES, 6]), buf("moments", [P, TILES, 2])
        parts2, moments2 = buf("parts2", [P, TILES, 6]), buf("moments2", [P, TILES, 2])
        power, rstd, rstd2 = buf("power", [P, T]), buf("rstd", [P, TILES]), buf("rstd2", [P, TILES])
        squares, column, row = buf("squares", [P, 2, D]), buf("column", [P, 2]), buf("row", [P, D])
        operand = buf("operand", [P, TILES, D]) if own_operand else core.x_tok
        shifted = buf("shifted", [P, TILES, D]) if layernorm else None

        identity_loaded, identity_converted, x_loaded = (
            sem("identity_loaded"), sem("identity_converted"), sem("x_loaded"))
        columns_loaded, column_ready, row_added = sem("columns_loaded"), sem("column_ready"), sem("row_added")
        power_ready, sum_ready, parts_ready = sem("power_ready"), sem("sum_ready"), sem("parts_ready")
        moments_ready, var_ready, rstd_ready = sem("moments_ready"), sem("var_ready"), sem("rstd_ready")
        x_ready, squares_ready = sem("x_ready"), sem("squares_ready")
        zeroed, half_copied, rest_shifted = sem("zeroed"), sem("half_copied"), sem("rest_shifted")
        parts2_ready, moments2_ready = sem("parts2_ready"), sem("moments2_ready")
        var2_ready, rstd2_ready = sem("var2_ready"), sem("rstd2_ready")
        operand_ready, transposed, stored = sem("operand_ready"), sem("transposed"), sem("stored")
        columns = [dram[n] for n in ([scale] if scale else list(layernorm or ()))]
        loads = 16 * (len(columns) + bool(branch_bias))

        def tiles(g):
            return range(g * T, (g + 1) * T)

        def group(g):
            return slice(g * T, (g + 1) * T)

        def wait_x(engine, g):
            if add_branch:
                engine.wait_ge(x_ready, g + 1)
            elif load:
                engine.wait_ge(x_loaded, 16 * (g + 1))

        with core.stage() as block:
            @block.sync
            def _(sp):
                core.clear_spent(sp)
                if load:
                    for g in range(B):
                        if g > 0:
                            sp.wait_ge(x_loaded, 16 * g)
                        sp.dma_start(core.x_tok[:, group(g), :],
                                     dram["tokens"][g].rearrange("(t p) d -> p t d", p=P)).then_inc(x_loaded, 16)
                        if g == 0:
                            sp.dma_start(core.identity[:], dram["identity"]).then_inc(identity_loaded, 16)
                for i, source in enumerate(columns):
                    sp.dma_start(column[:, i:i + 1], source).then_inc(columns_loaded, 16)
                if branch_bias:
                    sp.dma_start(row[:], dram[branch_bias].partition_broadcast(P)).then_inc(columns_loaded, 16)
                if layernorm:
                    for g in range(B):
                        wait_x(sp, g)
                        if g > 0:
                            sp.wait_ge(rest_shifted, 32 * g)
                        sp.dma_start(shifted[1:P, group(g), HALF:D],
                                     core.x_tok[0:P - 1, group(g), HALF:D]).then_inc(rest_shifted, 16)
                        sp.dma_start(shifted[0:1, g * T + 1:(g + 1) * T, HALF:D],
                                     core.x_tok[P - 1:P, g * T:(g + 1) * T - 1, HALF:D]).then_inc(rest_shifted, 16)
                if store is not None:
                    for g in range(B):
                        wait_x(sp, g)
                        sp.dma_start(store[g].rearrange("(t p) d -> p t d", p=P),
                                     core.x_tok[:, group(g), :]).then_inc(stored, 16)
                    sp.wait_ge(stored, 16 * B)
                if loads:
                    sp.wait_ge(columns_loaded, loads)

            @block.vector
            def _(dve):
                def add(g):
                    if branch_bias:
                        dve.wait_ge(row_added, g + 1)
                    x_g = core.x_tok[:, group(g), :]
                    tick = nc.vector.tensor_tensor(x_g, x_g, core.branch[:, group(g), :], ALU.add)
                    if not residual_norm:
                        tick.then_inc(x_ready, 1)
                        return
                    tick.then_inc(sum_ready, 1)
                    dve.wait_ge(sum_ready, g + 1)
                    for i in tiles(g):
                        tick = nc.vector.bn_stats(parts[:, i, :], core.x_tok[:, i, :])
                    tick.then_inc(parts_ready, 1)
                    dve.wait_ge(parts_ready, g + 1)
                    for i in tiles(g):
                        tick = nc.vector.bn_aggr(moments[:, i, :], parts[:, i, :])
                    tick.then_inc(moments_ready, 1)

                def normalize(g):
                    dve.wait_ge(moments_ready, g + 1)
                    dve.wait_ge(rstd_ready, g + 1)
                    for i in tiles(g):
                        tick = nc.vector.tensor_scalar(core.x_tok[:, i, :], core.x_tok[:, i, :], moments[:, i, 0:1],
                                                       rstd[:, i:i + 1], ALU.subtract, ALU.mult)
                    tick.then_inc(x_ready, 1)

                def measure(g):
                    dve.wait_ge(zeroed, 1)
                    dve.wait_ge(half_copied, g + 1)
                    dve.wait_ge(rest_shifted, 32 * (g + 1))
                    for i in tiles(g):
                        tick = nc.vector.bn_stats(parts2[:, i, :], shifted[:, i, :])
                    tick.then_inc(parts2_ready, 1)
                    dve.wait_ge(parts2_ready, g + 1)
                    for i in tiles(g):
                        tick = nc.vector.bn_aggr(moments2[:, i, :], parts2[:, i, :])
                    tick.then_inc(moments2_ready, 1)

                def make_operand(g):
                    dve.wait_ge(rstd2_ready, g + 1)
                    if layernorm:
                        dve.wait_ge(moments2_ready, g + 1)
                    else:
                        wait_x(dve, g)
                    for i in tiles(g):
                        if layernorm:
                            tick = nc.vector.tensor_scalar(operand[:, i, :], shifted[:, i, :], moments2[:, i, 0:1],
                                                           rstd2[:, i:i + 1], ALU.subtract, ALU.mult)
                        else:
                            tick = nc.vector.tensor_scalar(operand[:, i, :], core.x_tok[:, i, :],
                                                           rstd2[:, i:i + 1], None, ALU.mult)
                    tick.then_inc(operand_ready, 1)

                if load:
                    dve.wait_ge(identity_loaded, 16)
                    nc.vector.tensor_copy(core.identity_bf[:], core.identity[:]).then_inc(identity_converted, 1)
                for at in range(B + 3):
                    if add_branch and at < B:
                        add(at)
                    if add_branch and residual_norm and 0 <= at - 1 < B:
                        normalize(at - 1)
                    if layernorm and 0 <= at - 2 < B:
                        measure(at - 2)
                    if own_operand and 0 <= at - 3 < B:
                        make_operand(at - 3)

            @block.gpsimd
            def _(pool):
                nc.gpsimd.memset(power[:], -0.5).then_inc(power_ready, 1)
                pool.wait_ge(power_ready, 1)
                if shift:
                    for g in range(B):
                        place = (shifted[0:1, g * T, HALF:D] if layernorm else
                                 core.xn_chan[HALF:D, g * N:g * N + 1])
                        tick = nc.gpsimd.memset(place, 0.0)
                    tick.then_inc(zeroed, 1)
                    pool.wait_ge(zeroed, 1)
                if scale_plus:
                    pool.wait_ge(columns_loaded, loads)
                    nc.gpsimd.tensor_scalar(column[:, 0:1], column[:, 0:1], scale_plus, None,
                                            ALU.add).then_inc(column_ready, 1)

                def inverse_root(place, source, eps, ready, root_ready, g):
                    nc.gpsimd.tensor_scalar(place, source, eps, None, ALU.add).then_inc(ready, 1)
                    pool.wait_ge(ready, g + 1)
                    nc.gpsimd.tensor_tensor(place, place, power[:], ALU.pow).then_inc(root_ready, 1)

                for at in range(B + 2):
                    if branch_bias and at < B:
                        if at == 0:
                            pool.wait_ge(columns_loaded, loads)
                        br_g = core.branch[:, group(at), :]
                        nc.gpsimd.tensor_tensor(br_g, br_g, row[:].unsqueeze(1).broadcast_to([P, T, D]),
                                                ALU.add).then_inc(row_added, 1)
                    if add_branch and residual_norm and 0 <= at - 1 < B:
                        pool.wait_ge(moments_ready, at)
                        inverse_root(rstd[:, group(at - 1)], moments[:, group(at - 1), 1], 1e-5, var_ready,
                                     rstd_ready, at - 1)
                    if layernorm and 0 <= at - 2 < B:
                        pool.wait_ge(moments2_ready, at - 1)
                        inverse_root(rstd2[:, group(at - 2)], moments2[:, group(at - 2), 1], 1e-5, var2_ready,
                                     rstd2_ready, at - 2)
                    if rms is not None and 0 <= at - 2 < B:
                        pool.wait_ge(squares_ready, T * (at - 1))
                        r = rstd2[:, group(at - 2)]
                        nc.gpsimd.tensor_scalar(r, r, 1.0 / D, rms[1], ALU.mult, rms[0]).then_inc(var2_ready, 1)
                        pool.wait_ge(var2_ready, at - 1)
                        nc.gpsimd.tensor_tensor(r, r, power[:], ALU.pow).then_inc(rstd2_ready, 1)

            @block.scalar
            def _(act):
                def early(g):
                    wait_x(act, g)
                    if rms is not None:
                        for i in tiles(g):
                            if i >= 2:
                                act.wait_ge(squares_ready, i - 1)
                            nc.scalar.activation(squares[:, i % 2, :], core.x_tok[:, i, :], ACT.Square,
                                                 accum_out=rstd2[:, i:i + 1]).then_inc(squares_ready, 1)
                    if layernorm:
                        nc.scalar.copy(shifted[:, group(g), 0:HALF], core.x_tok[:, group(g), 0:HALF]
                                       ).then_inc(half_copied, 1)
                    if keep is not None:
                        nc.scalar.copy(keep[:, group(g), :], core.x_tok[:, group(g), :])

                def evacuate(g):
                    act.wait_ge(transposed, g + 1)
                    out, bank = core.xn_chan[:, g * N:(g + 1) * N], core.banks[g]
                    if layernorm:
                        nc.scalar.activation(out, bank[:], ACT.Identity, bias=column[:, 1:2], scale=column[:, 0:1])
                    elif scale:
                        nc.scalar.activation(out, bank[:], ACT.Copy, scale=column[:, 0:1])
                    elif shift:
                        nc.scalar.copy(core.xn_chan[0:HALF, g * N:(g + 1) * N], bank[0:HALF, :])
                        nc.scalar.copy(core.xn_chan[HALF:D, g * N + 1:(g + 1) * N], bank[HALF:D, 0:N - 1])
                    else:
                        nc.scalar.copy(out, bank[:])

                if columns:
                    act.wait_ge(columns_loaded, loads)
                if scale_plus:
                    act.wait_ge(column_ready, 1)
                LAG = 3 if own_operand else 1
                for at in range(B + LAG):
                    if at < B and (own_operand or keep is not None):
                        early(at)
                    if to_chan and 0 <= at - LAG < B:
                        evacuate(at - LAG)

            @block.tensor
            def _(pe):
                if load:
                    pe.wait_ge(identity_loaded, 16)
                for g in range(B if to_chan else 0):
                    if own_operand:
                        pe.wait_ge(operand_ready, g + 1)
                    else:
                        wait_x(pe, g)
                    for n, i in enumerate(tiles(g)):
                        tick = nc.tensor.transpose(core.banks[g][:, n * P:(n + 1) * P], operand[:, i, :],
                                                   core.identity[:])
                    tick.then_inc(transposed, 1)


def at_least(engine, semaphore, value):
    if not isinstance(value, int) or value > 0:
        engine.wait_ge(semaphore, value)


def attention(core, name, weights, pairs, causal=False, gates=None):
    nc, dram = core.nc, core.dram
    E = 64
    STEPS = B * T
    LAG_T, LAG_PV = 2, 3
    LAST_OF_SEQ = T - 1 + LAG_PV
    EDGE = 3 * T
    TAIL = LAST_OF_SEQ + 4 - T
    P_RING = 4
    W_AT, WO_AT = STEPS - T, T
    with ExitStack() as st:
        def buf(n, shape, dtype=F32):
            return core.sbuf(st, f"{name}_{n}", shape, dtype)

        def sem(n):
            return core.sem(f"{name}_{n}")

        w_land, w_now = buf("w_land", [P, 4, P]), buf("w_now", [P, 4, P])
        q_chan, k_chan, v_tok = buf("q_chan", [P, 2, N]), buf("k_chan", [P, 2, N]), buf("v_tok", [P, 2, T, P])
        neg_max, row_sum = buf("neg_max", [P, STEPS, 2]), buf("row_sum", [P, STEPS, 2])
        coef = buf("coef", [P, STEPS, 2])
        probs, probs_t = buf("probs", [P, P_RING, 2, N]), buf("probs_t", [P, 2, 2, T, P])
        heads_out, heads_out_t = buf("heads_out", [P, T, P]), buf("heads_out_t", [P, T, P])
        score_banks = [core.psum[:, 0:2, :], core.psum[:, 2:4, :]]
        pt_banks = core.psum[:, 4:6, :]
        pv_bank, free_bank = core.banks[6], core.banks[7]
        if causal:
            mask_f, mask = buf("mask_f", [P, P]), buf("mask", [P, P], BF16)
        if gates:
            w_gates, gate = buf("w_gates", [P, 2 * pairs]), buf("gate", [P, 2 * pairs, TILES])

        constants_loaded, mask_ready = sem("constants_loaded"), sem("mask_ready")
        gate_scores_ready, gate_ready = sem("gate_scores_ready"), sem("gate_ready")
        branch_zeroed = sem("branch_zeroed")
        w_loaded, w_ready, wo_ready = sem("w_loaded"), sem("w_ready"), sem("wo_ready")
        proj_ready, proj_copied = sem("proj_ready"), sem("proj_copied")
        scores_ready, max_ready, probs_ready = sem("scores_ready"), sem("max_ready"), sem("probs_ready")
        pt_ready, pt0_copied, pt1_copied = sem("pt_ready"), sem("pt0_copied"), sem("pt1_copied")
        pv_ready = sem("pv_ready")
        inverse_ready, coef_ready, normed = sem("inverse_ready"), sem("coef_ready"), sem("normed")
        ot_ready, ot_copied, out_ready, added = sem("ot_ready"), sem("ot_copied"), sem("out_ready"), sem("added")
        n_constants = 16 * (bool(causal) + bool(gates))

        def width(s):
            return (s % T + 1) * P if causal else N

        def run(engine, position):
            for n in range(EDGE):
                position(0, n, pairs * STEPS)
            with engine.Fori(0, pairs - 1) as pair:
                for n in range(EDGE, EDGE + STEPS):
                    position(pair, n, 2 * STEPS)
            for n in range(EDGE, STEPS + TAIL):
                position(pairs - 1, n, STEPS)

        def steps_at(n, lag, end):
            return [n - lag] if 0 <= n - lag < end else []

        def seqs_at(n, after, end):
            return [(n - after) // T] if (n - after) % T == 0 and 0 <= n - after < end else []

        def next_projection(n, end):
            seq = n // T + 1
            ahead = {1: (0,), 2: (1, 2)}.get(n % T, ())
            return [(seq, which) for which in ahead if seq * T < end]

        with core.stage() as block:
            @block.sync
            def _(sp):
                core.clear_spent(sp)
                sp.dma_start(w_land[:], dram[weights][0]).then_inc(w_loaded, 16)
                if causal:
                    sp.dma_start(mask_f[:], dram["causal_mask"]).then_inc(constants_loaded, 16)
                if gates:
                    sp.dma_start(w_gates[:], dram[gates]).then_inc(constants_loaded, 16)
                with sp.Fori(0, pairs - 1) as pair:
                    sp.wait_ge(wo_ready, pair + 1)
                    sp.dma_start(w_land[:], dram[weights][bass.ds(pair + 1, 1), :, :, :]).then_inc(w_loaded, 16)

            @block.gpsimd
            def _(pool):
                nc.gpsimd.memset(core.branch[:], 0.0).then_inc(branch_zeroed, 1)

            @block.tensor
            def _(pe):
                if gates:
                    pe.wait_ge(constants_loaded, n_constants)
                    for t in range(TILES):
                        tick = nc.tensor.matmul(pv_bank[:, t * 2 * pairs:(t + 1) * 2 * pairs],
                                                core.xn_chan[:, bass.ts(t, P)], w_gates[:])
                    tick.then_inc(gate_scores_ready, 1)
                if causal:
                    pe.wait_ge(mask_ready, 1)

                def project(pair, seq, which):
                    if which == 0:
                        at_least(pe, added, B * pair + (seq - 2))
                    at_least(pe, proj_copied, 3 * B * pair + (3 * seq + which))
                    if which == 0 and seq % B == 0:
                        pe.wait_ge(w_ready, pair + (seq // B + 1))
                    b = seq % B
                    if which < 2:
                        tick = nc.tensor.matmul(free_bank[:], w_now[:, which, :], core.xn_chan[:, bass.ts(b, N)])
                    else:
                        for t in range(T):
                            tick = nc.tensor.matmul(free_bank[:, bass.ts(t, P)],
                                                    core.xn_chan[:, bass.ts(b * T + t, P)], w_now[:, 2, :])
                    tick.then_inc(proj_ready, 1)

                def scores(pair, s):
                    seq, i = s // T, s % T
                    if i == 0:
                        pe.wait_ge(proj_copied, 3 * B * pair + (3 * seq + 3))
                    at_least(pe, probs_ready, 2 * STEPS * pair + 2 * (s - 1))
                    banks = score_banks[s % 2]
                    for h in range(2):
                        rows = slice(h * E, (h + 1) * E)
                        tick = nc.tensor.matmul(banks[:, h, 0:width(s)], q_chan[rows, seq % 2, bass.ts(i, P)],
                                                k_chan[rows, seq % 2, 0:width(s)], start=True, stop=not causal)
                    if causal:
                        for h in range(2):
                            tick = nc.tensor.matmul(banks[:, h, i * P:(i + 1) * P], core.identity_bf[:], mask[:],
                                                    start=False, stop=True)
                    tick.then_inc(scores_ready, 1)

                def transpose(pair, s):
                    pe.wait_ge(probs_ready, 2 * STEPS * pair + 2 * (s + 1))
                    at_least(pe, pt0_copied, STEPS * pair + s)
                    at_least(pe, pt1_copied, STEPS * pair + s)
                    for h in range(2):
                        for j in range(width(s) // P):
                            tick = nc.tensor.transpose(pt_banks[:, h, bass.ts(j, P)],
                                                       probs[:, s % P_RING, h, bass.ts(j, P)], core.identity[:])
                    tick.then_inc(pt_ready, 1)

                def product(pair, s):
                    seq, i = s // T, s % T
                    pe.wait_ge(pt0_copied, STEPS * pair + (s + 1))
                    pe.wait_ge(pt1_copied, STEPS * pair + (s + 1))
                    if i == 0:
                        at_least(pe, normed, B * pair + seq)
                    for h in range(2):
                        for j in range(width(s) // P):
                            tick = nc.tensor.matmul(pv_bank[:, i * P + h * E:i * P + (h + 1) * E],
                                                    probs_t[:, s % 2, h, j, :],
                                                    v_tok[:, seq % 2, j, h * E:(h + 1) * E],
                                                    start=(j == 0), stop=(j == width(s) // P - 1))
                    tick.then_inc(pv_ready, 1)

                def out_transpose(pair, seq, last):
                    pe.wait_ge(normed, B * pair + (seq + 1))
                    pe.wait_ge(proj_copied, 3 * B * pair + (3 * min(seq + 2, last // T - 1) + 3))
                    at_least(pe, added, B * pair + seq)
                    for t in range(T):
                        tick = nc.tensor.transpose(free_bank[:, bass.ts(t, P)], heads_out[:, t, :], core.identity[:])
                    tick.then_inc(ot_ready, 1)

                def out_product(pair, seq):
                    pe.wait_ge(ot_copied, B * pair + (seq + 1))
                    if seq % B == 0:
                        pe.wait_ge(wo_ready, pair + (seq // B + 1))
                    for t in range(T):
                        tick = nc.tensor.matmul(free_bank[:, bass.ts(t, P)], heads_out_t[:, t, :], w_now[:, 3, :])
                    tick.then_inc(out_ready, 1)

                def position(pair, n, end):
                    for s in steps_at(n, 0, end):
                        scores(pair, s)
                    ahead = next_projection(n, end)
                    for seq, which in ahead[:-1]:
                        project(pair, seq, which)
                    for s in steps_at(n, LAG_T, end):
                        transpose(pair, s)
                    for s in steps_at(n, LAG_PV, end):
                        product(pair, s)
                    for seq, which in ahead[-1:]:
                        project(pair, seq, which)
                    for seq in seqs_at(n, LAST_OF_SEQ + 1, end):
                        out_transpose(pair, seq, end)
                    for seq in seqs_at(n, LAST_OF_SEQ + 2, end):
                        out_product(pair, seq)

                if gates:
                    pe.wait_ge(gate_ready, 1)
                for which in range(3):
                    project(0, 0, which)
                run(pe, position)

            @block.scalar
            def _(act):
                if gates:
                    act.wait_ge(gate_scores_ready, 1)
                    nc.scalar.activation(gate[:].rearrange("p h t -> p t h"),
                                         pv_bank[:, 0:TILES * 2 * pairs].rearrange("p (t h) -> p t h", t=TILES),
                                         ACT.Sigmoid).then_inc(gate_ready, 1)

                def copy_projection(pair, seq, which):
                    act.wait_ge(proj_ready, 3 * B * pair + (3 * seq + which + 1))
                    if which == 0:
                        tick = nc.scalar.activation(q_chan[:, seq % 2, :], free_bank[:], ACT.Copy, scale=E ** -0.5)
                    elif which == 1:
                        tick = nc.scalar.copy(k_chan[:, seq % 2, :], free_bank[:])
                    else:
                        tick = nc.scalar.copy(v_tok[:, seq % 2, :, :], free_bank[:].rearrange("p (t c) -> p t c", t=T))
                    tick.then_inc(proj_copied, 1)

                def take_weights(pair, ahead):
                    act.wait_ge(w_loaded, 16 * pair + 16 * (ahead + 1))
                    nc.scalar.copy(w_now[:, 0:3, :], w_land[:, 0:3, :]).then_inc(w_ready, 1)

                def position(pair, n, end):
                    ahead = next_projection(n, end)
                    if n % STEPS == WO_AT and n < end:
                        at_least(act, out_ready, B * pair + B * (n // STEPS))
                        nc.scalar.copy(w_now[:, 3, :], w_land[:, 3, :]).then_inc(wo_ready, 1)
                    if n % STEPS == W_AT and (n // STEPS + 1) * STEPS < end:
                        take_weights(pair, n // STEPS + 1)
                    for seq, which in ahead[:-1]:
                        copy_projection(pair, seq, which)
                    for s in steps_at(n, LAG_T, end):
                        act.wait_ge(pt_ready, STEPS * pair + (s + 1))
                        at_least(act, pv_ready, STEPS * pair + (s - 1))
                        nc.scalar.copy(probs_t[:, s % 2, 1, 0:width(s) // P, :],
                                       pt_banks[:, 1, 0:width(s)].rearrange("p (j c) -> p j c", c=P)
                                       ).then_inc(pt1_copied, 1)
                    for s in steps_at(n, 0, end):
                        act.wait_ge(max_ready, STEPS * pair + (s + 1))
                        at_least(act, pt_ready, STEPS * pair + (s - P_RING + 1))
                        for h in range(2):
                            nc.scalar.activation(probs[:, s % P_RING, h, 0:width(s)],
                                                 score_banks[s % 2][:, h, 0:width(s)], ACT.Exp,
                                                 bias=neg_max[:, s % STEPS, h:h + 1],
                                                 accum_out=row_sum[:, s % STEPS, h:h + 1]).then_inc(probs_ready, 1)
                    for seq, which in ahead[-1:]:
                        copy_projection(pair, seq, which)
                    for seq in seqs_at(n, LAST_OF_SEQ + 1, end):
                        act.wait_ge(ot_ready, B * pair + (seq + 1))
                        at_least(act, out_ready, B * pair + seq)
                        nc.scalar.copy(heads_out_t[:], free_bank[:].rearrange("p (t c) -> p t c", t=T)
                                       ).then_inc(ot_copied, 1)

                take_weights(0, 0)
                for which in range(3):
                    copy_projection(0, 0, which)
                run(act, position)

            @block.vector
            def _(dve):
                if causal:
                    dve.wait_ge(constants_loaded, n_constants)
                    nc.vector.tensor_copy(mask[:], mask_f[:]).then_inc(mask_ready, 1)

                def normalize(pair, seq):
                    b = seq % B
                    steps = slice(b * T, (b + 1) * T)
                    dve.wait_ge(probs_ready, 2 * STEPS * pair + 2 * T * (seq + 1))
                    nc.vector.reciprocal(coef[:, steps, :], row_sum[:, steps, :]).then_inc(inverse_ready, 1)
                    dve.wait_ge(inverse_ready, B * pair + (seq + 1))
                    if gates:
                        nc.vector.tensor_tensor(coef[:, steps, :], coef[:, steps, :],
                                                gate[:, bass.ds(pair * 2 + 2 * (seq // B), 2), b * T:(b + 1) * T].rearrange(
                                                    "p h t -> p t h"), ALU.mult).then_inc(coef_ready, 1)
                        dve.wait_ge(coef_ready, B * pair + (seq + 1))
                    dve.wait_ge(pv_ready, STEPS * pair + T * (seq + 1))
                    at_least(dve, ot_ready, B * pair + seq)
                    nc.vector.tensor_tensor(
                        heads_out[:].rearrange("p t (h c) -> p t h c", h=2),
                        pv_bank[:].rearrange("p (t h c) -> p t h c", t=T, h=2),
                        coef[:, steps, :].unsqueeze(3).broadcast_to([P, T, 2, E]), ALU.mult).then_inc(normed, 1)

                def position(pair, n, end):
                    for seq in seqs_at(n, LAST_OF_SEQ + 3, end):
                        b = seq % B
                        dve.wait_ge(out_ready, B * pair + (seq + 1))
                        at_least(dve, added, B * pair + seq)
                        acc = core.branch[:, b * T:(b + 1) * T, :]
                        nc.vector.tensor_tensor(acc, acc, free_bank[:].rearrange("p (t c) -> p t c", t=T),
                                                ALU.add).then_inc(added, 1)
                    for s in steps_at(n, 0, end):
                        dve.wait_ge(scores_ready, STEPS * pair + (s + 1))
                        nc.vector.tensor_reduce(neg_max[:, s % STEPS, :], score_banks[s % 2][:, :, 0:width(s)],
                                                AX_X, ALU.max, negate=True).then_inc(max_ready, 1)
                    for s in steps_at(n, LAG_T, end):
                        dve.wait_ge(pt_ready, STEPS * pair + (s + 1))
                        at_least(dve, pv_ready, STEPS * pair + (s - 1))
                        nc.vector.tensor_copy(probs_t[:, s % 2, 0, 0:width(s) // P, :],
                                              pt_banks[:, 0, 0:width(s)].rearrange("p (j c) -> p j c", c=P)
                                              ).then_inc(pt0_copied, 1)
                    for seq in seqs_at(n, LAST_OF_SEQ, end):
                        normalize(pair, seq)

                if gates:
                    dve.wait_ge(gate_ready, 1)
                dve.wait_ge(branch_zeroed, 1)
                run(dve, position)


def two_of_eight(core, name, weights, gate):
    nc, dram = core.nc, core.dram
    X = 8
    HALF = 2
    STEPS = B * HALF
    LAG = 2
    with ExitStack() as st:
        def buf(n, shape, dtype=F32):
            return core.sbuf(st, f"{name}_{n}", shape, dtype)

        def sem(n):
            return core.sem(f"{name}_{n}")

        w_gate, numbers = buf("w_gate", [P, X]), buf("numbers", [P, X])
        score, top = buf("score", [P, TILES, X]), buf("top", [P, TILES, X])
        extreme = buf("extreme", [P, TILES])
        places, places_f = buf("places", [P, TILES, X], U32), buf("places_f", [P, TILES, X])
        chosen, chosen2 = buf("chosen", [P, TILES, X]), buf("chosen2", [P, TILES, X])
        w = [buf(f"w{u}", [P, 3, 2 * P]) for u in range(2)]
        gated, hidden = buf("gated", [P, 2, N]), buf("hidden", [P, 4, N])
        gate_bank = core.banks[6]
        w1_banks, w3_banks, y_banks = core.banks[0:2], core.banks[2:4], core.banks[4:6]

        loaded, logits_ready, zeroed = sem("loaded"), sem("logits_ready"), sem("zeroed")
        softmax_step, exp_ready, chosen_ready = sem("softmax_step"), sem("exp_ready"), sem("chosen_ready")
        w_loaded = [sem(f"w_loaded{u}") for u in range(2)]
        w1_ready, w3_ready, silu_ready = sem("w1_ready"), sem("w3_ready"), sem("silu_ready")
        hidden_ready, added = sem("hidden_ready"), sem("added")
        y_ready = [sem(f"y_ready{u}") for u in range(2)]

        with core.stage() as block:
            @block.sync
            def _(sp):
                core.clear_spent(sp)
                sp.dma_start(w_gate[:], dram[gate]).then_inc(loaded, 16)
                sp.dma_start(numbers[:], dram["numbers8"].partition_broadcast(P)).then_inc(loaded, 16)
                with sp.Fori(0, X // 2) as turn:
                    for u in range(2):
                        sp.wait_ge(y_ready[u], CREDIT + B * turn)
                        sp.dma_start(w[u][:], dram[weights][bass.ds(turn * 2 + u, 1), :, :, :]).then_inc(w_loaded[u], 16)

            @block.gpsimd
            def _(pool):
                nc.gpsimd.memset(core.branch[:], 0.0).then_inc(zeroed, 1)

            @block.tensor
            def _(pe):
                pe.wait_ge(loaded, 32)
                for t in range(TILES):
                    tick = nc.tensor.matmul(gate_bank[:, bass.ts(t, X)], core.xn_chan[:, bass.ts(t, P)], w_gate[:])
                tick.then_inc(logits_ready, 1)
                give_credit(pe, *y_ready)
                with pe.Fori(0, X // 2) as turn:
                    for u in range(2):
                        pe.wait_ge(w_loaded[u], 16 * turn + 16)
                        for at in range(STEPS + LAG):
                            if at < STEPS:
                                b, half = at // HALF, at % HALF
                                n = STEPS * u + at
                                x = core.xn_chan[:, bass.ts(b, N)]
                                if n >= 2:
                                    pe.wait_ge(silu_ready, 2 * STEPS * turn + (n - 1))
                                nc.tensor.matmul(w1_banks[at % 2][:], w[u][:, 0, bass.ts(half, P)], x
                                                 ).then_inc(w1_ready, 1)
                                if n >= 2:
                                    pe.wait_ge(hidden_ready, 2 * STEPS * turn + (n - 1))
                                nc.tensor.matmul(w3_banks[at % 2][:], w[u][:, 1, bass.ts(half, P)], x
                                                 ).then_inc(w3_ready, 1)
                            if at >= LAG and at % 2 == 1:
                                b = (at - LAG) // HALF
                                m = B * u + b
                                pe.wait_ge(hidden_ready, 2 * STEPS * turn + (STEPS * u + 2 * b + 2))
                                if m >= 2:
                                    pe.wait_ge(added, CREDIT + 2 * B * turn + (m - 1))
                                for t in range(T):
                                    for half in range(HALF):
                                        tick = nc.tensor.matmul(
                                            y_banks[b % 2][:, bass.ts(t, P)],
                                            hidden[:, 2 * (b % 2) + half, bass.ts(t, P)],
                                            w[u][:, 2, bass.ts(half, P)], start=(half == 0), stop=(half == 1))
                                tick.then_inc(y_ready[u], 1)

            @block.scalar
            def _(act):
                act.wait_ge(softmax_step, 2)
                nc.scalar.activation(score[:], score[:], ACT.Exp).then_inc(exp_ready, 1)
                with act.Fori(0, X // 2) as turn:
                    for n in range(2 * STEPS):
                        act.wait_ge(w1_ready, 2 * STEPS * turn + (n + 1))
                        if n >= 2:
                            act.wait_ge(hidden_ready, 2 * STEPS * turn + (n - 1))
                        nc.scalar.activation(gated[:, n % 2, :], w1_banks[n % 2][:], ACT.Silu).then_inc(silu_ready, 1)

            @block.vector
            def _(dve):
                dve.wait_ge(logits_ready, 1)
                logits = gate_bank[:, 0:TILES * X].rearrange("p (t e) -> p t e", e=X)
                nc.vector.tensor_reduce(extreme[:], logits, AX_X, ALU.max).then_inc(softmax_step, 1)
                dve.wait_ge(softmax_step, 1)
                nc.vector.tensor_tensor(score[:], logits, extreme[:].unsqueeze(2).broadcast_to([P, TILES, X]),
                                        ALU.subtract).then_inc(softmax_step, 1)
                dve.wait_ge(exp_ready, 1)
                nc.vector.tensor_reduce(extreme[:], score[:], AX_X, ALU.add).then_inc(softmax_step, 1)
                dve.wait_ge(softmax_step, 3)
                nc.vector.reciprocal(extreme[:], extreme[:]).then_inc(softmax_step, 1)
                dve.wait_ge(softmax_step, 4)
                nc.vector.tensor_tensor(score[:], score[:], extreme[:].unsqueeze(2).broadcast_to([P, TILES, X]),
                                        ALU.mult).then_inc(softmax_step, 1)
                dve.wait_ge(softmax_step, 5)
                for t in range(TILES):
                    nc.vector.max(top[:, t, :], score[:, t, :]).then_inc(chosen_ready, 1)
                for t in range(TILES):
                    dve.wait_ge(chosen_ready, t + 1)
                    tick = nc.vector.max_index(places[:, t, :], top[:, t, :], score[:, t, :])
                tick.then_inc(softmax_step, 1)
                dve.wait_ge(softmax_step, 6)
                nc.vector.tensor_copy(places_f[:], places[:]).then_inc(softmax_step, 1)
                dve.wait_ge(softmax_step, 7)
                dve.wait_ge(loaded, 32)
                number = numbers[:].unsqueeze(1).broadcast_to([P, TILES, X])
                for k, c in enumerate((chosen, chosen2)):
                    nc.vector.tensor_tensor(c[:], number, places_f[:, :, k:k + 1].broadcast_to([P, TILES, X]),
                                            ALU.is_equal).then_inc(softmax_step, 1)
                dve.wait_ge(softmax_step, 9)
                nc.vector.tensor_tensor(chosen[:], chosen[:], chosen2[:], ALU.add).then_inc(softmax_step, 1)
                dve.wait_ge(softmax_step, 10)
                nc.vector.tensor_tensor(score[:], score[:], chosen[:], ALU.mult).then_inc(softmax_step, 1)
                dve.wait_ge(softmax_step, 11)
                dve.wait_ge(zeroed, 1)
                give_credit(dve, added)
                with dve.Fori(0, X // 2) as turn:
                    for u in range(2):
                        for at in range(STEPS + LAG):
                            n = STEPS * u + at
                            if at < STEPS:
                                dve.wait_ge(silu_ready, 2 * STEPS * turn + (n + 1))
                                dve.wait_ge(w3_ready, 2 * STEPS * turn + (n + 1))
                                if n >= 4:
                                    m = (n - 4) // HALF
                                    dve.wait_ge(y_ready[m // B], CREDIT + B * turn + (m % B + 1))
                                nc.vector.tensor_tensor(hidden[:, at % 4, :], gated[:, n % 2, :], w3_banks[at % 2][:],
                                                        ALU.mult).then_inc(hidden_ready, 1)
                            if at >= LAG and at % 2 == 1:
                                b = (at - LAG) // HALF
                                m = B * u + b
                                dve.wait_ge(y_ready[u], CREDIT + B * turn + (b + 1))
                                for t in range(T):
                                    acc = core.branch[:, b * T + t, :]
                                    tick = nc.vector.scalar_tensor_tensor(
                                        acc, y_banks[b % 2][:, bass.ts(t, P)],
                                        score[:, b * T + t, bass.ds(turn * 2 + u, 1)], acc, ALU.mult, ALU.add)
                                tick.then_inc(added, 1)
                                if b == B - 1:
                                    dve.wait_ge(added, CREDIT + 2 * B * turn + (m + 1))


def one_of_many(core, name):
    nc, dram = core.nc, core.dram
    X, GROUPS = 32, 8
    with ExitStack() as st:
        def buf(n, shape, dtype=F32):
            return core.sbuf(st, f"{name}_{n}", shape, dtype)

        def sem(n):
            return core.sem(f"{name}_{n}")

        w_router, router_b, numbers = buf("w_router", [P, X]), buf("router_b", [P, X]), buf("numbers", [P, X])
        w1, b1 = buf("w1", [P, GROUPS, P]), buf("b1", [P, GROUPS])
        w2, b2 = buf("w2", [P, GROUPS, D]), buf("b2", [X, D])
        spread_f, spread = buf("spread_f", [X, GROUPS, P]), buf("spread", [X, GROUPS, P], BF16)
        logits, top = buf("logits", [P, TILES, X]), buf("top", [P, TILES, 8])
        places, places_f = buf("places", [P, TILES, 8], U32), buf("places_f", [P, TILES])
        onehot, onehot_t = buf("onehot", [P, TILES, X]), buf("onehot_t", [X, TOKENS])
        onehot_bf = buf("onehot_bf", [X, TOKENS], BF16)
        relued, hidden = buf("relued", [P, 2, N]), buf("hidden", [P, GROUPS, N])
        summed = buf("summed", [P, N])
        h_banks, mask_banks, y_bank = core.banks[0:2], core.banks[2:4], core.banks[4]

        loaded, logits_ready, step = sem("loaded"), sem("logits_ready"), sem("step")
        top_ready, onehot_ready, t_ready, t_copied = (
            sem("top_ready"), sem("onehot_ready"), sem("t_ready"), sem("t_copied"))
        bias_ready, bias_copied, spread_ready = sem("bias_ready"), sem("bias_copied"), sem("spread_ready")
        h_ready, mask_ready, relu_ready, hidden_ready = (
            sem("h_ready"), sem("mask_ready"), sem("relu_ready"), sem("hidden_ready"))
        y_ready, summed_ready, finished = sem("y_ready"), sem("summed_ready"), sem("finished")
        names = [(w_router, "w_router", False), (router_b, "router_b", True), (numbers, "numbers32", True),
                 (w1, "w1_many", False), (b1, "b1_many", False), (w2, "w2_many", False), (b2, "b2_many", False),
                 (spread_f, "spread", False)]

        with core.stage() as block:
            @block.sync
            def _(sp):
                core.clear_spent(sp)
                for place, source, every_partition in names:
                    src = dram[source].partition_broadcast(P) if every_partition else dram[source]
                    sp.dma_start(place[:], src).then_inc(loaded, 16)

            @block.tensor
            def _(pe):
                pe.wait_ge(loaded, 16 * len(names))
                for t in range(TILES):
                    tick = nc.tensor.matmul(y_bank[:, bass.ts(t, X)], core.xn_chan[:, bass.ts(t, P)], w_router[:])
                tick.then_inc(logits_ready, 1)
                pe.wait_ge(onehot_ready, 1)
                for b in range(B):
                    for t in range(T):
                        tick = nc.tensor.transpose(core.banks[b][0:X, bass.ts(t, P)], onehot[:, b * T + t, :],
                                                   core.identity[:])
                    tick.then_inc(t_ready, 1)
                for b in range(B):
                    pe.wait_ge(t_copied, b + 1)
                    for t in range(T):
                        tick = nc.tensor.matmul(core.banks[b + 4][:, bass.ts(t, P)],
                                                onehot_t[:, bass.ts(b * T + t, P)], b2[:])
                    tick.then_inc(bias_ready, 1)
                pe.wait_ge(t_copied, B + 1)
                pe.wait_ge(spread_ready, 1)
                pe.wait_ge(bias_copied, B)
                with pe.Fori(0, B) as b:
                    x = core.xn_chan[:, bass.ts(b, N)]
                    for g in range(GROUPS):
                        if g >= 2:
                            pe.wait_ge(relu_ready, GROUPS * b + (g - 1))
                            pe.wait_ge(hidden_ready, GROUPS * b + (g - 1))
                        nc.tensor.matmul(h_banks[g % 2][:], w1[:, g, :], x).then_inc(h_ready, 1)
                        nc.tensor.matmul(mask_banks[g % 2][:], spread[:, g, :], onehot_bf[:, bass.ts(b, N)]
                                         ).then_inc(mask_ready, 1)
                    pe.wait_ge(hidden_ready, GROUPS * b + GROUPS)
                    pe.wait_ge(summed_ready, CREDIT + b)
                    for t in range(T):
                        for g in range(GROUPS):
                            tick = nc.tensor.matmul(y_bank[:, bass.ts(t, P)], hidden[:, g, bass.ts(t, P)], w2[:, g, :],
                                                    start=(g == 0), stop=(g == GROUPS - 1))
                    tick.then_inc(y_ready, 1)

            @block.scalar
            def _(act):
                act.wait_ge(loaded, 16 * len(names))
                nc.scalar.copy(spread[:], spread_f[:]).then_inc(spread_ready, 1)
                for b in range(B):
                    act.wait_ge(bias_ready, b + 1)
                    nc.scalar.copy(core.branch[:, bass.ts(b, T), :],
                                   core.banks[b + 4][:].rearrange("p (t c) -> p t c", t=T)).then_inc(bias_copied, 1)
                with act.Fori(0, B) as b:
                    for g in range(GROUPS):
                        act.wait_ge(h_ready, GROUPS * b + (g + 1))
                        if g >= 2:
                            act.wait_ge(hidden_ready, GROUPS * b + (g - 1))
                        nc.scalar.activation(relued[:, g % 2, :], h_banks[g % 2][:], ACT.Relu, bias=b1[:, g:g + 1]
                                             ).then_inc(relu_ready, 1)
                    act.wait_ge(summed_ready, CREDIT + b + 1)
                    nc.scalar.activation(core.branch[:, bass.ts(b, T), :], summed[:].rearrange("p (t c) -> p t c", t=T),
                                         ACT.Relu).then_inc(finished, 1)

            @block.vector
            def _(dve):
                dve.wait_ge(loaded, 16 * len(names))
                dve.wait_ge(logits_ready, 1)
                nc.vector.tensor_tensor(logits[:], y_bank[:].rearrange("p (t e) -> p t e", e=X),
                                        router_b[:].unsqueeze(1).broadcast_to([P, TILES, X]), ALU.add).then_inc(step, 1)
                dve.wait_ge(step, 1)
                for t in range(TILES):
                    nc.vector.max(top[:, t, :], logits[:, t, :]).then_inc(top_ready, 1)
                for t in range(TILES):
                    dve.wait_ge(top_ready, t + 1)
                    tick = nc.vector.max_index(places[:, t, :], top[:, t, :], logits[:, t, :])
                tick.then_inc(step, 1)
                dve.wait_ge(step, 2)
                nc.vector.tensor_copy(places_f[:], places[:, :, 0]).then_inc(step, 1)
                dve.wait_ge(step, 3)
                nc.vector.tensor_tensor(onehot[:], numbers[:].unsqueeze(1).broadcast_to([P, TILES, X]),
                                        places_f[:].unsqueeze(2).broadcast_to([P, TILES, X]),
                                        ALU.is_equal).then_inc(onehot_ready, 1)
                for b in range(B):
                    dve.wait_ge(t_ready, b + 1)
                    nc.vector.tensor_copy(onehot_t[:, bass.ts(b, N)], core.banks[b][0:X, :]).then_inc(t_copied, 1)
                dve.wait_ge(t_copied, B)
                nc.vector.tensor_copy(onehot_bf[:], onehot_t[:]).then_inc(t_copied, 1)
                dve.wait_ge(bias_copied, B)
                give_credit(dve, summed_ready)
                with dve.Fori(0, B) as b:
                    for g in range(GROUPS):
                        dve.wait_ge(relu_ready, GROUPS * b + (g + 1))
                        dve.wait_ge(mask_ready, GROUPS * b + (g + 1))
                        nc.vector.tensor_tensor(hidden[:, g, :], relued[:, g % 2, :], mask_banks[g % 2][:],
                                                ALU.mult).then_inc(hidden_ready, 1)
                    dve.wait_ge(y_ready, b + 1)
                    nc.vector.tensor_tensor(summed[:].rearrange("p (t c) -> p t c", t=T),
                                            y_bank[:].rearrange("p (t c) -> p t c", t=T),
                                            core.branch[:, bass.ts(b, T), :], ALU.add).then_inc(summed_ready, 1)


def linear_attention(core, name):
    nc, dram = core.nc, core.dram
    PAIRS = D // 2
    EPS_RMS, EPS_DEN = 1.1920929e-07, 1e-06
    with ExitStack() as st:
        def buf(n, shape, dtype=F32):
            return core.sbuf(st, f"{name}_{n}", shape, dtype)

        def sem(n):
            return core.sem(f"{name}_{n}")

        w_qkv, b_qkv = buf("w_qkv", [P, 3 * D]), buf("b_qkv", [P, 3 * D])
        w_out, b_out, g_out = buf("w_out", [P, D]), buf("b_out", [P, D]), buf("g_out", [P, D])
        g_qk = buf("g_qk", [P, 2, D])
        cos, sin, same_head = buf("cos", [P, T, PAIRS]), buf("sin", [P, T, PAIRS]), buf("same_head", [P, D])
        power = buf("power", [P, 2 * T])
        x_now = buf("x_now", [P, N])
        qk, v = buf("qk", [P, T, 2, D]), buf("v", [P, T, D + 1])
        squares, qk_rms, out_rms = buf("squares", [P, 2, D]), buf("qk_rms", [P, 2 * T]), buf("out_rms", [P, T])
        turned = buf("turned", [P, T, 2, D])
        product = [buf(f"product{i}", [P, T, 2, PAIRS]) for i in range(4)]
        feature, feature_t = buf("feature", [P, T, 2, D]), buf("feature_t", [P, T, P])
        vk = buf("vk", [P, 2, D])
        k_sum = buf("k_sum", [P, 1])
        inverse, attn, attn_t = buf("inverse", [P, T, D]), buf("attn", [P, T, D]), buf("attn_t", [P, T, P])
        projected = buf("projected", [P, T, D])
        qkv_banks, t_bank, vk_bank, res_banks, out_bank = (
            core.banks[0:4], core.banks[4], core.banks[5], core.banks[6:8], core.banks[5])

        loads = [(w_qkv[:], "w_qkv2", False), (b_qkv[:], "b_qkv2", True), (w_out[:], "w_out2", False),
                 (b_out[:], "b_out2", True), (g_out[:], "g_out2", True), (g_qk[:, 0, :], "g_q2", True), (g_qk[:, 1, :], "g_k2", True),
                 (cos[:], "cos2", False), (sin[:], "sin2", False), (same_head[:], "same_head", False)]
        FIRST = 2
        first_loaded, loaded = sem("first_loaded"), sem("loaded")
        constants_ready, x_ready = sem("constants_ready"), sem("x_ready")
        qkv_ready, qk_ready, v_ready, squares_ready = sem("qkv_ready"), sem("qk_ready"), sem("v_ready"), sem("squares_ready")
        mean_ready, rms_ready, scaled = sem("mean_ready"), sem("rms_ready"), sem("scaled")
        products_ready, turned_ready, feature_ready = sem("products_ready"), sem("turned_ready"), sem("feature_ready")
        vk_ready, vk_masked, ft_ready, ft_copied = sem("vk_ready"), sem("vk_masked"), sem("ft_ready"), sem("ft_copied")
        res_ready, inverse_step, attn_ready = sem("res_ready"), sem("inverse_step"), sem("attn_ready")
        at_ready, at_copied, out_ready, projected_ready = (
            sem("at_ready"), sem("at_copied"), sem("out_ready"), sem("projected_ready"))
        out_squares, out_mean, out_rms_ready, branch_ready = (
            sem("out_squares"), sem("out_mean"), sem("out_rms_ready"), sem("branch_ready"))

        with core.stage() as block:
            @block.sync
            def _(sp):
                core.clear_spent(sp)
                for n, (place, source, every_partition) in enumerate(loads):
                    src = dram[source].partition_broadcast(P) if every_partition else dram[source]
                    sp.dma_start(place, src).then_inc(first_loaded if n < FIRST else loaded, 16)

            def turns(engine, front, turn, back):
                front(0)
                turn(0)
                with engine.Fori(1, B - 1) as b:
                    turn(b)
                back(B - 1)

            @block.gpsimd
            def _(pool):
                nc.gpsimd.memset(power[:], -0.5).then_inc(constants_ready, 1)
                nc.gpsimd.memset(v[:, :, D:D + 1], 1.0).then_inc(constants_ready, 1)
                pool.wait_ge(constants_ready, 2)

                def front(b):
                    pool.wait_ge(mean_ready, b + 1)
                    nc.gpsimd.tensor_tensor(qk_rms[:], qk_rms[:], power[:], ALU.pow).then_inc(rms_ready, 1)

                def back(b):
                    pool.wait_ge(out_mean, b + 1)
                    nc.gpsimd.tensor_tensor(out_rms[:], out_rms[:], power[:, 0:T], ALU.pow).then_inc(out_rms_ready, 1)

                def turn(b):
                    front(b + 1)
                    back(b)

                turns(pool, front, turn, back)

            @block.tensor
            def _(pe):
                def project(b):
                    pe.wait_ge(x_ready, b + 1)
                    at_least(pe, v_ready, b * T)
                    for t in range(T):
                        nc.tensor.matmul(qkv_banks[t][:, 0:3 * D], x_now[:, bass.ts(t, P)], w_qkv[:]
                                         ).then_inc(qkv_ready, 1)

                def sum_keys(b):
                    pe.wait_ge(v_ready, b * T + T)
                    pe.wait_ge(feature_ready, b + 1)
                    at_least(pe, projected_ready, b)
                    for t in range(T):
                        tick = nc.tensor.matmul(vk_bank[:, 0:D + 1], feature[:, t, 1, :], v[:, t, :],
                                                start=(t == 0), stop=(t == T - 1))
                    tick.then_inc(vk_ready, 1)
                    at_least(pe, at_copied, b)
                    for t in range(T):
                        tick = nc.tensor.transpose(t_bank[:, bass.ts(t, P)], feature[:, t, 0, :], core.identity[:])
                    tick.then_inc(ft_ready, 1)

                def attend(b):
                    pe.wait_ge(ft_copied, b + 1)
                    pe.wait_ge(vk_masked, b * 3 + 3)
                    for t in range(T):
                        tick = nc.tensor.matmul(res_banks[t // 2][:, bass.ts(t % 2, 2 * D)], feature_t[:, t, :],
                                                vk[:].rearrange("p a d -> p (a d)"))
                    tick.then_inc(res_ready, 1)
                    pe.wait_ge(attn_ready, b * 2 + 2)
                    for t in range(T):
                        tick = nc.tensor.transpose(t_bank[:, bass.ts(t, P)], attn[:, t, :], core.identity[:])
                    tick.then_inc(at_ready, 1)
                    pe.wait_ge(at_copied, b + 1)
                    for t in range(T):
                        tick = nc.tensor.matmul(out_bank[:, bass.ts(t, P)], attn_t[:, t, :], w_out[:])
                    tick.then_inc(out_ready, 1)

                def turn(b):
                    sum_keys(b)
                    project(b + 1)
                    if isinstance(b, int):
                        pe.wait_ge(loaded, 16 * (len(loads) - FIRST))
                    attend(b)

                def back(b):
                    sum_keys(b)
                    attend(b)

                pe.wait_ge(first_loaded, 16 * FIRST)
                pe.wait_ge(constants_ready, 2)
                turns(pe, project, turn, back)

            @block.scalar
            def _(act):
                def take_x(b):
                    at_least(act, qkv_ready, b * T)
                    nc.scalar.copy(x_now[:], core.xn_chan[:, bass.ts(b, N)]).then_inc(x_ready, 1)

                def square_qk(b):
                    for t in range(T):
                        act.wait_ge(qk_ready, b * T + (t + 1))
                        for which in range(2):
                            at_least(act, squares_ready, b * (2 * T) + (2 * t + which))
                            nc.scalar.activation(squares[:, 0, :], qk[:, t, which, :], ACT.Square,
                                                 accum_out=qk_rms[:, 2 * t + which:2 * t + which + 1]
                                                 ).then_inc(squares_ready, 1)

                def relu(b):
                    act.wait_ge(turned_ready, b * 2 + 2)
                    at_least(act, ft_ready, b)
                    nc.scalar.activation(feature[:], turned[:], ACT.Relu).then_inc(feature_ready, 1)

                def copy_ft(b):
                    act.wait_ge(ft_ready, b + 1)
                    at_least(act, res_ready, b)
                    nc.scalar.copy(feature_t[:], t_bank[:].rearrange("p (t c) -> p t c", t=T)).then_inc(ft_copied, 1)

                def copy_at(b):
                    act.wait_ge(at_ready, b + 1)
                    nc.scalar.copy(attn_t[:], t_bank[:].rearrange("p (t c) -> p t c", t=T)).then_inc(at_copied, 1)

                def square_out(b):
                    act.wait_ge(projected_ready, b + 1)
                    at_least(act, branch_ready, b)
                    for t in range(T):
                        at_least(act, out_squares, b * T + t)
                        nc.scalar.activation(squares[:, 1, :], projected[:, t, :], ACT.Square,
                                             accum_out=out_rms[:, t:t + 1]).then_inc(out_squares, 1)

                def front(b):
                    take_x(b)
                    square_qk(b)
                    relu(b)

                def turn(b):
                    take_x(b + 1)
                    copy_ft(b)
                    square_qk(b + 1)
                    copy_at(b)
                    square_out(b)
                    relu(b + 1)

                def back(b):
                    copy_ft(b)
                    copy_at(b)
                    square_out(b)

                turns(act, front, turn, back)

            @block.vector
            def _(dve):
                def add_bias(b):
                    for t in range(T):
                        dve.wait_ge(qkv_ready, b * T + (t + 1))
                        nc.vector.tensor_tensor(qk[:, t, :, :].rearrange("p a d -> p (a d)"), qkv_banks[t][:, 0:2 * D],
                                                b_qkv[:, 0:2 * D], ALU.add).then_inc(qk_ready, 1)
                        at_least(dve, vk_ready, b)
                        nc.vector.tensor_tensor(v[:, t, 0:D], qkv_banks[t][:, 2 * D:3 * D], b_qkv[:, 2 * D:3 * D],
                                                ALU.add).then_inc(v_ready, 1)

                def take_mean(b):
                    dve.wait_ge(squares_ready, b * (2 * T) + 2 * T)
                    nc.vector.tensor_scalar(qk_rms[:], qk_rms[:], 1.0 / D, EPS_RMS, ALU.mult, ALU.add
                                            ).then_inc(mean_ready, 1)

                def scale(b):
                    dve.wait_ge(rms_ready, b + 1)
                    for t in range(T):
                        for which in range(2):
                            i = 2 * t + which
                            tick = nc.vector.scalar_tensor_tensor(qk[:, t, which, :], qk[:, t, which, :],
                                                                  qk_rms[:, i:i + 1], g_qk[:, which, :],
                                                                  ALU.mult, ALU.mult)
                    tick.then_inc(scaled, 1)

                def rotate(b):
                    dve.wait_ge(scaled, b + 1)
                    at_least(dve, feature_ready, b)
                    pairs = qk[:].rearrange("p t a (m two) -> p t a m two", two=2)
                    table = [x[:].unsqueeze(2).broadcast_to([P, T, 2, PAIRS]) for x in (cos, sin)]
                    for i, (which, tab) in enumerate(((0, 0), (1, 1), (0, 1), (1, 0))):
                        nc.vector.tensor_tensor(product[i][:], pairs[:, :, :, :, which], table[tab], ALU.mult
                                                ).then_inc(products_ready, 1)
                    out = turned[:].rearrange("p t a (m two) -> p t a m two", two=2)
                    dve.wait_ge(products_ready, b * 4 + 2)
                    nc.vector.tensor_tensor(out[:, :, :, :, 0], product[0][:], product[1][:], ALU.subtract
                                            ).then_inc(turned_ready, 1)
                    dve.wait_ge(products_ready, b * 4 + 4)
                    nc.vector.tensor_tensor(out[:, :, :, :, 1], product[2][:], product[3][:], ALU.add
                                            ).then_inc(turned_ready, 1)

                def mask(b):
                    dve.wait_ge(vk_ready, b + 1)
                    nc.vector.tensor_tensor(vk[:, 0, :], vk_bank[:, 0:D], same_head[:], ALU.mult).then_inc(vk_masked, 1)
                    nc.vector.tensor_copy(k_sum[:], vk_bank[:, D:D + 1]).then_inc(vk_masked, 1)
                    dve.wait_ge(vk_masked, b * 3 + 2)
                    nc.vector.tensor_scalar(vk[:, 1, :], same_head[:], k_sum[:], None, ALU.mult).then_inc(vk_masked, 1)

                def divide(b):
                    dve.wait_ge(res_ready, b + 1)
                    for half in range(2):
                        res = res_banks[half][:].rearrange("p (t a d) -> p t a d", t=2, a=2)
                        inv = inverse[:, 2 * half:2 * half + 2, :]
                        nc.vector.tensor_scalar(inv, res[:, :, 1, :], EPS_DEN, None, ALU.add).then_inc(inverse_step, 1)
                        dve.wait_ge(inverse_step, b * 4 + (2 * half + 1))
                        nc.vector.reciprocal(inv, inv).then_inc(inverse_step, 1)
                        dve.wait_ge(inverse_step, b * 4 + (2 * half + 2))
                        nc.vector.tensor_tensor(attn[:, 2 * half:2 * half + 2, :], res[:, :, 0, :], inv, ALU.mult
                                                ).then_inc(attn_ready, 1)

                def take_out(b):
                    dve.wait_ge(out_ready, b + 1)
                    nc.vector.tensor_tensor(projected[:], out_bank[:].rearrange("p (t c) -> p t c", t=T),
                                            b_out[:].unsqueeze(1).broadcast_to([P, T, D]), ALU.add
                                            ).then_inc(projected_ready, 1)

                def take_out_mean(b):
                    dve.wait_ge(out_squares, b * T + T)
                    nc.vector.tensor_scalar(out_rms[:], out_rms[:], 1.0 / D, EPS_RMS, ALU.mult, ALU.add
                                            ).then_inc(out_mean, 1)

                def finish(b):
                    dve.wait_ge(out_rms_ready, b + 1)
                    for t in range(T):
                        tick = nc.vector.scalar_tensor_tensor(core.branch[:, bass.ds(b * T + t, 1), :].rearrange(
                            "p o d -> p (o d)"), projected[:, t, :], out_rms[:, t:t + 1], g_out[:], ALU.mult, ALU.mult)
                    tick.then_inc(branch_ready, 1)

                def front(b):
                    add_bias(b)
                    dve.wait_ge(loaded, 16 * (len(loads) - FIRST))
                    take_mean(b)
                    scale(b)
                    rotate(b)

                def turn(b):
                    mask(b)
                    add_bias(b + 1)
                    divide(b)
                    take_mean(b + 1)
                    take_out(b)
                    scale(b + 1)
                    take_out_mean(b)
                    rotate(b + 1)
                    finish(b)

                def back(b):
                    mask(b)
                    divide(b)
                    take_out(b)
                    take_out_mean(b)
                    finish(b)

                dve.wait_ge(first_loaded, 16 * FIRST)
                dve.wait_ge(constants_ready, 2)
                turns(dve, front, turn, back)


def token_mix(core, name):
    nc, dram = core.nc, core.dram
    PLACES = 2
    with ExitStack() as st:
        def buf(n, shape, dtype=F32):
            return core.sbuf(st, f"{name}_{n}", shape, dtype)

        def sem(n):
            return core.sem(f"{name}_{n}")

        w_r, w_k, w_v, mu = buf("w_r", [P, D]), buf("w_k", [P, D]), buf("w_v", [P, D]), buf("mu", [P, 2])
        x_now = buf("x_now", [P, PLACES, 1 + N])
        change, x_r, x_k = buf("change", [P, PLACES, N]), buf("x_r", [P, PLACES, N]), buf("x_k", [P, PLACES, N])
        relued, squared = buf("relued", [P, PLACES, N]), buf("squared", [P, PLACES, N])
        receptance = buf("receptance", [P, PLACES, N])
        loads = [(w_r, "w_r"), (w_k, "w_k"), (w_v, "w_v"), (mu, "mu")]
        loaded, zeroed, x_ready, change_ready = sem("loaded"), sem("zeroed"), sem("x_ready"), sem("change_ready")
        mixed, k_ready, r_ready, relu_ready = sem("mixed"), sem("k_ready"), sem("r_ready"), sem("relu_ready")
        squared_ready, sigmoid_ready, v_ready, done = (
            sem("squared_ready"), sem("sigmoid_ready"), sem("v_ready"), sem("done"))
        k_banks, r_banks, v_banks = core.banks[0:2], core.banks[2:4], core.banks[4:6]

        with core.stage() as block:
            @block.sync
            def _(sp):
                core.clear_spent(sp)
                for place, source in loads:
                    sp.dma_start(place[:], dram[source]).then_inc(loaded, 16)

            @block.tensor
            def _(pe):
                pe.wait_ge(loaded, 16 * len(loads))
                with pe.Fori(0, B // PLACES) as turn:
                    for u in range(PLACES):
                        pe.wait_ge(mixed, 2 * PLACES * turn + (2 * u + 1))
                        pe.wait_ge(squared_ready, CREDIT + PLACES * turn)
                        nc.tensor.matmul(k_banks[u][:], w_k[:], x_k[:, u, :]).then_inc(k_ready, 1)
                        pe.wait_ge(mixed, 2 * PLACES * turn + (2 * u + 2))
                        pe.wait_ge(done, CREDIT + PLACES * turn)
                        for t in range(T):
                            tick = nc.tensor.matmul(r_banks[u][:, bass.ts(t, P)], x_r[:, u, bass.ts(t, P)], w_r[:])
                        tick.then_inc(r_ready, 1)
                    for u in range(PLACES):
                        pe.wait_ge(squared_ready, CREDIT + PLACES * turn + (u + 1))
                        for t in range(T):
                            tick = nc.tensor.matmul(v_banks[u][:, bass.ts(t, P)], squared[:, u, bass.ts(t, P)], w_v[:])
                        tick.then_inc(v_ready, 1)

            @block.scalar
            def _(act):
                act.wait_ge(zeroed, 1)
                give_credit(act, sigmoid_ready)
                with act.Fori(0, B // PLACES) as turn:
                    for u in range(PLACES):
                        nc.scalar.copy(x_now[:, u, 1:1 + N], core.xn_chan[:, bass.ts(turn * PLACES + u, N)]
                                       ).then_inc(x_ready, 1)
                    for u in range(PLACES):
                        act.wait_ge(k_ready, PLACES * turn + (u + 1))
                        nc.scalar.activation(relued[:, u, :], k_banks[u][:], ACT.Relu).then_inc(relu_ready, 1)
                    for u in range(PLACES):
                        act.wait_ge(r_ready, PLACES * turn + (u + 1))
                        nc.scalar.activation(receptance[:, u, :], r_banks[u][:], ACT.Sigmoid).then_inc(sigmoid_ready, 1)

            @block.vector
            def _(dve):
                nc.vector.memset(x_now[:, :, 0:1], 0.0).then_inc(zeroed, 1)
                dve.wait_ge(loaded, 16 * len(loads))
                give_credit(dve, squared_ready, done)
                with dve.Fori(0, B // PLACES) as turn:
                    for u in range(PLACES):
                        dve.wait_ge(x_ready, PLACES * turn + (u + 1))
                        nc.vector.tensor_tensor(change[:, u, :], x_now[:, u, 1:1 + N], x_now[:, u, 0:N], ALU.subtract
                                                ).then_inc(change_ready, 1)
                        dve.wait_ge(change_ready, PLACES * turn + (u + 1))
                        for i, place in ((1, x_k), (0, x_r)):
                            nc.vector.scalar_tensor_tensor(place[:, u, :], change[:, u, :], mu[:, i:i + 1],
                                                           x_now[:, u, 0:N], ALU.mult, ALU.add).then_inc(mixed, 1)
                    for u in range(PLACES):
                        dve.wait_ge(relu_ready, PLACES * turn + (u + 1))
                        nc.vector.tensor_tensor(squared[:, u, :], relued[:, u, :], k_banks[u][:], ALU.mult
                                                ).then_inc(squared_ready, 1)
                    for u in range(PLACES):
                        dve.wait_ge(v_ready, PLACES * turn + (u + 1))
                        dve.wait_ge(sigmoid_ready, CREDIT + PLACES * turn + (u + 1))
                        nc.vector.tensor_tensor(core.branch[:, bass.ts(turn * PLACES + u, T), :],
                                                receptance[:, u, :].rearrange("p (t c) -> p t c", t=T),
                                                v_banks[u][:].rearrange("p (t c) -> p t c", t=T), ALU.mult
                                                ).then_inc(done, 1)


def local_attention(core, name, layer):
    nc, dram = core.nc, core.dram
    H, E, W = 8, 64, 64
    HALF = E // 2
    INNER = H * E
    PAIRS = H // 2
    KEYS = W + P
    STEPS = T * PAIRS
    LAG_T, LAG_PV = 2, 3
    AHEAD = 2
    START, EDGE = -AHEAD * PAIRS, 2 * PAIRS
    OT_AT = PAIRS + LAG_PV
    OUT_AT = OT_AT + 1
    END = (T - 1) * PAIRS + OUT_AT + 2
    RING, P_RING = 2, 4
    with ExitStack() as st:
        def buf(n, shape, dtype=F32):
            return core.sbuf(st, f"{name}_{n}", shape, dtype)

        def sem(n):
            return core.sem(f"{name}_{n}")

        w_qkv, w_out = buf("w_qkv", [P, 3, INNER]), buf("w_out", [P, PAIRS, D])
        table = [buf(f"table{i}", [P, T, E]) for i in range(4)]
        head_scale = buf("head_scale", [P, 4, E])
        mask_f, mask = buf("mask_f", [P, KEYS]), buf("mask", [P, 2, KEYS], BF16)
        power = buf("power", [P, H])
        x_now = buf("x_now", [P, N])
        raw = [buf("q_raw", [P, RING, INNER]), buf("k_raw", [P, RING, INNER])]
        squares, norm = buf("squares", [P, 2, INNER]), buf("norm", [P, RING, 2, H])
        part = [buf(f"part{i}", [P, INNER]) for i in range(4)]
        rotated = [buf("q_rotated", [P, RING, INNER]), buf("k_rotated", [P, RING, INNER])]
        chan = [buf("q_chan", [P, PAIRS, N]), buf("k_chan", [P, PAIRS, N])]
        v_tok = buf("v_tok", [P, T, INNER])
        neg_max, row_sum, inverse = buf("neg_max", [P, T, H]), buf("row_sum", [P, T, H]), buf("inverse", [P, T, H])
        probs = buf("probs", [P, P_RING, 2, 2 * P])
        probs_t = buf("probs_t", [P, RING, 4, P])
        heads_out, heads_out_t = buf("heads_out", [P, INNER]), buf("heads_out_t", [P, PAIRS, P])
        score_banks, pt_banks, pv_banks = core.banks[0:2], core.banks[2:4], core.banks[4:6]
        out_bank, free_bank = core.banks[6], core.banks[7]

        loads = [(w_qkv[:], dram["w_qkv_local"][layer]), (head_scale[:], dram["head_scale"][layer].partition_broadcast(P))]
        loads += [(table[i][:], dram["rotary"][i]) for i in range(4)]
        loads += [(mask_f[:], dram["local_mask"]), (w_out[:], dram["w_out_local"][layer])]
        w_loaded = sem("w_loaded")
        loaded, table_ready, mask_ready, zeroed, power_ready = (
            sem("loaded"), sem("table_ready"), sem("mask_ready"), sem("zeroed"), sem("power_ready"))
        x_ready = sem("x_ready")
        raw_ready = [sem("q_ready"), sem("k_ready"), sem("v_ready")]
        raw_copied = [sem("q_copied"), sem("k_copied"), sem("v_copied")]
        squared, sum_ready, floored, norm_ready = sem("squared"), sem("sum_ready"), sem("floored"), sem("norm_ready")
        part_ready = [sem("q_part_ready"), sem("k_part_ready")]
        whole_ready = [sem("q_whole_ready"), sem("k_whole_ready")]
        rotated_ready = [sem("q_rotated_ready"), sem("k_rotated_ready")]
        t_ready = [sem("q_t_ready"), sem("k_t_ready")]
        chan_ready = [sem("q_chan_ready"), sem("k_chan_ready")]
        scores_ready, max_ready, probs_ready = sem("scores_ready"), sem("max_ready"), sem("probs_ready")
        pt_ready, pt_copied, pv_ready = sem("pt_ready"), sem("pt_copied"), sem("pv_ready")
        inverse_ready, normed = sem("inverse_ready"), sem("normed")
        ot_ready, ot_copied, out_ready, out_copied = (
            sem("ot_ready"), sem("ot_copied"), sem("out_ready"), sem("out_copied"))

        def heads_of(step):
            first = 4 * (step % PAIRS // 2) + step % 2
            return first, first + 2

        def halves(x):
            return x.rearrange("p (h two c) -> p h two c", h=H, two=2)

        def by_head(x):
            return x.rearrange("p (h c) -> p h c", h=H)

        def skip(tile):
            return 0 if tile % T else W

        def run(engine, position):
            for n in range(START, EDGE):
                position(0, n, TILES)
            with engine.Fori(0, B - 1) as b:
                for n in range(EDGE, EDGE + STEPS):
                    position(b, n, 2 * T)
            for n in range(EDGE, END):
                position(B - 1, n, T)

        def steps_at(n, lag, end):
            return [n - lag] if 0 <= n - lag < PAIRS * end else []

        def tiles_at(n, after, end):
            return [(n - after) // PAIRS] if (n - after) % PAIRS == 0 and 0 <= (n - after) // PAIRS < end else []

        PROJECT_AT = [-AHEAD * PAIRS + position for position in (0, 1, 3)]
        NORMS_AT, SCALE_AT = PROJECT_AT[1] + 1, PROJECT_AT[1] + 2
        CHAN_AT = -PAIRS + 2

        with core.stage() as block:
            @block.sync
            def _(sp):
                core.clear_spent(sp)
                for n, (place, source) in enumerate(loads):
                    sp.dma_start(place, source).then_inc(loaded if n else w_loaded, 16)

            def rotate(engine, api, b, tile, which):
                source = raw[which][:, tile % RING, :]
                cos_part, sin_part = part[2 * which][:], part[2 * which + 1][:]
                engine.wait_ge(raw_copied[which], T * b + (tile + 1))
                at_least(engine, rotated_ready[which], T * b + tile)
                cos = table[2 * which][:, tile % T, :].unsqueeze(1).broadcast_to([P, H, E])
                api.tensor_tensor(by_head(cos_part), by_head(source), cos, ALU.mult).then_inc(part_ready[which], 1)
                for half in range(2):
                    sin = table[2 * which + 1][:, tile % T, half * HALF:(half + 1) * HALF]
                    api.tensor_tensor(halves(sin_part)[:, :, half, :], halves(source)[:, :, 1 - half, :],
                                      sin.unsqueeze(1).broadcast_to([P, H, HALF]), ALU.mult).then_inc(part_ready[which], 1)
                engine.wait_ge(part_ready[which], 3 * T * b + 3 * (tile + 1))
                api.tensor_tensor(cos_part, cos_part, sin_part, ALU.add).then_inc(whole_ready[which], 1)

            def scale(engine, api, b, tile, which):
                engine.wait_ge(whole_ready[which], T * b + (tile + 1))
                engine.wait_ge(norm_ready, T * b + (tile + 1))
                at_least(engine, t_ready[which], T * b + (tile - RING + 1))
                api.tensor_tensor(by_head(rotated[which][:, tile % RING, :]), by_head(part[2 * which][:]),
                                  norm[:, tile % RING, which, :].unsqueeze(2).broadcast_to([P, H, E]),
                                  ALU.mult).then_inc(rotated_ready[which], 1)

            @block.gpsimd
            def _(pool):
                nc.gpsimd.memset(power[:], -0.5).then_inc(power_ready, 1)
                nc.gpsimd.memset(probs[:], 0.0).then_inc(zeroed, 1)
                pool.wait_ge(power_ready, 1)
                pool.wait_ge(zeroed, 1)
                pool.wait_ge(table_ready, 4)

                def position(b, n, end):
                    for tile in tiles_at(n, PROJECT_AT[1], end):
                        rotate(pool, nc.gpsimd, b, tile, 1)
                        pool.wait_ge(whole_ready[1], T * b + (tile + 1))
                        pool.wait_ge(floored, T * b + (tile + 1))
                        nc.gpsimd.tensor_tensor(norm[:, tile % RING, :, :], norm[:, tile % RING, :, :],
                                                power[:].unsqueeze(1).broadcast_to([P, 2, H]), ALU.pow
                                                ).then_inc(norm_ready, 1)
                        scale(pool, nc.gpsimd, b, tile, 1)

                run(pool, position)

            @block.tensor
            def _(pe):
                def project(b, tile, which):
                    if which == 0:
                        at_least(pe, raw_copied[2], T * b + tile)
                        if tile % T == 0:
                            pe.wait_ge(x_ready, b + (tile // T + 1))
                    elif which == 1:
                        pe.wait_ge(raw_copied[0], T * b + (tile + 1))
                    else:
                        pe.wait_ge(raw_copied[1], T * b + (tile + 1))
                        at_least(pe, chan_ready[1], T * b + tile)
                    nc.tensor.matmul(free_bank[:], x_now[:, bass.ts(tile % T, P)], w_qkv[:, which, :]
                                     ).then_inc(raw_ready[which], 1)

                def to_chan(b, tile, which, end):
                    pe.wait_ge(rotated_ready[which], T * b + (tile + 1))
                    if which == 0:
                        pe.wait_ge(raw_copied[1], T * b + min(tile + 2, end))
                    else:
                        pe.wait_ge(chan_ready[0], T * b + (tile + 1))
                    for pair in range(PAIRS):
                        tick = nc.tensor.transpose(free_bank[:, bass.ts(pair, P)],
                                                   rotated[which][:, tile % RING, bass.ts(pair, P)], core.identity[:])
                    tick.then_inc(t_ready[which], 1)

                def scores(b, s):
                    tile = s // PAIRS
                    t, first = tile % T, skip(tile)
                    if s % PAIRS == 0:
                        pe.wait_ge(chan_ready[0], T * b + (tile + 1))
                        pe.wait_ge(chan_ready[1], T * b + (tile + 1))
                    at_least(pe, probs_ready, STEPS * b + (s - RING + 1))
                    both = score_banks[s % RING][:, 0:2 * KEYS].rearrange("p (h k) -> p h k", h=2)
                    nc.tensor.matmul(both[:, :, first:KEYS], core.identity_bf[:], mask[:, :, first:KEYS],
                                     start=True, stop=False)
                    for h, head in enumerate(heads_of(s)):
                        rows, pair = slice(head % 2 * E, (head % 2 + 1) * E), head // 2
                        tick = nc.tensor.matmul(both[:, h, first:KEYS], chan[0][rows, pair, bass.ts(t, P)],
                                                chan[1][rows, pair, t * P - W + first:(t + 1) * P],
                                                start=False, stop=(h == 1))
                    tick.then_inc(scores_ready, 1)

                def transpose(b, s):
                    pe.wait_ge(probs_ready, STEPS * b + (s + 1))
                    at_least(pe, pt_copied, STEPS * b + (s - RING + 1))
                    for h in range(2):
                        for keys in ((1,) if skip(s // PAIRS) else (0, 1)):
                            tick = nc.tensor.transpose(pt_banks[s % RING][:, bass.ts(2 * h + keys, P)],
                                                       probs[:, s % P_RING, h, bass.ts(keys, P)], core.identity[:])
                    tick.then_inc(pt_ready, 1)

                def product(b, s):
                    tile = s // PAIRS
                    pe.wait_ge(pt_copied, STEPS * b + (s + 1))
                    if s % PAIRS == 0:
                        pe.wait_ge(raw_copied[2], T * b + (tile + 1))
                        at_least(pe, normed, T * b + (tile - RING + 1))
                    for h, head in enumerate(heads_of(s)):
                        for keys in ((1,) if skip(tile) else (0, 1)):
                            tick = nc.tensor.matmul(pv_banks[tile % RING][:, bass.ts(head, E)],
                                                    probs_t[:, s % RING, 2 * h + keys, :],
                                                    v_tok[:, (tile - 1 + keys) % T, bass.ts(head, E)],
                                                    start=(keys == 0 or bool(skip(tile))), stop=(keys == 1))
                    tick.then_inc(pv_ready, 1)

                def position(b, n, end):
                    if n == 0:
                        pe.wait_ge(loaded, 16 * (len(loads) - 1))
                        pe.wait_ge(mask_ready, 2)
                    for s in steps_at(n, 0, end):
                        scores(b, s)
                    for which in range(3):
                        for tile in tiles_at(n, PROJECT_AT[which], end):
                            project(b, tile, which)
                    for tile in tiles_at(n, CHAN_AT, end):
                        to_chan(b, tile, 0, end)
                    for s in steps_at(n, LAG_T, end):
                        transpose(b, s)
                    for s in steps_at(n, LAG_PV, end):
                        product(b, s)
                    for tile in tiles_at(n, CHAN_AT, end):
                        to_chan(b, tile, 1, end)
                    for tile in tiles_at(n, OT_AT, end):
                        pe.wait_ge(normed, T * b + (tile + 1))
                        at_least(pe, out_copied, T * b + tile)
                        for pair in range(PAIRS):
                            tick = nc.tensor.transpose(out_bank[:, bass.ts(pair, P)], heads_out[:, bass.ts(pair, P)],
                                                       core.identity[:])
                        tick.then_inc(ot_ready, 1)
                    for tile in tiles_at(n, OUT_AT, end):
                        pe.wait_ge(ot_copied, T * b + (tile + 1))
                        for pair in range(PAIRS):
                            tick = nc.tensor.matmul(out_bank[:, 0:D], heads_out_t[:, pair, :], w_out[:, pair, :],
                                                    start=(pair == 0), stop=(pair == PAIRS - 1))
                        tick.then_inc(out_ready, 1)

                pe.wait_ge(w_loaded, 16)
                run(pe, position)

            @block.scalar
            def _(act):
                def copy_raw(b, tile, which):
                    act.wait_ge(raw_ready[which], T * b + (tile + 1))
                    if which < 2:
                        at_least(act, whole_ready[which], T * b + (tile - RING + 1))
                        at_least(act, squared, 2 * T * b + 2 * (tile - RING + 1))
                        place = raw[which][:, tile % RING, :]
                    else:
                        at_least(act, pv_ready, STEPS * b + PAIRS * (tile - T + 2))
                        place = v_tok[:, tile % T, :]
                    nc.scalar.copy(place, free_bank[:]).then_inc(raw_copied[which], 1)

                def square(b, tile, which):
                    act.wait_ge(raw_copied[which], T * b + (tile + 1))
                    at_least(act, sum_ready, T * b + tile)
                    nc.scalar.activation(squares[:, which, :], raw[which][:, tile % RING, :], ACT.Square
                                         ).then_inc(squared, 1)

                def copy_chan(b, tile, which):
                    act.wait_ge(t_ready[which], T * b + (tile + 1))
                    at_least(act, scores_ready, STEPS * b + PAIRS * (tile - T + 2))
                    nc.scalar.copy(chan[which][:, :, bass.ts(tile % T, P)],
                                   free_bank[:].rearrange("p (q c) -> p q c", q=PAIRS)).then_inc(chan_ready[which], 1)

                def position(b, n, end):
                    for tile in tiles_at(n, OUT_AT + 1, end):
                        act.wait_ge(out_ready, T * b + (tile + 1))
                        nc.scalar.copy(core.branch[:, bass.ds(b * T + tile, 1), :].rearrange("p o d -> p (o d)"),
                                       out_bank[:, 0:D]).then_inc(out_copied, 1)
                    for which in range(3):
                        for tile in tiles_at(n, PROJECT_AT[which], end):
                            if which == 0 and tile % T == 0:
                                at_least(act, raw_ready[2], T * b + tile)
                                nc.scalar.copy(x_now[:], core.xn_chan[:, bass.ts(b + tile // T, N)]).then_inc(x_ready, 1)
                            copy_raw(b, tile, which)
                    for tile in tiles_at(n, CHAN_AT, end):
                        copy_chan(b, tile, 0)
                    for s in steps_at(n, 0, end):
                        tile = s // PAIRS
                        t, first = tile % T, skip(tile)
                        act.wait_ge(max_ready, STEPS * b + (s + 1))
                        at_least(act, pt_ready, STEPS * b + (s - P_RING + 1))
                        both = score_banks[s % RING][:, 0:2 * KEYS].rearrange("p (h k) -> p h k", h=2)
                        for h, head in enumerate(heads_of(s)):
                            tick = nc.scalar.activation(probs[:, s % P_RING, h, W + first:2 * P],
                                                        both[:, h, first:KEYS], ACT.Exp,
                                                        bias=neg_max[:, t, head:head + 1],
                                                        accum_out=row_sum[:, t, head:head + 1])
                        tick.then_inc(probs_ready, 1)
                    for tile in tiles_at(n, CHAN_AT, end):
                        copy_chan(b, tile, 1)
                    for tile in tiles_at(n, OT_AT, end):
                        act.wait_ge(ot_ready, T * b + (tile + 1))
                        at_least(act, out_ready, T * b + tile)
                        nc.scalar.copy(heads_out_t[:], out_bank[:].rearrange("p (q c) -> p q c", q=PAIRS)
                                       ).then_inc(ot_copied, 1)
                    for which in range(2):
                        for tile in tiles_at(n, PROJECT_AT[which], end):
                            square(b, tile, which)

                act.wait_ge(zeroed, 1)
                run(act, position)

            @block.vector
            def _(dve):
                def normalize(b, tile):
                    t = tile % T
                    dve.wait_ge(probs_ready, STEPS * b + PAIRS * (tile + 1))
                    nc.vector.reciprocal(inverse[:, t, :], row_sum[:, t, :]).then_inc(inverse_ready, 1)
                    dve.wait_ge(inverse_ready, T * b + (tile + 1))
                    dve.wait_ge(pv_ready, STEPS * b + PAIRS * (tile + 1))
                    at_least(dve, ot_ready, T * b + tile)
                    nc.vector.tensor_tensor(by_head(heads_out[:]), by_head(pv_banks[tile % RING][:]),
                                            inverse[:, t, :].unsqueeze(2).broadcast_to([P, H, E]),
                                            ALU.mult).then_inc(normed, 1)

                def norms(b, tile):
                    slot = norm[:, tile % RING, :, :]
                    dve.wait_ge(squared, 2 * T * b + 2 * (tile + 1))
                    for which in range(2):
                        at_least(dve, rotated_ready[which], T * b + (tile - RING + 1))
                    nc.vector.tensor_reduce(slot, squares[:].rearrange("p a (h c) -> p a h c", h=H), AX_X, ALU.add
                                            ).then_inc(sum_ready, 1)
                    dve.wait_ge(sum_ready, T * b + (tile + 1))
                    nc.vector.tensor_scalar(slot, slot, 1e-24, None, ALU.max).then_inc(floored, 1)

                def position(b, n, end):
                    for s in steps_at(n, 0, end):
                        tile, head = s // PAIRS, heads_of(s)[0]
                        first = skip(tile)
                        dve.wait_ge(scores_ready, STEPS * b + (s + 1))
                        nc.vector.tensor_reduce(
                            neg_max[:, tile % T, head:head + 3:2],
                            score_banks[s % RING][:, 0:2 * KEYS].rearrange("p (h k) -> p h k", h=2)[:, :, first:KEYS],
                            AX_X, ALU.max, negate=True).then_inc(max_ready, 1)
                    for s in steps_at(n, LAG_T, end):
                        dve.wait_ge(pt_ready, STEPS * b + (s + 1))
                        at_least(dve, pv_ready, STEPS * b + (s - RING + 1))
                        blocks = probs_t[:, s % RING, :, :].rearrange("p (h k) c -> p h k c", h=2)
                        source = pt_banks[s % RING][:].rearrange("p (h k c) -> p h k c", h=2, k=2)
                        if skip(s // PAIRS):
                            blocks, source = blocks[:, :, 1, :], source[:, :, 1, :]
                        nc.vector.tensor_copy(blocks, source).then_inc(pt_copied, 1)
                    for tile in tiles_at(n, OT_AT - 1, end):
                        normalize(b, tile)
                    for tile in tiles_at(n, PROJECT_AT[0], end):
                        rotate(dve, nc.vector, b, tile, 0)
                    for tile in tiles_at(n, NORMS_AT, end):
                        norms(b, tile)
                    for tile in tiles_at(n, SCALE_AT, end):
                        scale(dve, nc.vector, b, tile, 0)

                dve.wait_ge(loaded, 16 * (len(loads) - 1))
                for h in range(2):
                    nc.vector.tensor_copy(mask[:, h, :], mask_f[:]).then_inc(mask_ready, 1)
                for i in range(4):
                    nc.vector.tensor_tensor(table[i][:], table[i][:], head_scale[:, i, :].unsqueeze(1).broadcast_to(
                        [P, T, E]), ALU.mult).then_inc(table_ready, 1)
                dve.wait_ge(table_ready, 4)
                run(dve, position)


def gated_gelu(core, name, layer, plus=None):
    nc, dram = core.nc, core.dram
    HID = 341
    CHUNKS = [(c, min(P, HID - c)) for c in range(0, HID, P)]
    C = len(CHUNKS)
    with ExitStack() as st:
        def buf(n, shape, dtype=F32):
            return core.sbuf(st, f"{name}_{n}", shape, dtype)

        def sem(n):
            return core.sem(f"{name}_{n}")

        w1, w2, b1 = buf("w1", [P, 2 * HID]), buf("w2", [P, C, D]), buf("b1", [P, 2, C])
        gelu, hidden = buf("gelu", [P, 2, N]), buf("hidden", [P, 2, C, N])
        a_banks, g_banks, y_banks = core.banks[0:2], core.banks[2:4], core.banks[4:6]
        loaded, g_ready, a_ready, gelu_ready = sem("loaded"), sem("g_ready"), sem("a_ready"), sem("gelu_ready")
        hidden_ready, y_ready, y_copied = sem("hidden_ready"), sem("y_ready"), sem("y_copied")
        loads = [(w1[:], dram["w1_gelu"][layer]), (w2[:], dram["w2_gelu"][layer]), (b1[:], dram["b1_gelu"][layer])]

        with core.stage() as block:
            @block.sync
            def _(sp):
                core.clear_spent(sp)
                for place, source in loads:
                    sp.dma_start(place, source).then_inc(loaded, 16)

            @block.tensor
            def _(pe):
                pe.wait_ge(loaded, 16 * len(loads))
                give_credit(pe, y_ready)
                with pe.Fori(0, B // 2) as turn:
                    for u in range(2):
                        x = core.xn_chan[:, bass.ts(turn * 2 + u, N)]
                        for c, (first, rows) in enumerate(CHUNKS):
                            n = C * u + c
                            if n >= 2:
                                pe.wait_ge(gelu_ready, 2 * C * turn + (n - 1))
                            nc.tensor.matmul(g_banks[n % 2][0:rows, :], w1[:, HID + first:HID + first + rows], x
                                             ).then_inc(g_ready, 1)
                            if n >= 2:
                                pe.wait_ge(hidden_ready, 2 * C * turn + (n - 1))
                            nc.tensor.matmul(a_banks[n % 2][0:rows, :], w1[:, first:first + rows], x
                                             ).then_inc(a_ready, 1)
                    for u in range(2):
                        pe.wait_ge(hidden_ready, 2 * C * turn + C * (u + 1))
                        pe.wait_ge(y_copied, CREDIT + 2 * turn)
                        for t in range(T):
                            for c, (_, rows) in enumerate(CHUNKS):
                                tick = nc.tensor.matmul(y_banks[u][:, bass.ts(t, P)], hidden[0:rows, u, c, bass.ts(t, P)],
                                                        w2[0:rows, c, :], start=(c == 0), stop=(c == C - 1))
                        tick.then_inc(y_ready, 1)

            @block.scalar
            def _(act):
                act.wait_ge(loaded, 16 * len(loads))
                with act.Fori(0, B // 2) as turn:
                    for n in range(2 * C):
                        rows = CHUNKS[n % C][1]
                        act.wait_ge(g_ready, 2 * C * turn + (n + 1))
                        if n >= 2:
                            act.wait_ge(hidden_ready, 2 * C * turn + (n - 1))
                        nc.scalar.activation(gelu[0:rows, n % 2, :], g_banks[n % 2][0:rows, :], ACT.Gelu,
                                             bias=b1[0:rows, 1, n % C:n % C + 1]).then_inc(gelu_ready, 1)

            @block.vector
            def _(dve):
                dve.wait_ge(loaded, 16 * len(loads))
                give_credit(dve, y_copied)
                with dve.Fori(0, B // 2) as turn:
                    for n in range(2 * C):
                        u, c = n // C, n % C
                        rows = CHUNKS[c][1]
                        dve.wait_ge(a_ready, 2 * C * turn + (n + 1))
                        dve.wait_ge(gelu_ready, 2 * C * turn + (n + 1))
                        if c == 0:
                            dve.wait_ge(y_ready, CREDIT + 2 * turn)
                        nc.vector.scalar_tensor_tensor(hidden[0:rows, u, c, :], a_banks[n % 2][0:rows, :],
                                                       b1[0:rows, 0, c:c + 1], gelu[0:rows, n % 2, :],
                                                       ALU.add, ALU.mult).then_inc(hidden_ready, 1)
                    for u in range(2):
                        dve.wait_ge(y_ready, CREDIT + 2 * turn + (u + 1))
                        tiles = bass.ts(turn * 2 + u, T)
                        out = core.branch[:, tiles, :]
                        y = y_banks[u][:].rearrange("p (t c) -> p t c", t=T)
                        if plus is None:
                            nc.vector.tensor_copy(out, y).then_inc(y_copied, 1)
                        else:
                            nc.vector.tensor_tensor(out, y, plus[:, tiles, :], ALU.add).then_inc(y_copied, 1)


def windowed_layers(core, layers=2):
    with ExitStack() as st:
        kept = core.sbuf(st, "x_kept", [P, TILES, D])
        join(core, "shift_first", shift=True, keep=kept)
        for n in range(layers):
            local_attention(core, f"local{n}", n)
            join(core, f"local_sum{n}", residual_norm=False, shift=True, layernorm=(f"ln_g{n}", f"ln_b{n}"))
            gated_gelu(core, f"gelu{n}", n, plus=kept if n == layers - 1 else None)
            if n < layers - 1:
                join(core, f"gelu_sum{n}", residual_norm=False, branch_bias=f"b2_gelu{n}", shift=True)
    return f"b2_gelu{layers - 1}"


def delta_gates(core, name, beta, neg_beta, rows):
    nc, dram = core.nc, core.dram
    H = 8
    GATE_STEPS = 18
    LARGEST, TOP, ENOUGH = 88.72284, 120.0, 2.5e12
    with ExitStack() as st:
        def buf(n, shape, dtype=F32):
            return core.sbuf(st, f"{name}_{n}", shape, dtype)

        def sem(n):
            return core.sem(f"{name}_{n}")

        w_ab, dt_bias, a_log, zeros = buf("w_ab", [P, 2 * H]), buf("dt_bias", [P, H]), buf("a_log", [P, H]), buf("zeros", [P, P])
        gate, above, below, u, s2, series = (buf(n, [P, H, TILES]) for n in ("gate", "above", "below", "u", "s2", "series"))
        infinite = buf("infinite", [P, H])
        decay_row, product_row = buf("decay_row", [P, P]), buf("product_row", [P, P])
        loaded, ab_ready, step, exp_ready = sem("loaded"), sem("ab_ready"), sem("step"), sem("exp_ready")
        decay_ready, row_ready, stored, zeroed = sem("decay_ready"), sem("row_ready"), sem("stored"), sem("zeroed")
        log_ready = sem("log_ready")
        ab = core.banks[0][:, 0:TILES * 2 * H].rearrange("p (t w h) -> p w h t", t=TILES, w=2)
        wide = [P, H, TILES]

        with core.stage() as block:
            @block.sync
            def _(sp):
                core.clear_spent(sp)
                sp.dma_start(w_ab[:], dram["w_ab"]).then_inc(loaded, 16)
                sp.dma_start(dt_bias[:], dram["dt_bias"].partition_broadcast(P)).then_inc(loaded, 16)
                sp.dma_start(a_log[:], dram["a_log"].partition_broadcast(P)).then_inc(loaded, 16)
                sp.wait_ge(step, GATE_STEPS + 3)
                sp.dma_start(rows[:, 0, :, :], decay_row[:]).then_inc(stored, 16)
                sp.dma_start(rows[:, 1, :, :], product_row[:]).then_inc(stored, 16)
                sp.wait_ge(stored, 32)

            @block.tensor
            def _(pe):
                pe.wait_ge(loaded, 48)
                for t in range(TILES):
                    tick = nc.tensor.matmul(core.banks[0][:, bass.ts(t, 2 * H)], core.xn_chan[:, bass.ts(t, P)], w_ab[:])
                tick.then_inc(ab_ready, 1)
                pe.wait_ge(decay_ready, 1)
                nc.tensor.transpose(core.banks[1][:, 0:P], gate[:].rearrange("p h t -> p (h t)"), core.identity[:]
                                    ).then_inc(row_ready, 1)

            @block.scalar
            def _(act):
                act.wait_ge(log_ready, 3)
                nc.scalar.activation(a_log[:], a_log[:], ACT.Exp).then_inc(exp_ready, 1)
                act.wait_ge(step, 3)
                nc.scalar.activation(u[:], below[:], ACT.Exp).then_inc(exp_ready, 1)
                act.wait_ge(step, GATE_STEPS)
                nc.scalar.activation(gate[:], gate[:], ACT.Exp, scale=-1.0).then_inc(decay_ready, 1)
                nc.scalar.activation(beta[:], ab[:, 1], ACT.Sigmoid).then_inc(exp_ready, 1)

            @block.vector
            def _(dve):
                nc.vector.memset(zeros[:], 0.0).then_inc(zeroed, 1)
                dve.wait_ge(loaded, 48)
                nc.vector.tensor_scalar(infinite[:], a_log[:], LARGEST, 1000.0, ALU.is_gt, ALU.mult).then_inc(log_ready, 1)
                dve.wait_ge(log_ready, 1)
                nc.vector.tensor_tensor(a_log[:], a_log[:], infinite[:], ALU.add).then_inc(log_ready, 1)
                dve.wait_ge(log_ready, 2)
                nc.vector.tensor_scalar(a_log[:], a_log[:], 0.5, TOP / 2, ALU.mult, ALU.min).then_inc(log_ready, 1)
                dve.wait_ge(ab_ready, 1)
                n = 0

                def done(tick):
                    nonlocal n
                    n += 1
                    tick.then_inc(step, 1)
                    dve.wait_ge(step, n)

                done(nc.vector.tensor_tensor(gate[:], ab[:, 0], dt_bias[:].unsqueeze(2).broadcast_to(wide), ALU.add))
                done(nc.vector.tensor_scalar(above[:], gate[:], 0.0, None, ALU.max))
                done(nc.vector.scalar_tensor_tensor(below[:], gate[:], 0.0, above[:], ALU.min, ALU.subtract))
                dve.wait_ge(exp_ready, 2)
                done(nc.vector.tensor_scalar(s2[:], u[:], 2.0, None, ALU.add))
                done(nc.vector.reciprocal(s2[:], s2[:]))
                done(nc.vector.tensor_tensor(u[:], u[:], s2[:], ALU.mult))
                done(nc.vector.tensor_tensor(s2[:], u[:], u[:], ALU.mult))
                done(nc.vector.tensor_scalar(series[:], s2[:], 1.0 / 15, 1.0 / 13, ALU.mult, ALU.add))
                done(nc.vector.tensor_tensor(series[:], series[:], s2[:], ALU.mult))
                for k in (11, 9, 7, 5, 3):
                    done(nc.vector.scalar_tensor_tensor(series[:], series[:], 1.0 / k, s2[:], ALU.add, ALU.mult))
                done(nc.vector.scalar_tensor_tensor(series[:], series[:], 1.0, u[:], ALU.add, ALU.mult))
                done(nc.vector.scalar_tensor_tensor(series[:], series[:], 2.0, above[:], ALU.mult, ALU.add))
                root = a_log[:].unsqueeze(2).broadcast_to(wide)
                done(nc.vector.tensor_tensor(gate[:], series[:], root, ALU.mult))
                done(nc.vector.scalar_tensor_tensor(gate[:], gate[:], ENOUGH, root, ALU.min, ALU.mult))
                assert n == GATE_STEPS
                dve.wait_ge(exp_ready, 3)
                nc.vector.tensor_scalar(neg_beta[:], beta[:], -1.0, None, ALU.mult).then_inc(zeroed, 1)
                dve.wait_ge(row_ready, 1)
                dve.wait_ge(zeroed, 2)
                done(nc.vector.tensor_copy(decay_row[:], core.banks[1][:, 0:P]))
                done(nc.vector.tensor_tensor_scan(product_row[:], decay_row[:], zeros[:], 1.0, ALU.mult, ALU.add))
                done(nc.vector.memset(decay_row[:, 0:1], 0.0))


def delta_rule(core, name, beta, neg_beta, rows):
    nc, dram = core.nc, core.dram
    H, TAPS = 8, 4
    EPS = 1e-6
    SLOTS = 18
    with ExitStack() as st:
        def buf(n, shape, dtype=F32):
            return core.sbuf(st, f"{name}_{n}", shape, dtype)

        def sem(n):
            return core.sem(f"{name}_{n}")

        w_in, w_out, w_conv = buf("w_in", [P, 4, P]), buf("w_out", [P, D]), buf("w_conv", [P, 3, TAPS])
        norm_w = buf("norm_w", [P, D])
        decay, product = buf("decay", [P, TILES, P]), buf("product", [P, TILES, P])
        last_product = buf("last_product", [P, TILES])
        padded = buf("padded", [P, TAPS - 1 + N])
        kq = buf("kq", [P, B, 2, T, P])
        v_chan, v_tok = buf("v_chan", [P, N]), buf("v_tok", [P, B, T, P])
        kq_decayed = buf("kq_decayed", [P, B, 2, T, P])
        k_decayed = buf("k_decayed", [P, B, T, P])
        silu_z, z_scaled = buf("silu_z", [P, T, P]), buf("z_scaled", [P, B, T, P])
        identities = buf("identities", [P, T, P])
        d_t, d_strict = buf("d_t", [P, T, P]), buf("d_strict", [P, T, P])
        x_first = buf("x_first", [P, T, P])
        scores = buf("scores", [P, B, T, P])
        x_t, x_n, inverse = buf("x_t", [P, T, P]), buf("x_n", [P, 2, T, P]), buf("inverse", [P, 2, T, P])
        w_rhs, u = buf("w_rhs", [P, P]), buf("u", [P, P])
        state = buf("state", [P, P])
        squares, o_rms, power = buf("squares", [P, T, P]), buf("o_rms", [P, T]), buf("power", [P, T])
        gated, gated_t = buf("gated", [P, T, P]), buf("gated_t", [P, T, P])
        in_bank, g_bank, a_bank, n_bank, t_bank, r_bank, chain_bank, o_bank = core.banks

        constants_loaded, constants_ready = sem("constants_loaded"), sem("constants_ready")
        w_in_loaded, decay_loaded, product_loaded, w_out_loaded = (
            sem("w_in_loaded"), sem("decay_loaded"), sem("product_loaded"), sem("w_out_loaded"))
        last_ready, place_free = sem("last_ready"), sem("place_free")
        in_ready = [sem(f"{n}_in_ready") for n in "kqvz"]
        padded_ready, tap_ready, conv_ready = sem("padded_ready"), sem("tap_ready"), sem("conv_ready")
        silu_ready, z_ready, kq_decayed_ready = sem("silu_ready"), sem("z_ready"), sem("kq_decayed_ready")
        kt_ready, k_decayed_ready, vt_ready, v_ready = (
            sem("kt_ready"), sem("k_decayed_ready"), sem("vt_ready"), sem("v_ready"))
        d_ready, strict_ready, g_ready, a_ready = sem("d_ready"), sem("strict_ready"), sem("g_ready"), sem("a_ready")
        x_ready, scores_ready = sem("x_ready"), sem("scores_ready")
        n_ready, n_copied, t_ready, t_copied = sem("n_ready"), sem("n_copied"), sem("t_ready"), sem("t_copied")
        r_started, r_ready, r_added = sem("r_started"), sem("r_ready"), sem("r_added")
        ks_ready, w_ready, y_ready, u_ready = sem("ks_ready"), sem("w_ready"), sem("y_ready"), sem("u_ready")
        o_ready, ds_ready, state_ready = sem("o_ready"), sem("ds_ready"), sem("state_ready")
        squares_ready, mean_ready, rms_ready = sem("squares_ready"), sem("mean_ready"), sem("rms_ready")
        gated_ready, gt_ready, gt_copied, out_ready, added = (
            sem("gated_ready"), sem("gt_ready"), sem("gt_copied"), sem("out_ready"), sem("added"))

        K, Q, V, Z = range(4)
        PROJECT_AT = {0: K, 3: Q, 6: V, 9: Z}
        LEVELS = (1, 2, 4, 8, 16)
        BY_PRODUCT = 1
        INVERT_AT = {0: (1, "n_first")}
        slot = 1
        for power_of in LEVELS:
            for what in ("n", "t") + (("r",) if power_of > 1 else ()):
                INVERT_AT[slot] = (power_of, what)
                slot += 1
        INVERT_AT.update({15: (32, "n"), 16: (32, "r"), 17: (64, "r")})
        assert slot == 15
        N_COPY = {1: 1, 2: 2, 4: 3, 8: 4, 16: 5, 32: 6, 64: 7}
        T_COPY = {2: 1, 4: 2, 8: 3, 16: 4, 32: 5}
        R_ADD = {2: 1, 4: 2, 8: 3, 16: 4, 32: 5, 64: 6}
        RECUR_AT = {}
        slot = 0
        for c in range(T):
            for what in ("w",) * (c > 0) + ("y", "o") + ("s",) * (c < T - 1):
                RECUR_AT[slot] = (c, what)
                slot += 1
        assert slot == 14

        def x_transposed(m):
            return x_first if m == 1 else x_t

        def extent(m):
            return P - m if m >= 16 else P

        def by_tile(bank):
            return bank[:].rearrange("p (t c) -> p t c", t=T)

        with core.stage() as block:
            def rounds(head, work, first=False, last=False):
                for b in range(B):
                    before = None if first and b == 0 else (head, b - 1) if b else (head - 1, B - 1)
                    after = None if last and b == B - 1 else (head, b + 1) if b < B - 1 else (head + 1, 0)
                    one_round(work, (head, b), after, before)

            def one_round(work, now, after, before):
                invert, prepare, recur = work
                for slot in range(SLOTS):
                    if now is not None:
                        invert(*now, slot)
                    if before is not None:
                        recur(*before, slot)
                    if after is not None:
                        prepare(*after, slot)

            def all_rounds(engine, *work):
                one_round(work, None, (0, 0), None)
                rounds(0, work, first=True)
                with engine.Fori(1, H - 1) as head:
                    rounds(head, work)
                rounds(H - 1, work, last=True)
                one_round(work, None, None, (H - 1, B - 1))

            def count(per_group, head, b, n):
                return head * (B * per_group) + (b * per_group + n)

            def wait(engine, semaphore, per_group, head, b, n):
                at_least(engine, semaphore, count(per_group, head, b, n))

            def column(gate, head, b, c):
                t = b * T + c
                if isinstance(head, int):
                    return gate[:, head, t:t + 1]
                return gate[:, bass.ds(head, 1), t:t + 1].rearrange("p o t -> p (o t)")

            @block.sync
            def _(sp):
                core.clear_spent(sp)
                sp.dma_start(norm_w[:], dram["norm_w"].partition_broadcast(P)).then_inc(constants_loaded, 16)
                sp.dma_start(identities[:, 0, :], core.identity[:]).then_inc(constants_loaded, 16)
                for t in range(1, T):
                    sp.dma_start(identities[:, t, :], core.identity[:]).then_inc(constants_loaded, 16)

                def load(head):
                    wait(sp, in_ready[Z], 1, head, 0, 0)
                    sp.sem_inc(place_free, 1)
                    wait(sp, conv_ready, 3, head, 0, 0)
                    sp.sem_inc(place_free, 1)
                    src = bass.ds(head, 1) if not isinstance(head, int) else slice(head, head + 1)
                    sp.dma_start(w_in[:], dram["w_in"][src, :, :, :]).then_inc(w_in_loaded, 16)
                    sp.dma_start(w_conv[:], dram["w_conv"][src, :, :, :]).then_inc(w_in_loaded, 16)
                    wait(sp, kq_decayed_ready, 1, head, 0, 0)
                    sp.sem_inc(place_free, 1)
                    wait(sp, last_ready, 1, 0, 0, head)
                    sp.sem_inc(place_free, 1)
                    sp.dma_start(product[:].rearrange("p t c -> p (t c)"), rows[src, 1, :, :].rearrange(
                        "h t c -> (h t c)").partition_broadcast(P)).then_inc(product_loaded, 16)
                    wait(sp, d_ready, 1, head, 0, 0)
                    sp.sem_inc(place_free, 1)
                    sp.dma_start(decay[:].rearrange("p t c -> p (t c)"), rows[src, 0, :, :].rearrange(
                        "h t c -> (h t c)").partition_broadcast(P)).then_inc(decay_loaded, 16)
                    wait(sp, out_ready, 1, head, 0, 0)
                    sp.sem_inc(place_free, 1)
                    sp.dma_start(w_out[:], dram["w_out_delta"][src, :, :]).then_inc(w_out_loaded, 16)

                load(0)
                with sp.Fori(1, H) as head:
                    load(head)

            @block.tensor
            def _(pe):
                def project(head, b, which):
                    if which == K:
                        wait(pe, w_in_loaded, 1, 0, 0, (head + 1) * 32)
                        wait(pe, v_ready, 1, head, b, 0)
                        wait(pe, added, 1, head, b, -2)
                    elif which in (Q, V):
                        wait(pe, padded_ready, 3, head, b, which)
                    else:
                        wait(pe, padded_ready, 3, head, b, 3)
                    if which == Z:
                        for t in range(T):
                            tick = nc.tensor.matmul(in_bank[:, bass.ts(t, P)], core.xn_chan[:, bass.ts(b * T + t, P)],
                                                    w_in[:, Z, :])
                    else:
                        tick = nc.tensor.matmul(in_bank[:], w_in[:, which, :], core.xn_chan[:, bass.ts(b, N)])
                    tick.then_inc(in_ready[which], 1)

                def prepare(head, b, slot):
                    if slot in PROJECT_AT:
                        project(head, b, PROJECT_AT[slot])
                    if slot == 13:
                        wait(pe, conv_ready, 3, head, b, 1)
                        wait(pe, silu_ready, 1, head, b, 1)
                        for t in range(T):
                            tick = nc.tensor.transpose(in_bank[:, bass.ts(t, P)], kq[:, b, 0, t, :], core.identity[:])
                        tick.then_inc(kt_ready, 1)
                    if slot == 14:
                        wait(pe, conv_ready, 3, head, b, 3)
                        wait(pe, k_decayed_ready, 1, head, b, 1)
                        for t in range(T):
                            tick = nc.tensor.transpose(in_bank[:, bass.ts(t, P)], v_chan[:, bass.ts(t, P)], core.identity[:])
                        tick.then_inc(vt_ready, 1)
                    if slot in (12, 15):
                        bank, done, place, read = {12: (g_bank, g_ready, 0, x_ready),
                                                   15: (a_bank, a_ready, 1, scores_ready)}[slot]
                        wait(pe, read, 1, head, b, 0)
                        for t in range(T):
                            tick = nc.tensor.matmul(bank[:, bass.ts(t, P)], kq[:, b, 0, t, :], kq[:, b, place, t, :])
                        tick.then_inc(done, 1)

                def invert(head, b, slot):
                    m, what = INVERT_AT[slot]
                    old = N_COPY[m] - 1 if m in N_COPY else 0
                    if what == "n_first":
                        wait(pe, x_ready, 1, head, b, 1)
                        for t in range(T):
                            tick = nc.tensor.transpose(n_bank[:, bass.ts(t, P)], x_first[:, t, :], core.identity[:])
                        tick.then_inc(n_ready, 1)
                        return
                    wait(pe, n_copied, 7, head, b, N_COPY[2 * m if what == "t" and m > BY_PRODUCT else m])
                    if what == "n" and m > 1:
                        wait(pe, t_copied, 5, head, b, T_COPY[m])
                    xn, xt, rows, after = x_n[:, old % 2], x_transposed(m), extent(m), extent(2 * m)
                    for t in range(T):
                        if what == "n":
                            tick = nc.tensor.matmul(by_tile(n_bank)[:, t, 0:after], xt[0:rows, t, :],
                                                    xn[0:rows, t, 0:after])
                        elif what == "t" and m <= BY_PRODUCT:
                            tick = nc.tensor.matmul(t_bank[:, bass.ts(t, P)], xn[:, t, :], xt[:, t, :])
                        elif what == "t":
                            tick = nc.tensor.transpose(t_bank[0:after, bass.ts(t, P)], x_n[:, (old + 1) % 2, t, 0:after],
                                                       core.identity[:])
                        else:
                            if t == 0:
                                wait(pe, r_started, 1, head, b, 1)
                                wait(pe, r_added, 6, head, b, R_ADD[m] - 1)
                            tick = nc.tensor.matmul(by_tile(r_bank)[0:rows, t, P - rows:P], xn[:, t, 0:rows],
                                                    inverse[:, b % 2, t, P - rows:P])
                    tick.then_inc({"n": n_ready, "t": t_ready, "r": r_ready}[what], 1)

                def recur(head, b, slot):
                    if slot in RECUR_AT:
                        c, what = RECUR_AT[slot]
                        if what == "w":
                            wait(pe, state_ready, 3, head, b, c)
                            wait(pe, kq_decayed_ready, 1, head, b, 1)
                            nc.tensor.matmul(chain_bank[:, 0:P], kq_decayed[:, b, 0, c, :], state[:]).then_inc(ks_ready, 1)
                        elif what == "y":
                            if c:
                                wait(pe, w_ready, 3, head, b, c)
                            else:
                                wait(pe, v_ready, 1, head, b, 1)
                                wait(pe, r_added, 6, head, b, 6)
                            nc.tensor.matmul(chain_bank[:, 0:P], inverse[:, b % 2, c, :],
                                             w_rhs[:] if c else v_tok[:, b, 0, :]).then_inc(y_ready, 1)
                        elif what == "o":
                            wait(pe, scores_ready, 1, head, b, 1)
                            wait(pe, u_ready, 4, head, b, c + 1)
                            out = o_bank[:, bass.ts(c, P)]
                            if c:
                                nc.tensor.matmul(out, kq_decayed[:, b, 1, c, :], state[:], start=True, stop=False)
                            else:
                                wait(pe, gated_ready, 1, head, b, 0)
                            tick = nc.tensor.matmul(out, scores[:, b, c, :], u[:], start=(c == 0), stop=True)
                            if c == T - 1:
                                tick.then_inc(o_ready, 1)
                        else:
                            wait(pe, k_decayed_ready, 1, head, b, 1)
                            nc.tensor.matmul(chain_bank[:, 0:P], k_decayed[:, b, c, :], u[:]).then_inc(ds_ready, 1)
                    if slot == 16:
                        wait(pe, gated_ready, 1, head, b, 1)
                        wait(pe, v_ready, 1, 0, 0, min(count(1, head, b, 3), H * B) if isinstance(head, int) else
                             count(1, head, b, 3))
                        for t in range(T):
                            tick = nc.tensor.transpose(in_bank[:, bass.ts(t, P)], gated[:, t, :], core.identity[:])
                        tick.then_inc(gt_ready, 1)
                    if slot == 17:
                        wait(pe, gt_copied, 1, head, b, 1)
                        wait(pe, w_out_loaded, 1, 0, 0, (head + 1) * 16)
                        for t in range(T):
                            tick = nc.tensor.matmul(in_bank[:, bass.ts(t, P)], gated_t[:, t, :], w_out[:])
                        tick.then_inc(out_ready, 1)

                all_rounds(pe, invert, prepare, recur)

            @block.scalar
            def _(act):
                act.wait_ge(constants_ready, 3)

                def prepare(head, b, slot):
                    if slot in (1, 4, 7):
                        which = PROJECT_AT[slot - 1]
                        wait(act, in_ready[which], 1, head, b, 1)
                        wait(act, conv_ready, 3, head, b, which)
                        nc.scalar.copy(padded[:, TAPS - 1:], in_bank[:]).then_inc(padded_ready, 1)
                    if slot == 10:
                        wait(act, in_ready[Z], 1, head, b, 1)
                        wait(act, z_ready, 1, head, b, 0)
                        nc.scalar.activation(silu_z[:], in_bank[:].rearrange("p (t c) -> p t c", t=T), ACT.Silu
                                             ).then_inc(silu_ready, 1)
                    if slot == 14:
                        wait(act, vt_ready, 1, head, b, 1)
                        nc.scalar.copy(v_tok[:, b, :, :], in_bank[:].rearrange("p (t c) -> p t c", t=T)
                                       ).then_inc(v_ready, 1)

                def invert(head, b, slot):
                    m, what = INVERT_AT[slot]
                    if what in ("n_first", "n"):
                        n = 0 if what == "n_first" else N_COPY[m]
                        wait(act, n_ready, 7, head, b, n + 1)
                        cols = P if what == "n_first" else extent(2 * m)
                        nc.scalar.copy(x_n[:, n % 2, :, 0:cols], by_tile(n_bank)[:, :, 0:cols]).then_inc(n_copied, 1)
                    elif what == "t":
                        wait(act, t_ready, 5, head, b, T_COPY[2 * m])
                        rows = extent(2 * m)
                        nc.scalar.copy(x_t[0:rows], by_tile(t_bank)[0:rows]).then_inc(t_copied, 1)

                def recur(head, b, slot):
                    if slot in RECUR_AT and RECUR_AT[slot][1] == "y":
                        c = RECUR_AT[slot][0]
                        wait(act, y_ready, 4, head, b, c + 1)
                        nc.scalar.activation(u[:], chain_bank[:, 0:P], ACT.Copy, scale=column(beta, head, b, c)
                                             ).then_inc(u_ready, 1)
                    if slot == 14:
                        wait(act, o_ready, 1, head, b, 1)
                        for t in range(T):
                            tick = nc.scalar.activation(squares[:, t, :], o_bank[:, bass.ts(t, P)], ACT.Square,
                                                        accum_out=o_rms[:, t:t + 1])
                        tick.then_inc(squares_ready, 1)
                    if slot == 16:
                        wait(act, gt_ready, 1, head, b, 1)
                        nc.scalar.copy(gated_t[:], in_bank[:].rearrange("p (t c) -> p t c", t=T)).then_inc(gt_copied, 1)

                all_rounds(act, invert, prepare, recur)

            @block.gpsimd
            def _(pool):
                nc.gpsimd.memset(power[:], -0.5).then_inc(constants_ready, 1)
                nc.gpsimd.memset(core.branch[:], 0.0).then_inc(constants_ready, 1)
                nc.gpsimd.memset(padded[:, 0:TAPS - 1], 0.0).then_inc(constants_ready, 1)
                pool.wait_ge(constants_ready, 3)
                pool.wait_ge(constants_loaded, 16 * (1 + T))

                def prepare(head, b, slot):
                    if slot == 7:
                        wait(pool, conv_ready, 3, head, b, 2)
                        wait(pool, product_loaded, 1, 0, 0, (head + 1) * 16)
                        for i in range(2):
                            tick = nc.gpsimd.tensor_tensor(kq_decayed[:, b, i], kq[:, b, i],
                                                           product[:, b * T:(b + 1) * T, :], ALU.mult)
                        tick.then_inc(kq_decayed_ready, 1)
                    if slot == 10:
                        wait(pool, d_ready, 1, head, b, 1)
                        nc.gpsimd.tensor_tensor(d_strict[:], d_t[:], identities[:], ALU.subtract).then_inc(strict_ready, 1)
                        wait(pool, silu_ready, 1, head, b, 1)
                        nc.gpsimd.tensor_tensor(z_scaled[:, b], silu_z[:], norm_w[:].unsqueeze(1).broadcast_to([P, T, P]),
                                                ALU.mult).then_inc(z_ready, 1)

                def invert(head, b, slot):
                    if slot == 0:
                        wait(pool, x_ready, 1, head, b, 1)
                        nc.gpsimd.tensor_tensor(inverse[:, b % 2], x_first[:], identities[:], ALU.add).then_inc(r_started, 1)

                def recur(head, b, slot):
                    if slot == 14:
                        wait(pool, mean_ready, 1, head, b, 1)
                        nc.gpsimd.tensor_tensor(o_rms[:], o_rms[:], power[:], ALU.pow).then_inc(rms_ready, 1)

                all_rounds(pool, invert, prepare, recur)

            @block.vector
            def _(dve):
                dve.wait_ge(constants_ready, 3)
                dve.wait_ge(constants_loaded, 16 * (1 + T))

                def tap(head, b, which, n):
                    def shifted(back):
                        place = padded[:, TAPS - 1 - back:TAPS - 1 - back + N]
                        return place if which == V else place.rearrange("p (t c) -> p t c", t=T)

                    out = v_chan[:] if which == V else kq[:, b, which, :, :]
                    if n == 0:
                        wait(dve, padded_ready, 3, head, b, which + 1)
                        nc.vector.tensor_scalar(out, shifted(0), w_conv[:, which, TAPS - 1:TAPS], None, ALU.mult
                                                ).then_inc(tap_ready, 1)
                    wait(dve, tap_ready, 9, head, b, 3 * which + n + 1)
                    nc.vector.scalar_tensor_tensor(out, shifted(n + 1), w_conv[:, which, TAPS - 2 - n:TAPS - 1 - n], out,
                                                   ALU.mult, ALU.add).then_inc(conv_ready if n == 2 else tap_ready, 1)

                def prepare(head, b, slot):
                    if 1 <= slot < 10:
                        tap(head, b, (slot - 1) // 3, (slot - 1) % 3)
                    if slot == 10:
                        wait(dve, decay_loaded, 1, 0, 0, (head + 1) * 16)
                        wait(dve, strict_ready, 1, head, b, 0)
                        nc.vector.tensor_tensor_scan(
                            d_t[:].rearrange("p t c -> p (t c)"),
                            decay[:, b * T:(b + 1) * T, :].rearrange("p t c -> p (t c)"),
                            identities[:].rearrange("p t c -> p (t c)"), 0.0, ALU.mult, ALU.add).then_inc(d_ready, 1)
                    if slot == 13:
                        wait(dve, kt_ready, 1, head, b, 1)
                        wait(dve, d_ready, 1, head, b, 1)
                        nc.vector.tensor_tensor(k_decayed[:, b], in_bank[:].rearrange("p (t c) -> p t c", t=T),
                                                d_t[:, :, P - 1:P].broadcast_to([P, T, P]), ALU.mult
                                                ).then_inc(k_decayed_ready, 1)
                    if slot == 12:
                        wait(dve, g_ready, 1, head, b, 1)
                        wait(dve, strict_ready, 1, head, b, 1)
                        for t in range(T):
                            tick = nc.vector.scalar_tensor_tensor(x_first[:, t, :], g_bank[:, bass.ts(t, P)],
                                                                  column(neg_beta, head, b, t), d_strict[:, t, :],
                                                                  ALU.mult, ALU.mult)
                        tick.then_inc(x_ready, 1)
                    if slot == 15:
                        wait(dve, a_ready, 1, head, b, 1)
                        nc.vector.tensor_tensor(scores[:, b], a_bank[:].rearrange("p (t c) -> p t c", t=T), d_t[:], ALU.mult
                                                ).then_inc(scores_ready, 1)

                def invert(head, b, slot):
                    m, what = INVERT_AT[slot]
                    if what == "r":
                        wait(dve, r_ready, 6, head, b, R_ADD[m])
                        wait(dve, r_started, 1, head, b, 1)
                        wait(dve, r_added, 6, head, b, R_ADD[m] - 1)
                        rows = extent(m)
                        r = inverse[0:rows, b % 2, :, P - rows:P]
                        nc.vector.tensor_tensor(r, r, by_tile(r_bank)[0:rows, :, P - rows:P], ALU.add
                                                ).then_inc(r_added, 1)

                def recur(head, b, slot):
                    if slot == 0 and b == 0:
                        wait(dve, product_loaded, 1, 0, 0, (head + 1) * 16)
                        nc.vector.tensor_copy(last_product[:], product[:, :, P - 1]).then_inc(last_ready, 1)
                    if slot in RECUR_AT:
                        c, what = RECUR_AT[slot]
                        if what == "w":
                            wait(dve, ks_ready, 3, head, b, c)
                            nc.vector.tensor_tensor(w_rhs[:], v_tok[:, b, c, :], chain_bank[:, 0:P], ALU.subtract
                                                    ).then_inc(w_ready, 1)
                        elif what == "s":
                            wait(dve, ds_ready, 3, head, b, c + 1)
                            if c == 0:
                                nc.vector.tensor_copy(state[:], chain_bank[:, 0:P]).then_inc(state_ready, 1)
                            else:
                                wait(dve, state_ready, 3, head, b, c)
                                wait(dve, last_ready, 1, 0, 0, head + 1)
                                nc.vector.scalar_tensor_tensor(state[:], state[:], last_product[:, b * T + c:b * T + c + 1],
                                                               chain_bank[:, 0:P], ALU.mult, ALU.add
                                                               ).then_inc(state_ready, 1)
                    if slot == 14:
                        wait(dve, squares_ready, 1, head, b, 1)
                        nc.vector.tensor_scalar(o_rms[:], o_rms[:], 1.0 / P, EPS, ALU.mult, ALU.add).then_inc(mean_ready, 1)
                    if slot == 15:
                        wait(dve, rms_ready, 1, head, b, 1)
                        wait(dve, z_ready, 1, head, b, 1)
                        for t in range(T):
                            tick = nc.vector.scalar_tensor_tensor(gated[:, t, :], o_bank[:, bass.ts(t, P)], o_rms[:, t:t + 1],
                                                                  z_scaled[:, b, t, :], ALU.mult, ALU.mult)
                        tick.then_inc(gated_ready, 1)
                    if slot == 17:
                        wait(dve, out_ready, 1, head, b, 1)
                        wait(dve, added, 1, head, b, 0)
                        out = core.branch[:, b * T:(b + 1) * T, :]
                        nc.vector.tensor_tensor(out, out, by_tile(in_bank), ALU.add
                                                ).then_inc(added, 1)

                all_rounds(dve, invert, prepare, recur)


def delta_layer(core):
    nc = core.nc
    with ExitStack() as st:
        beta = core.sbuf(st, "beta", [P, 8, TILES])
        neg_beta = core.sbuf(st, "neg_beta", [P, 8, TILES])
        rows = nc.dram_tensor("decay_rows", (8, 2, TILES, P), F32, kind="Internal").ap()
        delta_gates(core, "delta_gates", beta, neg_beta, rows)
        delta_rule(core, "delta", beta, neg_beta, rows)


def build(nc, dram):
    with ExitStack() as stack:
        core = Core(nc, stack, dram)
        join(core, "first", load=True, add_branch=False, rms=(ALU.add, float(np.finfo(np.float32).eps)), scale="rms_w")
        attention(core, "causal", "w_attn0", pairs=4, causal=True, gates="w_gates")
        join(core, "sum0")
        two_of_eight(core, "experts8", "w_experts8", "w_gate8")
        join(core, "sum1", rms=(ALU.max, 1e-24 / D), scale="gamma", scale_plus=1.0)
        attention(core, "full", "w_attn1", pairs=8)
        last_bias = windowed_layers(core)
        join(core, "sum3", branch_bias=last_bias)
        linear_attention(core, "linear")
        join(core, "sum4")
        token_mix(core, "mix")
        join(core, "sum5")
        delta_layer(core)
        join(core, "sum6")
        one_of_many(core, "experts32")
        join(core, "sum7", to_chan=False, store=dram["out"])


def layout(a):
    a = {k: np.asarray(v) for k, v in a.items()}
    out = {"tokens": a["L0_attn_tokens"], "identity": np.eye(P, dtype=np.float32)}

    def by_pair(w):
        return w.reshape(D, -1, 128).transpose(1, 0, 2)

    def by_tile(x):
        return x.reshape(T, P, -1).transpose(1, 0, 2).astype(np.float32)

    def by_head(w):
        return w.transpose(1, 0, 2).reshape(D, -1)

    q, k, v = (by_pair(by_head(a[f"L0_attn_w{n}"])) for n in "qkv")
    out["w_attn0"] = np.stack([q, k, v, a["L0_attn_wo"].reshape(-1, 128, D)], 2)
    out["w_gates"] = a["L0_attn_w_gates"]
    out["rms_w"] = a["L0_attn_rms_w"][:, None]
    i = np.arange(P)
    out["causal_mask"] = np.where(i[None, :] > i[:, None], -3.0e38, 0.0).astype(np.float32)
    q, k, v = (by_pair(w) for w in np.split(a["L1_attn_w_qkv"], 3, 1))
    out["w_attn1"] = np.stack([q, k, v, a["L1_attn_w_out"].reshape(-1, 128, D)], 2)
    out["gamma"] = a["L1_attn_gamma"][:, None]
    out["w_gate8"] = a["L0_ffn_gate_w"].T
    out["numbers8"] = np.arange(8, dtype=np.float32)
    w2 = a["L0_ffn_w2"].reshape(8, 2, P, D).transpose(0, 2, 1, 3).reshape(8, P, 2 * D)
    out["w_experts8"] = np.stack([a["L0_ffn_w1"], a["L0_ffn_w3"], w2], 2)
    out["w_router"] = a["L3_ffn_router_w"].T
    out["router_b"] = a["L3_ffn_router_b"]
    out["numbers32"] = np.arange(32, dtype=np.float32)
    out["w1_many"] = a["L3_ffn_weights1"].reshape(8, 4, D, 32).transpose(2, 0, 1, 3).reshape(D, 8, P)
    out["b1_many"] = a["L3_ffn_bias1"].reshape(8, P).T
    out["w2_many"] = a["L3_ffn_weights2"].reshape(8, P, D).transpose(1, 0, 2)
    out["b2_many"] = a["L3_ffn_bias2"]
    out["spread"] = np.repeat(np.eye(32, dtype=np.float32), 32, 1).reshape(32, 8, P)
    out["w_qkv2"] = a["L2_attn_Wqkv"].T
    out["b_qkv2"] = a["L2_attn_bqkv"]
    out["w_out2"] = a["L2_attn_Wout"].T
    out["b_out2"], out["g_out2"] = a["L2_attn_bout"], a["L2_attn_gout"]
    out["g_q2"], out["g_k2"] = a["L2_attn_gq"], a["L2_attn_gk"]
    inv_freq = 1.0 / 10000.0 ** (np.arange(0, 8, 2, dtype=np.float32) / 8)
    freqs = np.tile(np.outer(np.arange(N, dtype=np.float32), inv_freq.astype(np.float32)), (1, 16))
    out["cos2"], out["sin2"] = (by_tile(f(freqs.astype(np.float32))) for f in (np.cos, np.sin))
    out["same_head"] = np.kron(np.eye(16, dtype=np.float32), np.ones((8, 8), np.float32))
    out["w_r"], out["w_k"], out["w_v"] = (a[f"L2_ffn_W_{n}"].T for n in "rkv")
    out["mu"] = np.stack([a["L2_ffn_mu_r"], a["L2_ffn_mu_k"]], 1)
    H, E, HID = 8, 64, 341
    out["w_qkv_local"] = a["L1_ffn_wqkv"].reshape(2, D, 3, H * E)
    out["w_out_local"] = a["L1_ffn_wo"].reshape(2, 4, P, D).transpose(0, 2, 1, 3)
    r, k = np.arange(P)[:, None], np.arange(64 + P)[None, :]
    out["local_mask"] = np.where((k > r + 64) | (k < r), -3.0e38, 0.0).astype(np.float32)
    qs, ks = a["L1_ffn_q_scale"], a["L1_ffn_k_scale"]
    out["head_scale"] = np.stack([qs, np.roll(qs, E // 2, 1), ks, np.roll(ks, E // 2, 1)], 1)
    half = np.arange(0, E, 2, dtype=np.float32)
    t = np.arange(N, dtype=np.float32)
    freqs = t[:, None] * (1.0 / 10000.0 ** (half / E)).astype(np.float32)[None, :]
    xpos = ((half + 0.4 * E) / (1.4 * E))[None, :] ** ((t - N // 2) / 32.0)[:, None]
    cos, sin = np.cos(freqs), np.sin(freqs)
    tables = [np.concatenate([s * f * x, f * x], 1) for x in (8.0 * xpos, 1.0 / xpos) for s, f in ((1, cos), (-1, sin))]
    out["rotary"] = np.stack([by_tile(x) for x in tables])
    pad = [(0, 0), (0, 0), (0, 3 * P - HID)]
    out["w1_gelu"] = a["L1_ffn_w1"]
    out["w2_gelu"] = np.pad(a["L1_ffn_w2"], [(0, 0), (0, 3 * P - HID), (0, 0)]).reshape(2, 3, P, D).transpose(0, 2, 1, 3)
    out["b1_gelu"] = np.pad(a["L1_ffn_b1"].reshape(2, 2, HID), pad).reshape(2, 2, 3, P).transpose(0, 3, 1, 2)
    for n in range(2):
        out[f"b2_gelu{n}"] = a["L1_ffn_b2"][n]
        out[f"ln_g{n}"], out[f"ln_b{n}"] = a["L1_ffn_ln_g"][n][:, None], a["L1_ffn_ln_b"][n][:, None]
    H = 8
    qkv = a["L3_attn_qkv_w"].reshape(3, H, P, D)[[1, 0, 2]]
    w_in = np.concatenate([qkv, a["L3_attn_z_w"].reshape(1, H, P, D)])
    out["w_in"] = w_in.transpose(1, 3, 0, 2)
    out["w_conv"] = a["L3_attn_conv_w"].reshape(3, H, P, 4)[[1, 0, 2]].transpose(1, 2, 0, 3)
    out["w_out_delta"] = a["L3_attn_out_w"].T.reshape(H, P, D)
    out["w_ab"] = np.concatenate([a["L3_attn_a_w"], a["L3_attn_b_w"]]).T
    out["dt_bias"], out["a_log"], out["norm_w"] = a["L3_attn_dt_bias"], a["L3_attn_A_log"], a["L3_attn_norm_w"]
    return out


def kernel(**inputs):
    import concourse.bacc as bacc
    from concourse.bass_utils import run_bass_kernel_spmd

    nc = bacc.Bacc("TRN2", target_bir_lowering=False, num_devices=1)
    arrays, dram = {}, {}
    for name, a in layout(inputs).items():
        a = np.ascontiguousarray(a)
        arrays[f"in_{name}"] = a
        dram[name] = nc.dram_tensor(f"in_{name}", a.shape, mybir.dt.from_np(a.dtype), kind="ExternalInput").ap()
    dram["out"] = nc.dram_tensor("out", (B, N, D), F32, kind="ExternalOutput").ap()
    build(nc, dram)
    done = run_bass_kernel_spmd(nc, [arrays], core_ids=[0])
    return done.results[0]["out"]
```
